# Optimizing a Trainium2 kernel written in Bass

```python
import numpy as np
import jax
import jax.numpy as jnp

def _softmax(x, axis=-1):
    return jax.nn.softmax(x, axis=axis)

def _gelu(x):
    return jax.nn.gelu(x, approximate=True)

def _silu(x):
    return jax.nn.silu(x)

def _sigmoid(x):
    return jax.nn.sigmoid(x)

def _layernorm(x, axis=-1, eps=1e-05):
    m = jnp.mean(x, axis=axis, keepdims=True)
    v = jnp.var(x, axis=axis, keepdims=True)
    return (x - m) / jnp.sqrt(v + eps)

def _scatter_add(tgt, idx, src, axis=0):
    return tgt.at[idx].add(src)

def _segment_sum(src, seg, n):
    return jax.ops.segment_sum(src, seg, n)
kernel_name = 'mk_gnn_resnorm_d4_gnn_r32_364877'

def setup_inputs(seed: int=0):
    np.random.seed(seed)
    _w = jnp.asarray

    def _rec_inputs():
        import jax
        import jax.numpy as jnp
        _gk = jax.random.key(seed)
        x = -0.000202 + 1 * jax.random.normal(jax.random.fold_in(_gk, 1), (3125, 128), jnp.float32)
        src = jax.random.randint(jax.random.fold_in(_gk, 2), (50000,), 0, 3125, jnp.int32)
        dst = jnp.minimum((3125 * jax.random.uniform(jax.random.fold_in(_gk, 3), (50000,)) ** 2.0).astype(jnp.int32), 99999)
        _o = jnp.argsort(dst, stable=True)
        src = src[_o]
        dst = dst[_o]
        edge_attr_128 = -5.3897e-05 + 0.999841 * jax.random.normal(jax.random.fold_in(_gk, 13), (50000, 128), jnp.float32)
        edge_type_8 = jax.random.randint(jax.random.fold_in(_gk, 15), (50000,), 0, 8, jnp.int32)
        return (x, src, dst, edge_attr_128, edge_type_8)
    x, src, dst, edge_attr_128, edge_type_8 = _rec_inputs()

    def _L0_gnn_setup():
        import jax, jax.numpy as jnp
        import numpy as np
        IN_DIM = 128
        OUT_DIM = 128
        NUM_RELS = 8
        N_NODES = 50000
        N_EDGES = 15625
        key = jax.random.key(seed)
        k_x, k_ei_s, k_ei_d, k_et, k_w, k_sw = jax.random.split(key, 6)
        x = jax.random.normal(k_x, (N_NODES, IN_DIM), dtype=jnp.float32)
        src = jax.random.randint(k_ei_s, (N_EDGES,), 0, N_NODES)
        dst = jax.random.randint(k_ei_d, (N_EDGES,), 0, N_NODES)
        edge_index = jnp.stack([src, dst], axis=0).astype(jnp.int64)
        edge_type = jax.random.randint(k_et, (N_EDGES,), 0, NUM_RELS).astype(jnp.int64)
        bw = float(np.sqrt(6.0 / (IN_DIM + OUT_DIM)))
        weight = jax.random.uniform(k_w, (NUM_RELS, IN_DIM, OUT_DIM), dtype=jnp.float32, minval=-bw, maxval=bw)
        self_loop_weight = jax.random.uniform(k_sw, (IN_DIM, OUT_DIM), dtype=jnp.float32, minval=-bw, maxval=bw)
        bias = jnp.zeros((OUT_DIM,), dtype=jnp.float32)
        return {'x': x, 'weight': weight, 'self_loop_weight': self_loop_weight, 'bias': bias, 'edge_index': edge_index, 'edge_type': edge_type, 'num_entities': N_NODES}
    _L0_gnn_all = _L0_gnn_setup()
    _L0_gnn_in = {k: v for k, v in _L0_gnn_all.items() if k in ('weight', 'self_loop_weight', 'bias')}
    del _L0_gnn_all

    def _L1_gnn_setup():
        import jax, jax.numpy as jnp
        import numpy as np
        N_NODES = 3125
        N_EDGES = 50000
        D_IN = 128
        D_OUT = 128
        BN_EPS = 1e-05
        L2_EPS = 1e-12
        key = jax.random.key(seed)
        k_x, k_e, k_wl, k_bl, k_wr = jax.random.split(key, 5)
        x = jax.random.normal(k_x, (N_NODES, D_IN), dtype=jnp.float32)
        edge_index = jax.random.randint(k_e, (2, N_EDGES), 0, N_NODES, dtype=jnp.int64)
        s = 1.0 / np.sqrt(D_IN)
        W_l = jax.random.uniform(k_wl, (D_OUT, D_IN), jnp.float32, -s, s)
        b_l = jax.random.uniform(k_bl, (D_OUT,), jnp.float32, -s, s)
        W_r = jax.random.uniform(k_wr, (D_OUT, D_IN), jnp.float32, -s, s)
        gamma = jnp.ones((D_OUT,), jnp.float32)
        beta = jnp.zeros((D_OUT,), jnp.float32)
        return {'x': x, 'edge_index': edge_index, 'W_l': W_l, 'b_l': b_l, 'W_r': W_r, 'gamma': gamma, 'beta': beta}
    _L1_gnn_all = _L1_gnn_setup()
    _L1_gnn_in = {k: v for k, v in _L1_gnn_all.items() if k in ('W_l', 'b_l', 'W_r', 'gamma', 'beta')}
    del _L1_gnn_all

    def _L2_gnn_setup():
        import jax, jax.numpy as jnp
        import numpy as np
        N, E = (50000, 25000)
        D_IN, D_HID, D_OUT = (128, 256, 128)

        def _sage_layer(h, edge_src, edge_dst, W, b, inv_deg):
            msgs = h[edge_src]
            agg = jax.ops.segment_sum(msgs, edge_dst, num_segments=h.shape[0]) * inv_deg
            y = jnp.concatenate([h, agg], axis=1)
            return y @ W + b
        key = jax.random.key(seed)
        k = jax.random.split(key, 7)
        x = jax.random.normal(k[0], (N, D_IN), dtype=jnp.float32)
        edge_src = jax.random.randint(k[1], (E,), 0, N, dtype=jnp.int32)
        edge_dst = jax.random.randint(k[2], (E,), 0, N, dtype=jnp.int32)
        s1 = 1.0 / np.sqrt(2 * D_IN)
        s2 = 1.0 / np.sqrt(2 * D_HID)
        W1 = jax.random.uniform(k[3], (2 * D_IN, D_HID), jnp.float32, -s1, s1)
        b1 = jax.random.uniform(k[4], (D_HID,), jnp.float32, -s1, s1)
        W2 = jax.random.uniform(k[5], (2 * D_HID, D_OUT), jnp.float32, -s2, s2)
        b2 = jax.random.uniform(k[6], (D_OUT,), jnp.float32, -s2, s2)
        return {'x': x, 'edge_src': edge_src, 'edge_dst': edge_dst, 'W1': W1, 'b1': b1, 'W2': W2, 'b2': b2}
    _L2_gnn_all = _L2_gnn_setup()
    _L2_gnn_in = {k: v for k, v in _L2_gnn_all.items() if k in ('W1', 'b1', 'W2', 'b2')}
    del _L2_gnn_all

    def _L3_gnn_setup():
        import jax, jax.numpy as jnp
        import numpy as np
        N, E, G = (50000, 6250, 64)
        ND, ED, GD = (128, 128, 128)
        EPS = 1e-05

        def _seg_mean(vals, idx, num):
            s = jax.ops.segment_sum(vals, idx, num_segments=num)
            c = jax.ops.segment_sum(jnp.ones((vals.shape[0], 1), vals.dtype), idx, num_segments=num)
            return s / jnp.maximum(c, 1.0)
        key = jax.random.key(seed)
        ks = jax.random.split(key, 16)
        s = 0.02
        return {'x': jax.random.normal(ks[0], (N, ND), jnp.float32), 'edge_attr': jax.random.normal(ks[1], (E, ED), jnp.float32), 'u': jax.random.normal(ks[2], (G, GD), jnp.float32), 'W1a': jax.random.normal(ks[3], (ND + ED, 4 * ED), jnp.float32) * s, 'b1a': jnp.zeros((4 * ED,), jnp.float32), 'W2a': jax.random.normal(ks[4], (4 * ED, ND), jnp.float32) * s, 'b2a': jnp.zeros((ND,), jnp.float32), 'W1u': jax.random.normal(ks[5], (ND + ED + GD, 4 * ND), jnp.float32) * s, 'b1u': jnp.zeros((4 * ND,), jnp.float32), 'W2u': jax.random.normal(ks[6], (4 * ND, ND), jnp.float32) * s, 'b2u': jnp.zeros((ND,), jnp.float32), 'gn_weight': jnp.ones((ND,), jnp.float32), 'gn_bias': jnp.zeros((ND,), jnp.float32), 'gn_alpha': jnp.ones((ND,), jnp.float32), 'edge_index': jax.random.randint(ks[7], (2, E), 0, N, jnp.int64), 'batch': jnp.sort(jax.random.randint(ks[8], (N,), 0, G, jnp.int64))}
    _L3_gnn_all = _L3_gnn_setup()
    _L3_gnn_in = {k: v for k, v in _L3_gnn_all.items() if k in ('u', 'W1a', 'b1a', 'W2a', 'b2a', 'W1u', 'b1u', 'W2u', 'b2u', 'gn_weight', 'gn_bias', 'gn_alpha')}
    del _L3_gnn_all
    return {'x': x, 'src': src, 'dst': dst, 'edge_attr_128': edge_attr_128, 'edge_type_8': edge_type_8, 'L0_gnn_weight': _L0_gnn_in['weight'], 'L0_gnn_self_loop_weight': _L0_gnn_in['self_loop_weight'], 'L0_gnn_bias': _L0_gnn_in['bias'], 'L1_gnn_W_l': _L1_gnn_in['W_l'], 'L1_gnn_b_l': _L1_gnn_in['b_l'], 'L1_gnn_W_r': _L1_gnn_in['W_r'], 'L1_gnn_gamma': _L1_gnn_in['gamma'], 'L1_gnn_beta': _L1_gnn_in['beta'], 'L2_gnn_W1': _L2_gnn_in['W1'], 'L2_gnn_b1': _L2_gnn_in['b1'], 'L2_gnn_W2': _L2_gnn_in['W2'], 'L2_gnn_b2': _L2_gnn_in['b2'], 'L3_gnn_u': _L3_gnn_in['u'], 'L3_gnn_W1a': _L3_gnn_in['W1a'], 'L3_gnn_b1a': _L3_gnn_in['b1a'], 'L3_gnn_W2a': _L3_gnn_in['W2a'], 'L3_gnn_b2a': _L3_gnn_in['b2a'], 'L3_gnn_W1u': _L3_gnn_in['W1u'], 'L3_gnn_b1u': _L3_gnn_in['b1u'], 'L3_gnn_W2u': _L3_gnn_in['W2u'], 'L3_gnn_b2u': _L3_gnn_in['b2u'], 'L3_gnn_gn_weight': _L3_gnn_in['gn_weight'], 'L3_gnn_gn_bias': _L3_gnn_in['gn_bias'], 'L3_gnn_gn_alpha': _L3_gnn_in['gn_alpha']}

def reference(x, src, dst, edge_attr_128, edge_type_8, L0_gnn_weight, L0_gnn_self_loop_weight, L0_gnn_bias, L1_gnn_W_l, L1_gnn_b_l, L1_gnn_W_r, L1_gnn_gamma, L1_gnn_beta, L2_gnn_W1, L2_gnn_b1, L2_gnn_W2, L2_gnn_b2, L3_gnn_u, L3_gnn_W1a, L3_gnn_b1a, L3_gnn_W2a, L3_gnn_b2a, L3_gnn_W1u, L3_gnn_b1u, L3_gnn_W2u, L3_gnn_b2u, L3_gnn_gn_weight, L3_gnn_gn_bias, L3_gnn_gn_alpha):
    import jax
    import jax.numpy as jnp

    def _L0_gnn_ref(x, weight, self_loop_weight, bias, edge_index, edge_type, num_entities):
        import jax, jax.numpy as jnp
        import numpy as np
        IN_DIM = 128
        OUT_DIM = 128
        NUM_RELS = 8
        N_NODES = 50000
        N_EDGES = 15625
        hr = jnp.einsum('nd,rdo->rno', x, weight)
        src, dst = (edge_index[0], edge_index[1])
        msg = hr[edge_type, src]
        agg = jax.ops.segment_sum(msg, dst, num_segments=num_entities)
        out = agg + x @ self_loop_weight + bias
        return jax.nn.relu(out)

    def _L1_gnn_ref(x, edge_index, W_l, b_l, W_r, gamma, beta):
        import jax, jax.numpy as jnp
        import numpy as np
        N_NODES = 3125
        N_EDGES = 50000
        D_IN = 128
        D_OUT = 128
        BN_EPS = 1e-05
        L2_EPS = 1e-12
        src, dst = (edge_index[0], edge_index[1])
        n = x.shape[0]
        msg = x[src]
        agg_sum = jax.ops.segment_sum(msg, dst, num_segments=n)
        deg = jax.ops.segment_sum(jnp.ones((src.shape[0],), x.dtype), dst, num_segments=n)
        agg = agg_sum / jnp.maximum(deg, 1.0)[:, None]
        out = agg @ W_l.T + b_l + x @ W_r.T
        norm = jnp.sqrt(jnp.sum(out * out, axis=-1, keepdims=True))
        out = out / jnp.maximum(norm, L2_EPS)
        mu = jnp.mean(out, axis=0)
        var = jnp.mean((out - mu) ** 2, axis=0)
        out = (out - mu) * jax.lax.rsqrt(var + BN_EPS) * gamma + beta
        return jax.nn.relu(out)

    def _L2_gnn_ref(x, edge_src, edge_dst, W1, b1, W2, b2):
        import jax, jax.numpy as jnp
        import numpy as np
        N, E = (50000, 25000)
        D_IN, D_HID, D_OUT = (128, 256, 128)

        def _sage_layer(h, edge_src, edge_dst, W, b, inv_deg):
            msgs = h[edge_src]
            agg = jax.ops.segment_sum(msgs, edge_dst, num_segments=h.shape[0]) * inv_deg
            y = jnp.concatenate([h, agg], axis=1)
            return y @ W + b
        n = x.shape[0]
        deg = jax.ops.segment_sum(jnp.ones_like(edge_dst, dtype=x.dtype), edge_dst, num_segments=n)
        inv_deg = (1.0 / jnp.maximum(deg, 1.0))[:, None]
        h = _sage_layer(x, edge_src, edge_dst, W1, b1, inv_deg)
        h = jax.nn.relu(h)
        h = _sage_layer(h, edge_src, edge_dst, W2, b2, inv_deg)
        return jax.nn.log_softmax(h, axis=1)

    def _L3_gnn_ref(x, edge_attr, u, W1a, b1a, W2a, b2a, W1u, b1u, W2u, b2u, gn_weight, gn_bias, gn_alpha, edge_index, batch):
        import jax, jax.numpy as jnp
        import numpy as np
        N, E, G = (50000, 6250, 64)
        ND, ED, GD = (128, 128, 128)
        EPS = 1e-05

        def _seg_mean(vals, idx, num):
            s = jax.ops.segment_sum(vals, idx, num_segments=num)
            c = jax.ops.segment_sum(jnp.ones((vals.shape[0], 1), vals.dtype), idx, num_segments=num)
            return s / jnp.maximum(c, 1.0)
        src, dst = (edge_index[0], edge_index[1])
        agg = jnp.concatenate([x[src], edge_attr], axis=1)
        agg = jax.nn.relu(agg @ W1a + b1a) @ W2a + b2a
        agg = _seg_mean(agg, dst, x.shape[0])
        out = jnp.concatenate([x, agg, u[batch]], axis=1)
        out = jax.nn.relu(out @ W1u + b1u) @ W2u + b2u
        h = out + x
        mean = _seg_mean(h, batch, G)
        h = h - gn_alpha * mean[batch]
        var = _seg_mean(h * h, batch, G)
        return gn_weight * h / jnp.sqrt(var + EPS)[batch] + gn_bias
    edge_index = jnp.stack([src, dst])
    batch0 = jnp.zeros((3125,), jnp.int32)
    x = _layernorm(x + _L0_gnn_ref(x, L0_gnn_weight, L0_gnn_self_loop_weight, L0_gnn_bias, edge_index, edge_type_8, 3125), axis=-1)
    x = _layernorm(x + _L1_gnn_ref(x, edge_index, L1_gnn_W_l, L1_gnn_b_l, L1_gnn_W_r, L1_gnn_gamma, L1_gnn_beta), axis=-1)
    x = _layernorm(x + _L2_gnn_ref(x, src, dst, L2_gnn_W1, L2_gnn_b1, L2_gnn_W2, L2_gnn_b2), axis=-1)
    x = _layernorm(x + _L3_gnn_ref(x, edge_attr_128, L3_gnn_u, L3_gnn_W1a, L3_gnn_b1a, L3_gnn_W2a, L3_gnn_b2a, L3_gnn_W1u, L3_gnn_b1u, L3_gnn_W2u, L3_gnn_b2u, L3_gnn_gn_weight, L3_gnn_gn_bias, L3_gnn_gn_alpha, edge_index, batch0), axis=-1)
    return x

_drawn_inputs = setup_inputs


def setup_inputs(seed=0):
    import zlib

    import numpy as np

    out = dict(_drawn_inputs(seed))
    spreads = {'L0_gnn_bias': (0.0, 0.326),
     'L1_gnn_gamma': (1.0, 0.2),
     'L1_gnn_beta': (0.0, 0.1),
     'L3_gnn_b1a': (0.0, 0.8),
     'L3_gnn_b2a': (0.0, 2.0),
     'L3_gnn_b1u': (0.0, 0.8),
     'L3_gnn_b2u': (0.0, 0.741),
     'L3_gnn_gn_weight': (1.0, 0.2),
     'L3_gnn_gn_bias': (0.0, 0.1),
     'L3_gnn_gn_alpha': (1.0, 0.6)}
    factors = {'edge_attr_128': 8.0,
     'L1_gnn_b_l': 8.0,
     'L2_gnn_b1': 6.057,
     'L2_gnn_b2': 4.465,
     'L3_gnn_u': 3.185,
     'L3_gnn_W1a': 8.0,
     'L3_gnn_W2a': 8.0}
    for name, (base, spread) in spreads.items():
        noise = np.random.default_rng([zlib.crc32(name.encode()), seed]).standard_normal(out[name].shape)
        drawn = base * np.exp(spread * noise) if base else spread * noise
        out[name] = jnp.asarray(drawn.astype(out[name].dtype))
    for name, factor in factors.items():
        out[name] = (out[name] * factor).astype(out[name].dtype)
    return out
```

```python
from contextlib import ExitStack

import concourse.bass as bass
from concourse import mybir

ALU = mybir.AluOpType
ACT = mybir.ActivationFunctionType
F32 = mybir.dt.float32
I32 = mybir.dt.int32
AX_X = mybir.AxisListType.X

P = 128
N = 3125
E = 50000
D = 128
R = 8
HID = 4 * D
TILES = (N + P - 1) // P
NP = TILES * P
TAIL = N - (TILES - 1) * P
BANK = 4
CHUNK = 125
U = 4
CHUNKS = E // CHUNK
GROUPS = CHUNKS // U
GE = CHUNK * U
PAIRS = GROUPS // 2
LN_EPS = 1e-5
assert CHUNK * CHUNKS == E and U * GROUPS == CHUNKS and GROUPS % 2 == 0

NODE_GROUPS = [(g * BANK, min(BANK, TILES - g * BANK)) for g in range((TILES + BANK - 1) // BANK)]


def build(nc, a, out):
    scratch = lambda name, shape, dt: nc.dram_tensor(name, shape, dt, kind="Internal").ap()
    rel_table = scratch("rel_table", (N * R, D), F32)
    x1_table = scratch("x1_table", (N, D), F32)
    x2_table = scratch("x2_table", (N, D), F32)
    z_table = scratch("z_table", (N, D), F32)
    p_table = scratch("p_table", (N, HID), F32)
    tile_table = scratch("tile_table", (GROUPS, 2), I32)

    with ExitStack() as ctx:
        def sb(name, shape, dt=F32):
            return ctx.enter_context(nc.sbuf_tensor(name, shape, dt))

        def sem(name):
            return ctx.enter_context(nc.semaphore(name))

        x_in = sb("x_in", [P, TILES, D])
        cur = sb("cur", [P, TILES, D])
        agg = sb("agg", [P, TILES, D + 4])
        val = sb("val", [P, TILES, D])
        curT = sb("curT", [P, NP])
        aggT = sb("aggT", [P, NP])
        square = aggT[:, :].rearrange("p (t d) -> p t d", d=D)
        big = sb("big", [P, TILES * HID])
        hidT = big[:, 0:2 * NP].rearrange("p (h n) -> p h n", h=2)
        hsum = big[:, :].rearrange("p (t h) -> p t h", h=HID)
        own = x_in
        rows = sb("rows", [CHUNK, 2 * U, D + 4])
        rows_p = sb("rows_p", [P, 2 * U, HID])
        hidden = sb("hidden", [P, U, HID])
        onehot = sb("onehot", [CHUNK, U, P])
        edge_in = sb("edge_in", [P, 2, GE])
        ubuf = rows_p[:, :, :].rearrange("p (b c) n -> p b c n", b=2)
        wide = hidden[:, :, :].rearrange("p (b c) n -> p b (c n)", b=2)
        src_c = sb("src_c", [CHUNK, CHUNKS], I32)
        typ_c = sb("typ_c", [CHUNK, CHUNKS], I32)
        dst_c = sb("dst_c", [CHUNK, CHUNKS], I32)
        rel_c = sb("rel_c", [CHUNK, CHUNKS], I32)
        dst_f = sb("dst_f", [CHUNK, CHUNKS])
        idx = sb("idx", [CHUNK, 2, U], I32)
        dst_g = rows_p[0:GROUPS, 0, 0:GE].bitcast(I32)
        dst_gf = rows_p[0:GROUPS, 1, 0:GE]
        span_f = sb("span_f", [GROUPS, 2])
        span_i = sb("span_i", [GROUPS, 2], I32)
        span_t = sb("span_t", [GROUPS, 2], I32)
        span = sb("span", [1, 2 * GROUPS], I32)
        lane = sb("lane", [P, P])
        tile_off = sb("tile_off", [P, TILES])
        ident = sb("ident", [P, P])
        ones = sb("ones", [P, P])
        w_rel = sb("w_rel", [P, R * D])
        w_self = sb("w_self", [P, D])
        w_l = sb("w_l", [P, D])
        w_r = sb("w_r", [P, D])
        w1 = sb("w1", [P, 2, 2 * D])
        w2 = sb("w2", [P, 2, 2, D])
        w1a = sb("w1a", [P, 2, HID])
        w2a = sb("w2a", [P, 4, D])
        w1u = sb("w1u", [P, 3, HID])
        w2u = sb("w2u", [P, 4, D])
        b1_col = sb("b1_col", [P, 2])
        b1u_col = sb("b1u_col", [P, 4])
        u_col = sb("u_col", [P, 1])
        bcast = {k: sb("bc_" + k, [P, D]) for k in
                 ("b0", "bl", "gamma", "beta", "b2", "b2a", "b2u", "gnw", "gnb", "gna")}
        b1a_b = sb("b1a_b", [P, HID])
        stats = sb("stats", [P, TILES, 6])
        mv = sb("mv", [P, TILES, 2])
        rstd = sb("rstd", [P, TILES])
        inv_deg = sb("inv_deg", [P, TILES])
        has_edge = sb("has_edge", [P, TILES])
        small = sb("small", [P, TILES])
        col_a = sb("col_a", [P, D])
        col_b = sb("col_b", [P, D])
        u_bias = sb("u_bias", [P, 4])

        ps = [ctx.enter_context(nc.psum_tensor(f"ps{i}", [P, 512], F32)) for i in range(8)]

        zeroed = sem("zeroed")
        loaded_w = sem("loaded_w")
        loaded_x = sem("loaded_x")
        loaded_idx = sem("loaded_idx")
        consts = sem("consts")
        const_step = sem("const_step")
        spans_made = sem("spans_made")
        spans_out = sem("spans_out")
        spans_in = sem("spans_in")
        tables_made = sem("tables_made")
        rel_mm = sem("rel_mm")
        rel_evac = [sem("rel_evac_act"), sem("rel_evac_dve")]
        rel_stored = [sem(f"rel_stored{i}") for i in range(2)]
        idx_ready = [sem(f"idx_ready{i}") for i in range(2)]
        gathered = [sem(f"gathered{i}") for i in range(2)]
        rows_used = [sem(f"rows_used{i}") for i in range(2)]
        gather_go = sem("gather_go")
        onehot_ready = sem("onehot_ready")
        seg_done = sem("seg_done")
        seg_added = sem("seg_added")
        agg_clear = sem("agg_clear")
        dve_step = sem("dve_step")
        act_step = sem("act_step")
        x_mm = sem("x_mm")
        x_free = sem("x_free")
        var_ready = sem("var_ready")
        std_ready = sem("std_ready")
        cur_ready = sem("cur_ready")
        stored = [sem(f"stored{i}") for i in range(4)]
        pass_done = sem("pass_done")
        scaled = sem("scaled")
        tr_mm = sem("tr_mm")
        tr_evac = sem("tr_evac")
        lin_mm = sem("lin_mm")
        lin_free = sem("lin_free")
        col_ready = sem("col_ready")
        col_mm = sem("col_mm")
        hid_mm = sem("hid_mm")
        hid_evac = sem("hid_evac")
        yz_mm = sem("yz_mm")
        y_evac = sem("y_evac")
        z_evac = sem("z_evac")
        max_ready = sem("max_ready")
        lse_ready = sem("lse_ready")
        p_mm = sem("p_mm")
        p_evac = sem("p_evac")
        p_stored = [sem(f"p_stored{i}") for i in range(2)]
        edge_loaded = [sem(f"edge_loaded{i}") for i in range(2)]
        edge_ready = sem("edge_ready")
        pre_done = sem("pre_done")
        relu_done = sem("relu_done")
        hst_mm = sem("hst_mm")
        hst_evac = sem("hst_evac")
        s_mm = sem("s_mm")
        s_evac = sem("s_evac")
        ub_mm = sem("ub_mm")
        ub_ready = sem("ub_ready")
        u_mm = sem("u_mm")
        u_evac = sem("u_evac")
        o_mm = sem("o_mm")
        o_free = sem("o_free")
        out_ready = sem("out_ready")
        out_stored = sem("out_stored")

        block = ctx.enter_context(nc.Block())

        NARROW = [("rel", rel_table), ("x1", x1_table), ("x2", x2_table), ("z", z_table)]

        def span_of(eng, group):
            first = eng.value_load(span[0:1, bass.ds(group * 2, 1)], min_val=0, max_val=TILES - 1)
            end = eng.value_load(span[0:1, bass.ds(group * 2 + 1, 1)], min_val=1, max_val=TILES)
            return first, end

        @block.sync
        def _(sp):
            def load(dst, src, s):
                sp.dma_start(dst, src).then_inc(s, 16)

            sp.wait_ge(zeroed, 2)
            load(curT[:, 0:N], a["xT"], loaded_w)
            load(w_rel[:], a["w_rel"], loaded_w)
            load(dst_g, a["dst"].rearrange("(g e) -> g e", e=GE), loaded_idx)
            load(src_c[:], a["src_c"], loaded_idx)
            load(typ_c[:], a["typ_c"], loaded_idx)
            load(dst_c[:], a["dst_c"], loaded_idx)
            load(x_in[:, 0:TILES - 1, :], a["x"][0:N - TAIL, :].rearrange("(t p) d -> p t d", p=P), loaded_x)
            load(x_in[0:TAIL, TILES - 1, :], a["x"][N - TAIL:N, :], loaded_x)
            load(w_self[:], a["w_self"], loaded_x)
            load(w_l[:], a["w_lT"], loaded_x)
            load(w_r[:], a["w_rT"], loaded_x)
            load(w1[:], a["w1"].rearrange("(k p) n -> p k n", p=P), loaded_x)
            for part in range(2):
                load(w2[:, :, part, :], a["w2"].rearrange("(s h p) n -> s p h n", p=P, s=2)[part], loaded_x)
            load(w1a[:], a["w1a"].rearrange("(k p) n -> p k n", p=P), loaded_x)
            load(w2a[:], a["w2a"].rearrange("(k p) n -> p k n", p=P), loaded_x)
            load(w1u[:], a["w1u"].rearrange("(k p) n -> p k n", p=P), loaded_x)
            load(w2u[:], a["w2u"].rearrange("(k p) n -> p k n", p=P), loaded_x)
            load(b1_col[:], a["b1_col"], loaded_x)
            load(b1u_col[:], a["b1u_col"], loaded_x)
            load(u_col[:], a["u_col"], loaded_x)
            for k, t in bcast.items():
                load(t[:], a[k].rearrange("(a n) -> a n", a=1).broadcast_to([P, D]), loaded_x)
            load(b1a_b[:], a["b1a"].rearrange("(a n) -> a n", a=1).broadcast_to([P, HID]), loaded_x)

            sp.wait_ge(spans_made, 1)
            sp.dma_start(tile_table, span_t[:]).then_inc(spans_out, 16)
            sp.wait_ge(spans_out, 16)
            sp.dma_start(span[:], tile_table.rearrange("(a g) s -> a (g s)", a=1)).then_inc(spans_in, 16)

            for t in range(TILES):
                n = P if t < TILES - 1 else TAIL
                sp.wait_ge(rel_evac[0], t + 1)
                sp.wait_ge(rel_evac[1], t + 1)
                sp.dma_start(rel_table.rearrange("(n r) d -> n (r d)", r=R)[t * P:t * P + n, :],
                             wide[0:n, t % 2, :]).then_inc(rel_stored[t % 2], 16)

            def store(table, node_sb, ready, value, s):
                sp.wait_ge(ready, value)
                sp.dma_start(table[0:N - TAIL, :].rearrange("(t p) d -> p t d", p=P),
                             node_sb[:, 0:TILES - 1, :]).then_inc(s, 16)
                sp.dma_start(table[N - TAIL:N, :], node_sb[0:TAIL, TILES - 1, :]).then_inc(s, 16)

            store(x1_table, cur, cur_ready, 1, stored[0])
            store(x2_table, cur, cur_ready, 2, stored[1])
            store(z_table, val, z_evac, (TILES + 1) // 2, stored[2])

            for t in range(TILES):
                n = P if t < TILES - 1 else TAIL
                sp.wait_ge(p_evac, t + 1)
                sp.dma_start(p_table[t * P:t * P + n, :], hidden[0:n, t % 2, :]).then_inc(p_stored[t % 2], 16)

            with sp.Fori(0, PAIRS) as it:
                for half in range(2):
                    sp.wait_ge(edge_ready, it * (2 * U) + (half + 1) * U)
                    sp.dma_start(edge_in[:, half, :],
                                 a["edgeT"][:, bass.ds((it * 2 + half) * GE, GE)]).then_inc(edge_loaded[half], 16)

            store(out, val, out_ready, 1, out_stored)
            sp.wait_ge(out_stored, 32)

        @block.gpsimd
        def _(pool):
            pool.memset(curT[:, N:NP], 0.0).then_inc(zeroed, 1)
            pool.memset(x_in[:, TILES - 1, :], 0.0).then_inc(zeroed, 1)
            pool.memset(ident[:], 0.0).then_inc(const_step, 1)
            pool.memset(ones[:], 1.0).then_inc(consts, 1)
            pool.memset(rows[:, :, D:D + 1], 1.0).then_inc(consts, 1)
            pool.iota(lane[:], pattern=[[1, P]], base=0, channel_multiplier=0,
                      allow_small_or_imprecise_dtypes=True).then_inc(consts, 1)
            pool.iota(tile_off[:], pattern=[[P, TILES]], base=0, channel_multiplier=0,
                      allow_small_or_imprecise_dtypes=True).then_inc(consts, 1)
            pool.wait_ge(const_step, 1)
            pool.affine_select(out=ident[:], in_=ident[:], compare_op=ALU.not_equal, fill=1.0,
                               base=0, pattern=[[-1, P]], channel_multiplier=1).then_inc(consts, 1)

            def gather_pass(n_pass, table, buf, width):
                with pool.Fori(0, PAIRS) as it:
                    for half in range(2):
                        pool.wait_ge(idx_ready[half], it + (n_pass * PAIRS + 1))
                        pool.sem_inc(gather_go, 1)
                        for u in range(U):
                            pool.indirect_dma_start(
                                buf[0:CHUNK, half * U + u, 0:width], None, table,
                                bass.IndirectOffsetOnAxis(ap=idx[:, half, u:u + 1], axis=0)
                            ).then_inc(gathered[half], 16)

            pool.wait_ge(rel_stored[0], 16 * ((TILES + 1) // 2))
            pool.wait_ge(rel_stored[1], 16 * (TILES // 2))
            gather_pass(0, rel_table, rows, D)
            for n_pass in range(1, 4):
                pool.wait_ge(stored[n_pass - 1], 32)
                gather_pass(n_pass, NARROW[n_pass][1], rows, D)
            pool.wait_ge(p_stored[0], 16 * ((TILES + 1) // 2))
            pool.wait_ge(p_stored[1], 16 * (TILES // 2))
            gather_pass(4, p_table, rows_p, HID)

        @block.scalar
        def _(act):
            steps = [0]

            def link(ins):
                steps[0] += 1
                ins.then_inc(act_step, 1)
                act.wait_ge(act_step, steps[0])

            for t in range(TILES):
                act.wait_ge(rel_mm, t + 1)
                if t >= 2:
                    act.wait_ge(rel_stored[t % 2], 16 * (t // 2))
                act.copy(wide[:, t % 2, 0:512], ps[2 * (t % 2)][:, :]).then_inc(rel_evac[0], 1)

            def copy_indices(n_pass, table, relu=False):
                with act.Fori(0, PAIRS) as it:
                    for half in range(2):
                        act.wait_ge(rows_used[half], it + (n_pass * PAIRS + 1))
                        act.copy(idx[:, half, :], table[:, bass.ds((it * 2 + half) * U, U)]).then_inc(idx_ready[half], 1)

            def sqrt_of(arr, n):
                act.wait_ge(var_ready, n)
                act.activation(arr, arr, ACT.Sqrt).then_inc(std_ready, 1)

            def evac_transposes(n):
                for g, (t0, k) in enumerate(NODE_GROUPS):
                    for w, dst in enumerate((curT, aggT)):
                        act.wait_ge(tr_mm, 2 * len(NODE_GROUPS) * n + 2 * g + w + 1)
                        act.copy(dst[:, t0 * P:(t0 + k) * P], ps[2 * (g % 2) + w][:, 0:k * P]).then_inc(tr_evac, 1)

            act.wait_ge(tables_made, 2)
            copy_indices(0, rel_c)
            sqrt_of(rstd[:], 1)
            copy_indices(1, src_c)
            evac_transposes(0)
            sqrt_of(small[:], 2)
            sqrt_of(col_b[:], 3)
            sqrt_of(rstd[:], 4)
            copy_indices(2, src_c)
            evac_transposes(1)
            for g, (t0, k) in enumerate(NODE_GROUPS):
                for h in range(2):
                    act.wait_ge(hid_mm, 2 * g + h + 1)
                    act.activation(hidT[:, h, t0 * P:(t0 + k) * P], ps[4 + h][:, 0:k * P], ACT.Relu,
                                   bias=b1_col[:, h:h + 1]).then_inc(hid_evac, 1)
            for b in range((TILES + 1) // 2):
                k = min(2, TILES - 2 * b)
                act.wait_ge(yz_mm, b + 1)
                act.copy(val[:, 2 * b:2 * b + k, :],
                         ps[6 + b % 2][:, 0:k * 256].rearrange("p (t s d) -> p t s d", s=2, d=D)[:, :, 1, :]
                         ).then_inc(z_evac, 1)
            copy_indices(3, src_c)
            act.wait_ge(max_ready, 1)
            for t in range(TILES):
                ins = act.activation(square[:, t, :], own[:, t, :], ACT.Exp, accum_out=small[:, t:t + 1])
            link(ins)
            act.activation(small[:], small[:], ACT.Ln).then_inc(lse_ready, 1)
            sqrt_of(rstd[:], 5)
            for g, (t0, k) in enumerate(NODE_GROUPS):
                act.wait_ge(tr_mm, 4 * len(NODE_GROUPS) + g + 1)
                act.copy(curT[:, t0 * P:(t0 + k) * P], ps[g % 2][:, 0:k * P]).then_inc(tr_evac, 1)

            with act.Fori(0, PAIRS) as it:
                for half in range(2):
                    act.wait_ge(rows_used[half], it + (4 * PAIRS + 1))
                    act.copy(idx[:, half, :], src_c[:, bass.ds((it * 2 + half) * U, U)]).then_inc(idx_ready[half], 1)
                    for u in range(U):
                        act.wait_ge(pre_done, it * (2 * U) + ((half + 1) * U + u + 1))
                        act.activation(hidden[0:CHUNK, u, :], hidden[0:CHUNK, u, :], ACT.Relu).then_inc(relu_done, 1)
            for t in range(TILES):
                act.wait_ge(hst_mm, t + 1)
                if t >= 2:
                    act.wait_ge(s_mm, t - 1)
                act.copy(hidden[:, t % 2, :], ps[t % 2][:, :]).then_inc(hst_evac, 1)
            for g, (t0, k) in enumerate(NODE_GROUPS):
                act.wait_ge(tr_mm, 5 * len(NODE_GROUPS) + g + 1)
                act.copy(aggT[:, t0 * P:(t0 + k) * P], ps[4 + g % 2][:, 0:k * P]).then_inc(tr_evac, 1)
            act.wait_ge(ub_ready, 1)
            for g, (t0, k) in enumerate(NODE_GROUPS):
                for c in range(4):
                    act.wait_ge(u_mm, 4 * g + c + 1)
                    if g >= 2:
                        act.wait_ge(o_mm, g - 1)
                    act.activation(ubuf[:, g % 2, c, 0:k * P], ps[c][:, 0:k * P], ACT.Relu,
                                   bias=u_bias[:, c:c + 1]).then_inc(u_evac, 1)
            sqrt_of(col_b[:], 6)
            sqrt_of(rstd[:], 7)

        @block.tensor
        def _(pe):
            mm = pe.matmul
            pe.wait_ge(loaded_w, 32)
            for t in range(TILES):
                for h in range(2):
                    if t >= 2:
                        pe.wait_ge(rel_evac[h], t - 1)
                    ins = mm(ps[2 * (t % 2) + h][:, :], curT[:, t * P:(t + 1) * P], w_rel[:, h * 512:(h + 1) * 512],
                             start=True, stop=True)
                ins.then_inc(rel_mm, 1)

            count = pe.alloc_register("pe_segments")
            pe.reg_mov(count, 1)

            def add_rows(width, rhs_of):
                n = pe.snap(count, min_val=1, max_val=5 * GROUPS * TILES + 1)
                pe.wait_ge(onehot_ready, n)
                pe.wait_ge(seg_added, n)
                for u in range(U):
                    ins = mm(ps[4][:, 0:width], onehot[:, u, :], rhs_of(u), start=(u == 0), stop=(u == U - 1))
                ins.then_inc(seg_done, 1)
                pe.reg_add(count, count, 1)

            def narrow_pass(n_pass):
                width = D + 1 if n_pass == 0 else D
                with pe.Fori(0, PAIRS) as it:
                    for half in range(2):
                        pe.wait_ge(gathered[half], it * (16 * U) + 16 * U * (n_pass * PAIRS + 1))
                        first, end = span_of(pe, it * 2 + half)
                        with pe.Fori(first, end):
                            add_rows(width, lambda u: rows[:, half * U + u, 0:width])

            def transpose_nodes(n, srcs, banks, ready, value, base):
                pe.wait_ge(ready, value)
                for g, (t0, k) in enumerate(NODE_GROUPS):
                    for w, src in enumerate(srcs):
                        if g >= 2:
                            pe.wait_ge(tr_evac, base + len(srcs) * (g - 2) + w + 1)
                        for i in range(k):
                            ins = pe.transpose(ps[banks[w] + len(srcs) * (g % 2)][:, i * P:(i + 1) * P],
                                               src[:, t0 + i, 0:D], ident[:])
                        ins.then_inc(tr_mm, 1)

            def column_sums(src, bank, ready, value):
                pe.wait_ge(ready, value)
                for t in range(TILES):
                    k = P if t < TILES - 1 else TAIL
                    ins = mm(ps[bank][:, 0:D], ones[0:k, :], src[0:k, t, :], start=(t == 0), stop=(t == TILES - 1))
                ins.then_inc(col_mm, 1)

            pe.wait_ge(consts, 5)
            pe.wait_ge(spans_in, 16)
            narrow_pass(0)
            pe.wait_ge(loaded_x, 16 * LOADS)
            for g, (t0, k) in enumerate(NODE_GROUPS):
                if g >= 2:
                    pe.wait_ge(x_free, g - 1)
                for i in range(k):
                    ins = mm(ps[g % 2][:, i * P:(i + 1) * P], curT[:, (t0 + i) * P:(t0 + i + 1) * P], w_self[:],
                             start=True, stop=True)
                ins.then_inc(x_mm, 1)
            NG = len(NODE_GROUPS)
            narrow_pass(1)
            transpose_nodes(0, (cur, agg), (0, 1), scaled, 1, 0)
            for g, (t0, k) in enumerate(NODE_GROUPS):
                pe.wait_ge(tr_evac, 2 * g + 2)
                if g >= 2:
                    pe.wait_ge(lin_free, g - 1)
                for i in range(k):
                    cols = slice((t0 + i) * P, (t0 + i + 1) * P)
                    mm(ps[5 + g % 2][:, i * P:(i + 1) * P], aggT[:, cols], w_l[:], start=True, stop=False)
                    ins = mm(ps[5 + g % 2][:, i * P:(i + 1) * P], curT[:, cols], w_r[:], start=False, stop=True)
                ins.then_inc(lin_mm, 1)
            column_sums(val, 7, col_ready, 1)
            column_sums(square, 6, col_ready, 2)
            narrow_pass(2)
            transpose_nodes(1, (cur, agg), (0, 1), scaled, 2, 2 * NG)
            for g, (t0, k) in enumerate(NODE_GROUPS):
                pe.wait_ge(tr_evac, 2 * NG + 2 * g + 2)
                cols = slice(t0 * P, (t0 + k) * P)
                for h in range(2):
                    if g >= 1:
                        pe.wait_ge(hid_evac, 2 * (g - 1) + h + 1)
                    mm(ps[4 + h][:, 0:k * P], w1[:, 0, h * D:(h + 1) * D], curT[:, cols], start=True, stop=False)
                    mm(ps[4 + h][:, 0:k * P], w1[:, 1, h * D:(h + 1) * D], aggT[:, cols], start=False,
                       stop=True).then_inc(hid_mm, 1)
            for b in range((TILES + 1) // 2):
                pe.wait_ge(hid_evac, 2 * ((2 * b) // BANK + 1))
                if b >= 2:
                    pe.wait_ge(y_evac, b - 1)
                    pe.wait_ge(z_evac, b - 1)
                for i in range(min(2, TILES - 2 * b)):
                    t = 2 * b + i
                    for h in range(2):
                        ins = mm(ps[6 + b % 2][:, i * 256:(i + 1) * 256], hidT[:, h, t * P:(t + 1) * P],
                                 w2[:, h, :, :].rearrange("p s n -> p (s n)"), start=(h == 0), stop=(h == 1))
                ins.then_inc(yz_mm, 1)
            narrow_pass(3)
            transpose_nodes(2, (cur,), (0,), cur_ready, 3, 4 * NG)
            for t in range(TILES):
                if t % BANK == 0:
                    pe.wait_ge(tr_evac, 4 * NG + t // BANK + 1)
                if t >= 2:
                    pe.wait_ge(p_evac, t - 1)
                mm(ps[2 + t % 2][:, :], curT[:, t * P:(t + 1) * P], w1a[:, 0, :], start=True, stop=True).then_inc(p_mm, 1)
            for c in range(4):
                ins = mm(ps[7][:, c:c + 1], w1u[:, 2, c * D:(c + 1) * D], u_col[:], start=True, stop=True)
            ins.then_inc(ub_mm, 1)
            pe.wait_ge(p_evac, TILES)
            with pe.Fori(0, PAIRS) as it:
                for half in range(2):
                    pe.wait_ge(edge_loaded[half], it * 16 + 16)
                    for u in range(U):
                        pe.wait_ge(pre_done, it * (2 * U) + (half * U + u + 1))
                        mm(ps[u][0:CHUNK, :], edge_in[:, half, u * CHUNK:(u + 1) * CHUNK], w1a[:, 1, :],
                           start=True, stop=True).then_inc(edge_ready, 1)
                    pe.wait_ge(relu_done, it * (2 * U) + (half + 1) * U)
                    first, end = span_of(pe, it * 2 + half)
                    with pe.Fori(first, end):
                        add_rows(HID, lambda u: hidden[0:CHUNK, u, :])
            pe.wait_ge(scaled, 3)
            for t in range(TILES + 1):
                if t < TILES:
                    if t >= 2:
                        pe.wait_ge(hst_evac, t - 1)
                    for c in range(4):
                        ins = pe.transpose(ps[t % 2][:, c * P:(c + 1) * P], hsum[:, t, c * P:(c + 1) * P], ident[:])
                    ins.then_inc(hst_mm, 1)
                if t >= 1:
                    q = t - 1
                    pe.wait_ge(hst_evac, q + 1)
                    if q >= 2:
                        pe.wait_ge(s_evac, q - 1)
                    for c in range(4):
                        ins = mm(ps[2 + q % 2][:, 0:D], hidden[:, q % 2, c * P:(c + 1) * P], w2a[:, c, :],
                                 start=(c == 0), stop=(c == 3))
                    ins.then_inc(s_mm, 1)
            transpose_nodes(3, (agg,), (4,), s_evac, TILES, 5 * NG)
            for g, (t0, k) in enumerate(NODE_GROUPS):
                pe.wait_ge(tr_evac, 5 * NG + g + 1)
                cols = slice(t0 * P, (t0 + k) * P)
                for c in range(4):
                    if g >= 1:
                        pe.wait_ge(u_evac, 4 * (g - 1) + c + 1)
                    mm(ps[c][:, 0:k * P], w1u[:, 0, c * D:(c + 1) * D], curT[:, cols], start=True, stop=False)
                    mm(ps[c][:, 0:k * P], w1u[:, 1, c * D:(c + 1) * D], aggT[:, cols], start=False,
                       stop=True).then_inc(u_mm, 1)
                pe.wait_ge(u_evac, 4 * g + 4)
                if g >= 2:
                    pe.wait_ge(o_free, g - 1)
                for i in range(k):
                    for c in range(4):
                        ins = mm(ps[6 + g % 2][:, i * P:(i + 1) * P], ubuf[:, g % 2, c, i * P:(i + 1) * P],
                                 w2u[:, c, :], start=(c == 0), stop=(c == 3))
                ins.then_inc(o_mm, 1)
            column_sums(val, 4, col_ready, 3)
            column_sums(square, 5, col_ready, 4)

        @block.vector
        def _(dve):
            steps = [0]

            def link(ins):
                steps[0] += 1
                ins.then_inc(dve_step, 1)
                dve.wait_ge(dve_step, steps[0])

            tt, ts, stt = dve.tensor_tensor, dve.tensor_scalar, dve.scalar_tensor_tensor

            def over_tiles(v):
                return v.rearrange("p (a d) -> p a d", a=1).broadcast_to([P, TILES, D])

            dve.sem_inc(rows_used[0], 1)
            dve.sem_inc(rows_used[1], 1)
            dve.sem_inc(seg_added, 1)
            dve.sem_inc(edge_ready, 2 * U)
            dve.sem_inc(pre_done, U)

            dve.wait_ge(loaded_idx, 64)
            link(dve.tensor_copy(dst_gf, dst_g))
            dve.tensor_reduce(span_f[:, 0:1], dst_gf, AX_X, ALU.min)
            link(dve.tensor_reduce(span_f[:, 1:2], dst_gf, AX_X, ALU.max))
            link(dve.tensor_copy(span_i[:], span_f[:]))
            link(ts(span_t[:], span_i[:], 7, None, ALU.arith_shift_right))
            ts(span_t[:, 1:2], span_t[:, 1:2], 1, None, ALU.add).then_inc(spans_made, 1)
            stt(rel_c[:], src_c[:], float(R), typ_c[:], ALU.mult, ALU.add).then_inc(tables_made, 1)
            dve.tensor_copy(dst_f[:], dst_c[:]).then_inc(tables_made, 1)
            dve.memset(agg[:], 0.0).then_inc(agg_clear, 1)

            for t in range(TILES):
                dve.wait_ge(rel_mm, t + 1)
                if t >= 2:
                    dve.wait_ge(rel_stored[t % 2], 16 * (t // 2))
                dve.tensor_copy(wide[:, t % 2, 512:1024], ps[2 * (t % 2) + 1][:, :]).then_inc(rel_evac[1], 1)

            count = dve.alloc_register("dve_segments")
            dve.reg_mov(count, 1)
            dve.wait_ge(consts, 5)
            dve.wait_ge(tables_made, 2)
            dve.wait_ge(spans_in, 16)

            def add_group(group, total, width):
                first, end = span_of(dve, group)
                with dve.Fori(first, end) as t:
                    n = dve.snap(count, min_val=1, max_val=5 * GROUPS * TILES + 1)
                    for u in range(U):
                        ins = ts(onehot[:, u, :], lane[0:CHUNK, :], tile_off[0:CHUNK, bass.ds(t, 1)],
                                 dst_f[:, bass.ds(group * U + u, 1)], ALU.add, ALU.is_equal)
                    ins.then_inc(onehot_ready, 1)
                    dve.wait_ge(seg_done, n)
                    dve.wait_ge(seg_added, n)
                    part = total[:, bass.ds(t, 1), 0:width].rearrange("p a d -> p (a d)")
                    tt(part, ps[4][:, 0:width], part, ALU.add).then_inc(seg_added, 1)
                    dve.reg_add(count, count, 1)

            def narrow_pass(n_pass):
                dve.wait_ge(agg_clear, n_pass + 1)
                with dve.Fori(0, PAIRS) as it:
                    for half in range(2):
                        add_group(it * 2 + half, agg, D + 1 if n_pass == 0 else D)
                        dve.sem_inc(rows_used[half], 1)
                dve.wait_ge(seg_added, dve.snap(count, min_val=1, max_val=5 * GROUPS * TILES + 1))

            def layer_norm(n_sqrt):
                for t in range(TILES):
                    ins = dve.bn_stats(stats[:, t, :], val[:, t, :])
                link(ins)
                for t in range(TILES):
                    ins = dve.bn_aggr(mv[:, t, :], stats[:, t, :])
                link(ins)
                ts(rstd[:], mv[:, :, 1], LN_EPS, None, ALU.add).then_inc(var_ready, 1)
                dve.wait_ge(std_ready, n_sqrt)
                link(dve.reciprocal(rstd[:], rstd[:]))

            def normalise(dst):
                for t in range(TILES):
                    ins = ts(dst[:, t, :], val[:, t, :], mv[:, t, 0:1], rstd[:, t:t + 1], ALU.subtract, ALU.mult)
                return ins

            def scale_agg(n):
                for t in range(TILES):
                    ins = ts(agg[:, t, 0:D], agg[:, t, 0:D], inv_deg[:, t:t + 1], None, ALU.mult)
                ins.then_inc(scaled, 1)

            narrow_pass(0)
            dve.wait_ge(loaded_x, 16 * LOADS)
            ts(has_edge[:], agg[:, :, D], 0.0, None, ALU.is_gt)
            link(ts(inv_deg[:], agg[:, :, D], 1.0, None, ALU.max))
            dve.reciprocal(inv_deg[:], inv_deg[:])
            for g, (t0, k) in enumerate(NODE_GROUPS):
                dve.wait_ge(x_mm, g + 1)
                ins = tt(val[:, t0:t0 + k, :], ps[g % 2][:, 0:k * P].rearrange("p (t d) -> p t d", d=D),
                         agg[:, t0:t0 + k, 0:D], ALU.add)
                ins.then_inc(x_free, 1)
            dve.wait_ge(x_free, len(NODE_GROUPS))
            dve.memset(agg[:], 0.0).then_inc(agg_clear, 1)
            link(tt(val[:], val[:], over_tiles(bcast["b0"][:]), ALU.add))
            link(stt(val[:], val[:], 0.0, x_in[:], ALU.max, ALU.add))
            layer_norm(1)
            normalise(cur).then_inc(cur_ready, 1)

            narrow_pass(1)
            scale_agg(1)
            for g, (t0, k) in enumerate(NODE_GROUPS):
                dve.wait_ge(lin_mm, g + 1)
                ins = tt(val[:, t0:t0 + k, :], ps[5 + g % 2][:, 0:k * P].rearrange("p (t d) -> p t d", d=D),
                         bcast["bl"][:].rearrange("p (a d) -> p a d", a=1).broadcast_to([P, k, D]), ALU.add)
                ins.then_inc(lin_free, 1)
            dve.wait_ge(lin_free, len(NODE_GROUPS))
            for t in range(TILES):
                ins = dve.tensor_tensor_reduce(square[:, t, :], val[:, t, :], val[:, t, :], 1.0, 0.0,
                                               ALU.mult, ALU.add, small[:, t:t + 1])
            link(ins)
            ts(small[:], small[:], 1e-24, None, ALU.max).then_inc(var_ready, 1)
            dve.wait_ge(std_ready, 2)
            link(dve.reciprocal(small[:], small[:]))
            for t in range(TILES):
                ins = ts(val[:, t, :], val[:, t, :], small[:, t:t + 1], None, ALU.mult)
            ins.then_inc(col_ready, 1)
            dve.wait_ge(col_mm, 1)
            link(ts(col_a[:], ps[7][:, 0:D], 1.0 / N, None, ALU.mult))
            dve.wait_ge(col_ready, 1)
            link(tt(val[:], val[:], over_tiles(col_a[:]), ALU.subtract))
            tt(square, val[:], val[:], ALU.mult).then_inc(col_ready, 1)
            dve.wait_ge(col_mm, 2)
            ts(col_b[:], ps[6][:, 0:D], 1.0 / N, LN_EPS, ALU.mult, ALU.add).then_inc(var_ready, 1)
            dve.wait_ge(std_ready, 3)
            link(dve.reciprocal(col_b[:], col_b[:]))
            link(tt(col_b[:], col_b[:], bcast["gamma"][:], ALU.mult))
            link(tt(val[:], val[:], over_tiles(col_b[:]), ALU.mult))
            link(tt(val[:], val[:], over_tiles(bcast["beta"][:]), ALU.add))
            link(stt(val[:], val[:], 0.0, cur[:], ALU.max, ALU.add))
            layer_norm(4)
            dve.wait_ge(stored[0], 32)
            normalise(cur).then_inc(cur_ready, 1)
            dve.wait_ge(tr_mm, 2 * len(NODE_GROUPS))
            dve.memset(agg[:], 0.0).then_inc(agg_clear, 1)

            narrow_pass(2)
            scale_agg(2)
            for b in range((TILES + 1) // 2):
                k = min(2, TILES - 2 * b)
                dve.wait_ge(z_evac, b + 1)
                dve.tensor_copy(own[:, 2 * b:2 * b + k, :],
                                ps[6 + b % 2][:, 0:k * 256].rearrange("p (t s d) -> p t s d", s=2, d=D)[:, :, 0, :]
                                ).then_inc(y_evac, 1)
            dve.memset(agg[:], 0.0).then_inc(agg_clear, 1)
            dve.wait_ge(y_evac, (TILES + 1) // 2)
            narrow_pass(3)
            for t in range(TILES):
                ins = stt(own[:, t, :], agg[:, t, 0:D], inv_deg[:, t:t + 1], own[:, t, :], ALU.mult, ALU.add)
            link(ins)
            link(tt(own[:], own[:], over_tiles(bcast["b2"][:]), ALU.add))
            link(dve.tensor_reduce(small[:], own[:], AX_X, ALU.max))
            for t in range(TILES):
                ins = ts(own[:, t, :], own[:, t, :], small[:, t:t + 1], None, ALU.subtract)
            ins.then_inc(max_ready, 1)
            dve.wait_ge(lse_ready, 1)
            dve.wait_ge(stored[2], 32)
            for t in range(TILES):
                ins = stt(val[:, t, :], own[:, t, :], small[:, t:t + 1], cur[:, t, :], ALU.subtract, ALU.add)
            link(ins)
            layer_norm(5)
            dve.wait_ge(stored[1], 32)
            normalise(cur).then_inc(cur_ready, 1)

            for t in range(TILES):
                dve.wait_ge(p_mm, t + 1)
                if t >= 2:
                    dve.wait_ge(p_stored[t % 2], 16 * (t // 2))
                tt(hidden[:, t % 2, :], ps[2 + t % 2][:, :], b1a_b[:], ALU.add).then_inc(p_evac, 1)
            dve.wait_ge(ub_mm, 1)
            tt(u_bias[:], ps[7][:, 0:4], b1u_col[:], ALU.add).then_inc(ub_ready, 1)
            link(dve.memset(big[:], 0.0))
            dve.wait_ge(p_stored[0], 16 * ((TILES + 1) // 2))
            dve.wait_ge(p_stored[1], 16 * (TILES // 2))
            with dve.Fori(0, PAIRS) as it:
                for half in range(2):
                    dve.wait_ge(gathered[half], it * (16 * U) + 16 * U * (4 * PAIRS + 1))
                    for u in range(U):
                        dve.wait_ge(edge_ready, it * (2 * U) + ((half + 2) * U + u + 1))
                        tt(hidden[0:CHUNK, u, :], ps[u][0:CHUNK, :], rows_p[0:CHUNK, half * U + u, :],
                           ALU.add).then_inc(pre_done, 1)
                    add_group(it * 2 + half, hsum, HID)
                    dve.sem_inc(rows_used[half], 1)
            dve.wait_ge(seg_added, dve.snap(count, min_val=1, max_val=5 * GROUPS * TILES + 1))
            for t in range(TILES):
                ins = ts(hsum[:, t, :], hsum[:, t, :], inv_deg[:, t:t + 1], None, ALU.mult)
            ins.then_inc(scaled, 1)
            for t in range(TILES):
                dve.wait_ge(s_mm, t + 1)
                ins = stt(agg[:, t, 0:D], bcast["b2a"][:], has_edge[:, t:t + 1], ps[2 + t % 2][:, 0:D],
                          ALU.mult, ALU.add)
                ins.then_inc(s_evac, 1)
            for g, (t0, k) in enumerate(NODE_GROUPS):
                dve.wait_ge(o_mm, g + 1)
                ins = tt(val[:, t0:t0 + k, :], ps[6 + g % 2][:, 0:k * P].rearrange("p (t d) -> p t d", d=D),
                         bcast["b2u"][:].rearrange("p (a d) -> p a d", a=1).broadcast_to([P, k, D]), ALU.add)
                ins.then_inc(o_free, 1)
            dve.wait_ge(o_free, len(NODE_GROUPS))
            tt(val[:], val[:], cur[:], ALU.add).then_inc(col_ready, 1)
            dve.wait_ge(col_mm, 3)
            link(stt(col_a[:], ps[4][:, 0:D], 1.0 / N, bcast["gna"][:], ALU.mult, ALU.mult))
            dve.wait_ge(col_ready, 3)
            link(tt(val[:], val[:], over_tiles(col_a[:]), ALU.subtract))
            tt(square, val[:], val[:], ALU.mult).then_inc(col_ready, 1)
            dve.wait_ge(col_mm, 4)
            ts(col_b[:], ps[5][:, 0:D], 1.0 / N, LN_EPS, ALU.mult, ALU.add).then_inc(var_ready, 1)
            dve.wait_ge(std_ready, 6)
            link(dve.reciprocal(col_b[:], col_b[:]))
            link(tt(col_b[:], col_b[:], bcast["gnw"][:], ALU.mult))
            link(tt(val[:], val[:], over_tiles(col_b[:]), ALU.mult))
            link(tt(val[:], val[:], over_tiles(bcast["gnb"][:]), ALU.add))
            link(tt(val[:], val[:], cur[:], ALU.add))
            layer_norm(7)
            normalise(val).then_inc(out_ready, 1)


LOADS = 2 + 10 + 3 + 10 + 1


def kernel(**inputs):
    import numpy as np
    import concourse.bacc as bacc
    from concourse.bass_utils import run_bass_kernel_spmd

    g = {k: np.ascontiguousarray(v) for k, v in inputs.items()}
    c = np.ascontiguousarray
    chunks = lambda v: c(v.reshape(CHUNKS, CHUNK).T)
    columns = lambda v: c(v.reshape(-1, P).T)
    arrays = {
        "x": g["x"], "xT": c(g["x"].T), "dst": g["dst"],
        "src_c": chunks(g["src"]), "dst_c": chunks(g["dst"]), "typ_c": chunks(g["edge_type_8"]),
        "edgeT": c(g["edge_attr_128"].T),
        "w_rel": c(g["L0_gnn_weight"].transpose(1, 0, 2).reshape(D, R * D)),
        "w_self": g["L0_gnn_self_loop_weight"], "b0": g["L0_gnn_bias"],
        "w_lT": c(g["L1_gnn_W_l"].T), "bl": g["L1_gnn_b_l"], "w_rT": c(g["L1_gnn_W_r"].T),
        "gamma": g["L1_gnn_gamma"], "beta": g["L1_gnn_beta"],
        "w1": g["L2_gnn_W1"], "b1_col": columns(g["L2_gnn_b1"]), "w2": g["L2_gnn_W2"], "b2": g["L2_gnn_b2"],
        "u_col": c(g["L3_gnn_u"][0:1].T), "w1a": g["L3_gnn_W1a"], "b1a": g["L3_gnn_b1a"],
        "w2a": g["L3_gnn_W2a"], "b2a": g["L3_gnn_b2a"], "w1u": g["L3_gnn_W1u"],
        "b1u_col": columns(g["L3_gnn_b1u"]), "w2u": g["L3_gnn_W2u"], "b2u": g["L3_gnn_b2u"],
        "gnw": g["L3_gnn_gn_weight"], "gnb": g["L3_gnn_gn_bias"], "gna": g["L3_gnn_gn_alpha"],
    }
    nc = bacc.Bacc("TRN2", target_bir_lowering=False, num_devices=1)
    aps = {k: nc.dram_tensor("in_" + k, v.shape, mybir.dt.from_np(v.dtype), kind="ExternalInput").ap()
           for k, v in arrays.items()}
    out = nc.dram_tensor("out", (N, D), F32, kind="ExternalOutput").ap()
    build(nc, aps, out)
    r = run_bass_kernel_spmd(nc, [{"in_" + k: v for k, v in arrays.items()}], core_ids=[0])
    return r.results[0]["out"]
```

```python
from contextlib import ExitStack

import concourse.bass as bass
from concourse import mybir

ALU = mybir.AluOpType
ACT = mybir.ActivationFunctionType
F32 = mybir.dt.float32
F16 = mybir.dt.float16
BF16 = mybir.dt.bfloat16
I32 = mybir.dt.int32
AX_X = mybir.AxisListType.X

P = 128
N = 3125
E = 50000
D = 128
R = 8
HID = 4 * D
TILES = (N + P - 1) // P
NP = TILES * P
TAIL = N - (TILES - 1) * P
BANK = 4
CHUNK = 125
U = 4
CHUNKS = E // CHUNK
GROUPS = CHUNKS // U
GE = CHUNK * U
Q = 4
ROUNDS = GROUPS // Q
SUB = 64
SUBS = NP // SUB
BLOCKS_A_BANK = 512 // SUB
CP = 2
STEPS = CHUNKS // CP
MID = NP // 2
LN_EPS = 1e-5
ROW_SCALE = 4096.0
assert CHUNK * CHUNKS == E and ROUNDS * Q * U == CHUNKS and STEPS * CP == CHUNKS and SUBS * SUB == NP
assert MID <= 2048 and (D - 1) ** 0.5 * ROW_SCALE < 65504

NODE_GROUPS = [(g * BANK, min(BANK, TILES - g * BANK)) for g in range((TILES + BANK - 1) // BANK)]
NG = len(NODE_GROUPS)


def build(nc, a, out):
    scratch = lambda name, shape, dt=F32: nc.dram_tensor(name, shape, dt, kind="Internal").ap()
    rel_table = scratch("rel_table", (N * R, D))
    messages = scratch("messages", (E, D))
    x1_table = scratch("x1_table", (NP, D))
    x2_table = scratch("x2_table", (NP, D))
    z_table = scratch("z_table", (NP, D))
    p_table = scratch("p_table", (N, HID))
    inv_table = scratch("inv_table", (NP,))
    tile_table = scratch("tile_table", (GROUPS, 2), I32)

    by_tile = lambda table: table.rearrange("(t p) d -> p t d", p=P)
    messages_v = messages.rearrange("(c p) d -> p c d", p=CHUNK)

    with ExitStack() as ctx:
        def sb(name, shape, dt=F32):
            return ctx.enter_context(nc.sbuf_tensor(name, shape, dt))

        def sem(name):
            return ctx.enter_context(nc.semaphore(name))

        arena = sb("arena", [P, TILES * TILES * P], F16)
        AT = arena[:, :].rearrange("p (t j n) -> p t j n", t=TILES, j=TILES)

        def in_arena(start_f32, n_f32):
            return arena[:, 2 * start_f32:2 * (start_f32 + n_f32)].bitcast(F32)

        at = [(TILES - 5) * NP // 2]

        def early(n):
            at[0] += n
            assert at[0] <= TILES * NP // 2
            return in_arena(at[0] - n, n)

        xT = early(NP)
        w_rel = early(R * D)
        wide = early(2 * R * D).rearrange("p (b n) -> p b n", b=2)
        src_c = early(CHUNKS)[0:CHUNK, :].bitcast(I32)
        typ_c = early(CHUNKS)[0:CHUNK, :].bitcast(I32)
        dst_c = early(CHUNKS)[0:CHUNK, :].bitcast(I32)

        at3 = [0]

        def late(n):
            at3[0] += n
            assert at3[0] <= TILES * NP // 2
            return in_arena(at3[0] - n, n)

        w1a = late(2 * HID).rearrange("p (k n) -> p k n", k=2)
        w2a = late(4 * D).rearrange("p (k n) -> p k n", k=4)
        w1u = late(3 * HID).rearrange("p (k n) -> p k n", k=3)
        w2u = late(4 * D).rearrange("p (k n) -> p k n", k=4)
        b1a_b = late(HID)
        b2a_b, b2u_b, gnw_b, gnb_b, gna_b = (late(D) for _ in range(5))
        src_late = late(CHUNKS)[0:CHUNK, :].bitcast(I32)
        x3T = late(NP)
        hsum = late(TILES * HID).rearrange("p (t h) -> p t h", h=HID)
        rows_p = late(Q * U * HID).rearrange("p (s h) -> p s h", h=HID)
        hidden = late(2 * U * HID).rearrange("p (b u h) -> p b u h", b=2, u=U)
        edge_in = late(Q * GE).rearrange("p (q e) -> p q e", q=Q)
        x2_back = rows_p.rearrange("p s h -> p (s h)")[:, 0:NP].rearrange("p (t d) -> p t d", d=D)
        ubuf = rows_p.rearrange("p s h -> p (s h)")[:, 0:2 * 4 * 512].rearrange("p (b c n) -> p b c n", b=2, c=4)
        sT = rows_p.rearrange("p s h -> p (s h)")[:, 4096:4096 + NP]
        s_nodes = hidden.rearrange("p b u h -> p (b u h)")[:, 0:NP].rearrange("p (t d) -> p t d", d=D)
        hsT = edge_in.rearrange("p q e -> p (q e)")[:, 0:2 * HID].rearrange("p (b h) -> p b h", b=2)
        val3 = hsum.rearrange("p t h -> p (t h)")[:, 0:NP].rearrange("p (t d) -> p t d", d=D)

        share = sb("share", [P, TILES * 3 * D], F16)
        oh_src = share[0:CHUNK, 0:CP * NP].rearrange("p (u n) -> p u n", u=CP)
        src_line = share[0:CHUNK, CP * NP:(CP + 1) * NP]
        share_f = share[:, :].bitcast(F32)
        rows_in = share_f[0:CHUNK, 0:Q * U * (D + 4)].rearrange("p (s d) -> p s d", d=D + 4)
        onehot = share_f[0:CHUNK, 2112:2112 + 3 * U * P].rearrange("p (b u n) -> p b u n", b=3, u=U)
        x_grp = [share_f[:, 3648:4160], share_f[:, 0:512]]
        xT_grp = [share_f[:, 4160:4672], share_f[:, 512:1024]]
        split = share[:, 0:TILES * 2 * D].rearrange("p (t s d) -> p t s d", t=TILES, s=2)
        square = share_f[:, 0:NP].rearrange("p (t d) -> p t d", d=D)
        xT_buf = share_f[:, 3200:3712]
        inv_b = share_f[:, 3712:4224]
        z_out = share_f[:, 4224:4736]
        split3 = share[:, :].bitcast(BF16).rearrange("p (t s d) -> p t s d", t=TILES, s=3)

        nodes = sb("nodes", [P, TILES * (D + 4)])
        agg = nodes[:, :].rearrange("p (t d) -> p t d", d=D + 4)
        val = agg[:, :, 0:D]
        rows_g = nodes[0:CHUNK, 0:Q * U * D].rearrange("p (s d) -> p s d", d=D)
        rel_c = nodes[0:CHUNK, 2048:2048 + CHUNKS].bitcast(I32)
        src_f = nodes[0:CHUNK, 2448:2448 + CHUNKS]

        hT_buf = sb("hT_buf", [P, 2, 512])
        aggT_buf = sb("aggT_buf", [P, 512])
        dst_g = hT_buf[0:GROUPS, 0, 0:GE].bitcast(I32)
        dst_gf = hT_buf[0:GROUPS, 1, 0:GE]
        col_a = hT_buf[:, 0, 0:D]
        col_b = hT_buf[:, 1, 0:D]
        z_in = hT_buf
        stats = aggT_buf[:, 0:TILES * 6].rearrange("p (t s) -> p t s", s=6)
        z_mid = aggT_buf

        dst_f = sb("dst_f", [CHUNK, CHUNKS + U])
        oh_dst = sb("oh_dst", [CHUNK, CP, SUB], F16)
        zero16 = sb("zero16", [1, P], F16)
        idx = sb("idx", [CHUNK, Q, U], I32)
        span = sb("span", [1, 2 * (GROUPS + 1)], I32)
        sub_span = sb("sub_span", [1, 2 * SUBS], I32)
        lane = sb("lane", [P, P])
        tile_off = sb("tile_off", [P, SUBS])
        ident = sb("ident", [P, P])
        ones = sb("ones", [P, P])
        w_self = sb("w_self", [P, D])
        w_l = sb("w_l", [P, D])
        w_r = sb("w_r", [P, D])
        w1 = sb("w1", [P, 2, 2 * D])
        w2 = sb("w2", [P, 2, 2, D])
        b1_col = sb("b1_col", [P, 2])
        b1u_col = sb("b1u_col", [P, 4])
        u_col = sb("u_col", [P, 1])
        b0_b, bl_b, gamma_b, beta_b, b2_b = (sb(n, [P, D]) for n in ("b0_b", "bl_b", "gamma_b", "beta_b", "b2_b"))
        mv = sb("mv", [P, TILES, 2])
        rstd = sb("rstd", [P, TILES])
        inv_deg = sb("inv_deg", [P, TILES])
        has_edge = sb("has_edge", [P, TILES])
        small = sb("small", [P, TILES])
        u_bias = sb("u_bias", [P, 4])
        lows = share_f[0:GROUPS, 1024:1028]
        spans_f = share_f[0:GROUPS, 1032:1034]
        spans_i = share_f[0:GROUPS, 1036:1038].bitcast(I32)
        weight_c = share_f[0:GROUPS, 1040:1044]
        reach = share_f[0:GROUPS, 0:4 * SUBS].rearrange("p (q n) -> p q n", q=2)
        reach_col = share_f[0:2 * SUBS, 4 * SUBS:4 * SUBS + 1]
        reach_line = share_f[0:1, 4 * SUBS + 4:6 * SUBS + 4]

        ps = [ctx.enter_context(nc.psum_tensor(f"ps{i}", [P, 512], F32)) for i in range(8)]

        names = """zeroed loaded_w loaded_dst loaded_idx loaded_late loaded_e consts const_step spans_made spans_out
            spans_in tables_made reach_made reach_tr reach_max reach_row subs_made rel_mm rel_evac_a rel_evac_v
            idx_copied wait_carried block_done seg_first oh_first_ready first_added more_ready seg_more more_added
            agg_clear dve_step act_step x_mm x_used var_ready std_ready x1_ready x2_ready inv_tr inv_row inv_stored
            split_ready dense_mm dense_taken turn_mm turn_evac lin_mm lin_taken inv_used col_ready col_mm x1_back
            square_done hid_mm hid_evac yz_mm z_evac y_evac split3_ready sum_mm sum_taken x2_loaded max_ready
            lse_ready x3_ready arena_free pre_done relu_done edge_ready p_mm p_evac ub_mm ub_ready hsum_clear
            scaled hst_mm hst_evac s_mm s_evac u_mm u_evac o_mm o_taken out_ready out_stored
            xT3_evac turn3_mm z_split x1_used""".split()
        s = {n: sem(n) for n in names}
        rel_stored = [sem(f"rel_stored{i}") for i in range(2)]
        gathered = [sem(f"gathered{i}") for i in range(Q)]
        message_out = [sem(f"message_out{i}") for i in range(Q)]
        message_in = [sem(f"message_in{i}") for i in range(Q)]
        rows_used = [sem(f"rows_used{i}") for i in range(Q)]
        oh_ready = [sem(f"oh_ready{i}") for i in range(CP)]
        oh_used = [sem(f"oh_used{i}") for i in range(CP)]
        block_taken = [sem(f"block_taken{i}") for i in range(2)]
        x_loaded = [sem(f"x_loaded{i}") for i in range(2)]
        x1_stored, x2_stored, z_stored, inv_loaded = sem("x1_stored"), sem("x2_stored"), sem("z_stored"), sem("inv_loaded")
        z_loaded = [sem(f"z_loaded{i}") for i in range(2)]
        p_stored = [sem(f"p_stored{i}") for i in range(2)]
        edge_loaded = [sem(f"edge_loaded{i}") for i in range(Q)]
        p_gathered = [sem(f"p_gathered{i}") for i in range(Q)]
        p_used = [sem(f"p_used{i}") for i in range(Q)]

        block = ctx.enter_context(nc.Block())

        def span_of(eng, group):
            first = eng.value_load(span[0:1, bass.ds(group * 2, 1)], min_val=0, max_val=TILES - 1)
            end = eng.value_load(span[0:1, bass.ds(group * 2 + 1, 1)], min_val=0, max_val=TILES)
            return first, end

        def steps_of(eng, blk):
            first = eng.value_load(sub_span[0:1, bass.ds(blk, 1)], min_val=0, max_val=STEPS - 1)
            end = eng.value_load(sub_span[0:1, bass.ds(blk + SUBS, 1)], min_val=1, max_val=STEPS)
            return first, end

        def tiles_of(bank, k):
            return bank[:, 0:k * P].rearrange("p (t d) -> p t d", d=D)

        @block.sync
        def _(sp):
            def load(dst, src, done):
                sp.dma_start(dst, src).then_inc(done, 16)

            row = lambda name, n: a[name].rearrange("(a n) -> a n", a=1).broadcast_to([P, n])

            load(dst_g, a["dst"].rearrange("(g e) -> g e", e=GE), s["loaded_dst"])
            sp.wait_ge(s["zeroed"], 1)
            load(xT[:, 0:N], a["xT"], s["loaded_w"])
            load(w_rel, a["w_rel"], s["loaded_w"])
            load(src_c, a["src_c"], s["loaded_idx"])
            load(typ_c, a["typ_c"], s["loaded_idx"])
            load(dst_c, a["dst_c"], s["loaded_idx"])
            early_loads = [(w_self[:], a["w_self"]), (w_l[:], a["w_lT"]), (w_r[:], a["w_rT"]),
                           (w1[:], a["w1"].rearrange("(k p) n -> p k n", p=P)),
                           (w2[:, :, 0, :], a["w2"][0:2 * D, :].rearrange("(h p) n -> p h n", p=P)),
                           (w2[:, :, 1, :], a["w2"][2 * D:4 * D, :].rearrange("(h p) n -> p h n", p=P)),
                           (b1_col[:], a["b1_col"]), (b1u_col[:], a["b1u_col"]), (u_col[:], a["u_col"]),
                           (b0_b[:], row("b0", D)), (bl_b[:], row("bl", D)), (gamma_b[:], row("gamma", D)),
                           (beta_b[:], row("beta", D)), (b2_b[:], row("b2", D))]
            assert len(early_loads) == EARLY_LOADS
            for dst, src in early_loads:
                load(dst, src, s["loaded_e"])

            sp.wait_ge(s["spans_made"], 1)
            load(tile_table, spans_i, s["spans_out"])
            sp.wait_ge(s["spans_out"], 16)
            load(span[:, 0:2 * GROUPS], tile_table.rearrange("(a g) s -> a (g s)", a=1), s["spans_in"])

            for t in range(TILES):
                n = P if t < TILES - 1 else TAIL
                sp.wait_ge(s["rel_evac_a"], t + 1)
                sp.wait_ge(s["rel_evac_v"], t + 1)
                load(rel_table.rearrange("(n r) d -> n (r d)", r=R)[t * P:t * P + n, :], wide[0:n, t % 2, :],
                     rel_stored[t % 2])

            with sp.Fori(0, ROUNDS) as it:
                for q in range(Q):
                    sp.wait_ge(gathered[q], it * (16 * U) + 16 * U)
                    load(messages_v[:, bass.ds((it * Q + q) * U, U), :], rows_g[:, q * U:(q + 1) * U, :], message_out[q])
            for q in range(Q):
                sp.wait_ge(message_out[q], 16 * ROUNDS)
            sp.wait_ge(s["agg_clear"], 1)
            with sp.Fori(0, ROUNDS) as it:
                for q in range(Q):
                    sp.wait_ge(rows_used[q], it + 1)
                    load(rows_in[:, q * U:(q + 1) * U, 0:D], messages_v[:, bass.ds((it * Q + q) * U, U), :], message_in[q])

            for g, (t0, k) in enumerate(NODE_GROUPS):
                if g == 1:
                    for q in range(Q):
                        sp.wait_ge(rows_used[q], ROUNDS + 1)
                if g >= 2:
                    sp.wait_ge(s["x_used"], g - 1)
                full = k if t0 + k < TILES else k - 1
                if full:
                    load(x_grp[g % 2][:, 0:full * D].rearrange("p (t d) -> p t d", d=D),
                         by_tile(a["x"][t0 * P:(t0 + full) * P, :]), x_loaded[g % 2])
                else:
                    load(x_grp[g % 2][0:TAIL, 0:D], a["x"][t0 * P:N, :], x_loaded[g % 2])
                cols = min(N, (t0 + k) * P) - t0 * P
                load(xT_grp[g % 2][:, 0:cols], a["xT"][:, t0 * P:t0 * P + cols], x_loaded[g % 2])

            sp.wait_ge(s["inv_row"], 1)
            load(inv_table.rearrange("(t p) -> t p", p=P), aggT_buf[0:TILES, 256:256 + P], s["inv_stored"])
            sp.wait_ge(s["x1_ready"], 1)
            load(by_tile(x1_table), val, x1_stored)

            def inv_groups(base):
                for g, (t0, k) in enumerate(NODE_GROUPS):
                    if base + g >= 1:
                        sp.wait_ge(s["dense_taken"], base + g)
                    load(inv_b[:, 0:k * P], inv_table[t0 * P:(t0 + k) * P].rearrange("(a n) -> a n", a=1)
                         .broadcast_to([P, k * P]), inv_loaded)

            sp.wait_ge(s["inv_stored"], 16)
            sp.wait_ge(s["split_ready"], 1)
            inv_groups(0)
            sp.wait_ge(s["square_done"], 1)
            load(square, by_tile(x1_table), s["x1_back"])
            sp.wait_ge(s["x2_ready"], 1)
            load(by_tile(x2_table), val, x2_stored)
            sp.wait_ge(s["split_ready"], 2)
            inv_loads = NG
            for g, (t0, k) in enumerate(NODE_GROUPS):
                sp.wait_ge(s["dense_taken"], NG + g)
                load(inv_b[:, 0:k * P], inv_table[t0 * P:(t0 + k) * P].rearrange("(a n) -> a n", a=1)
                     .broadcast_to([P, k * P]), inv_loaded)
                if g >= 2:
                    gz, (tz, kz) = g - 2, NODE_GROUPS[g - 2]
                    sp.wait_ge(s["z_evac"], gz + 1)
                    load(by_tile(z_table[tz * P:(tz + kz) * P, :]), z_out[:, 0:kz * P].rearrange("p (t d) -> p t d", d=D), z_stored)
            for gz in (NG - 2, NG - 1):
                tz, kz = NODE_GROUPS[gz]
                sp.wait_ge(s["z_evac"], gz + 1)
                load(by_tile(z_table[tz * P:(tz + kz) * P, :]), z_out[:, 0:kz * P].rearrange("p (t d) -> p t d", d=D), z_stored)
            sp.wait_ge(z_stored, 16 * NG)
            for g, (t0, k) in enumerate(NODE_GROUPS):
                if g >= 2:
                    sp.wait_ge(s["z_split"], g - 1)
                else:
                    sp.wait_ge(s["y_evac"], NG)
                load(z_in[:, g % 2, 0:k * P].rearrange("p (t d) -> p t d", d=D), by_tile(z_table[t0 * P:(t0 + k) * P, :]), z_loaded[g % 2])

            sp.wait_ge(s["sum_mm"], TILES)
            load(x2_back, by_tile(x2_table), s["x2_loaded"])
            late_loads = [(w1a, a["w1a"].rearrange("(k p) n -> p k n", p=P)), (w2a, a["w2a"].rearrange("(k p) n -> p k n", p=P)),
                          (w1u, a["w1u"].rearrange("(k p) n -> p k n", p=P)), (w2u, a["w2u"].rearrange("(k p) n -> p k n", p=P)),
                          (b1a_b, row("b1a", HID)), (b2a_b, row("b2a", D)), (b2u_b, row("b2u", D)),
                          (gnw_b, row("gnw", D)), (gnb_b, row("gnb", D)), (gna_b, row("gna", D)), (src_late, a["src_c"])]
            assert len(late_loads) == LATE_LOADS
            for dst, src in late_loads:
                load(dst, src, s["loaded_late"])

            def load_edges(it, q):
                load(edge_in[:, q, :], a["edgeT"][:, bass.ds((it * Q + q) * GE, GE)], edge_loaded[q])

            for q in range(Q):
                load_edges(0, q)
            for t in range(TILES):
                n = P if t < TILES - 1 else TAIL
                sp.wait_ge(s["p_evac"], t + 1)
                load(p_table[t * P:t * P + n, :], hidden[0:n, 0, t % 2, :], p_stored[t % 2])
            with sp.Fori(1, ROUNDS) as it:
                for q in range(Q):
                    sp.wait_ge(s["edge_ready"], it * (Q * U) + ((q + 1) * U - Q * U))
                    load_edges(it, q)

            sp.wait_ge(s["out_ready"], 1)
            load(by_tile(out[0:N - TAIL, :]), val3[:, 0:TILES - 1, :], s["out_stored"])
            load(out[N - TAIL:N, :], val3[0:TAIL, TILES - 1, :], s["out_stored"])
            sp.wait_ge(s["out_stored"], 32)
            sp.wait_ge(x2_stored, 16)
            sp.wait_ge(x1_stored, 16)

        @block.gpsimd
        def _(pool):
            pool.memset(xT[:, N:NP], 0.0).then_inc(s["zeroed"], 1)
            pool.memset(ident[:], 0.0).then_inc(s["const_step"], 1)
            pool.iota(tile_off[:], pattern=[[SUB, SUBS]], base=0, channel_multiplier=0,
                      allow_small_or_imprecise_dtypes=True).then_inc(s["consts"], 1)
            pool.iota(weight_c[:, 0:2], pattern=[[-1, 2]], base=STEPS, channel_multiplier=-2,
                      allow_small_or_imprecise_dtypes=True).then_inc(s["consts"], 1)
            pool.iota(weight_c[:, 2:4], pattern=[[1, 2]], base=1, channel_multiplier=2,
                      allow_small_or_imprecise_dtypes=True).then_inc(s["consts"], 1)
            pool.iota(lane[:], pattern=[[1, P]], base=0, channel_multiplier=0,
                      allow_small_or_imprecise_dtypes=True).then_inc(s["consts"], 1)
            pool.iota(src_line, pattern=[[1, NP]], base=-MID, channel_multiplier=0,
                      allow_small_or_imprecise_dtypes=True).then_inc(s["consts"], 1)
            pool.memset(ones[:], 1.0).then_inc(s["consts"], 1)
            pool.memset(zero16[:], 0.0).then_inc(s["consts"], 1)
            pool.memset(span[:, 2 * GROUPS:], 0).then_inc(s["consts"], 1)
            pool.memset(dst_f[:, CHUNKS:], -1.0).then_inc(s["consts"], 1)
            pool.wait_ge(s["const_step"], 1)
            pool.affine_select(out=ident[:], in_=ident[:], compare_op=ALU.not_equal, fill=1.0,
                               base=0, pattern=[[-1, P]], channel_multiplier=1).then_inc(s["consts"], 1)

            def gather_group(q, table, buf, index, it, copies, done):
                pool.tensor_copy(idx[:, q, :], index[:, bass.ds((it * Q + q) * U, U)]).then_inc(s["idx_copied"], 1)
                pool.wait_ge(s["idx_copied"], copies + (q + 1) + it * Q)
                pool.sem_inc(s["wait_carried"], 1)
                for u in range(U):
                    pool.indirect_dma_start(buf[0:CHUNK, q * U + u, :], None, table,
                                            bass.IndirectOffsetOnAxis(ap=idx[:, q, u:u + 1], axis=0)).then_inc(done[q], 16)

            pool.wait_ge(s["tables_made"], 3)
            pool.wait_ge(rel_stored[0], 16 * ((TILES + 1) // 2))
            pool.wait_ge(rel_stored[1], 16 * (TILES // 2))
            for q in range(Q):
                gather_group(q, rel_table, rows_g, rel_c, 0, 0, gathered)
            with pool.Fori(1, ROUNDS) as it:
                for q in range(Q):
                    pool.wait_ge(message_out[q], it * 16)
                    gather_group(q, rel_table, rows_g, rel_c, it, 0, gathered)

            pool.wait_ge(s["loaded_late"], 16 * LATE_LOADS)
            pool.wait_ge(p_stored[0], 16 * ((TILES + 1) // 2))
            pool.wait_ge(p_stored[1], 16 * (TILES // 2))
            for q in range(Q):
                gather_group(q, p_table, rows_p, src_late, 0, GROUPS, p_gathered)
            with pool.Fori(1, ROUNDS) as it:
                for q in range(Q):
                    pool.wait_ge(s["pre_done"], it * (Q * U) + ((q + 1) * U - Q * U))
                    gather_group(q, p_table, rows_p, src_late, it, GROUPS, p_gathered)

        @block.scalar
        def _(act):
            for t in range(TILES):
                act.wait_ge(s["rel_mm"], t + 1)
                if t >= 2:
                    act.wait_ge(rel_stored[t % 2], 16 * (t // 2))
                act.copy(wide[:, t % 2, 0:512], ps[2 * (t % 2)][:, :]).then_inc(s["rel_evac_a"], 1)

            act.wait_ge(rel_stored[0], 16 * ((TILES + 1) // 2))
            act.wait_ge(rel_stored[1], 16 * (TILES // 2))
            act.wait_ge(s["tables_made"], 3)
            with act.Fori(0, TILES) as t:
                for par in range(2):
                    act.wait_ge(s["block_done"], t * 2 + (par + 1))
                    for b in range(4):
                        j0, j1 = b * BLOCKS_A_BANK, min(TILES, (b + 1) * BLOCKS_A_BANK)
                        ins = act.copy(AT[:, bass.ds(t, 1), j0:j1, par * SUB:(par + 1) * SUB].rearrange("p a j n -> p (a j) n"),
                                       ps[4 * par + b][:, 0:(j1 - j0) * SUB].rearrange("p (j n) -> p j n", n=SUB))
                    ins.then_inc(block_taken[par], 1)

            def sqrt_of(arr, n):
                act.wait_ge(s["var_ready"], n)
                act.activation(arr, arr, ACT.Sqrt).then_inc(s["std_ready"], 1)

            sqrt_of(rstd[:], 1)
            for g, (t0, k) in enumerate(NODE_GROUPS):
                act.wait_ge(s["turn_mm"], g + 1)
                if g >= 1:
                    act.wait_ge(s["lin_mm"], g)
                act.copy(xT_buf[:, 0:k * P], ps[2][:, 0:k * P]).then_inc(s["turn_evac"], 1)
            sqrt_of(small[:], 2)
            sqrt_of(col_b, 3)
            sqrt_of(rstd[:], 4)

            def hidden_group(g):
                t0, k = NODE_GROUPS[g]
                for h in range(2):
                    act.wait_ge(s["hid_mm"], 2 * g + h + 1)
                    if g >= 1:
                        act.wait_ge(s["yz_mm"], g)
                    act.activation(hT_buf[:, h, 0:k * P], ps[3 + h][:, 0:k * P], ACT.Relu,
                                   bias=b1_col[:, h:h + 1]).then_inc(s["hid_evac"], 1)

            def z_group(g):
                t0, k = NODE_GROUPS[g]
                act.wait_ge(s["yz_mm"], g + 1)
                if g >= 1:
                    act.wait_ge(z_stored, 16 * g)
                for b in range((k + 1) // 2):
                    n = min(2, k - 2 * b)
                    ins = act.copy(z_out[:, 2 * b * P:(2 * b + n) * P].rearrange("p (t d) -> p t d", d=D),
                                   ps[5 + b][:, 0:n * 256].rearrange("p (t s d) -> p t s d", s=2, d=D)[:, :, 1, :])
                ins.then_inc(s["z_evac"], 1)

            for g, (t0, k) in enumerate(NODE_GROUPS):
                if g >= 1:
                    hidden_group(g - 1)
                act.wait_ge(s["turn_mm"], NG + g + 1)
                act.copy(xT_buf[:, 0:k * P], ps[2][:, 0:k * P]).then_inc(s["turn_evac"], 1)
                if g >= 1:
                    z_group(g - 1)
            hidden_group(NG - 1)
            z_group(NG - 1)

            act.wait_ge(s["max_ready"], 1)
            for t in range(TILES):
                ins = act.activation(square[:, t, :], val[:, t, :], ACT.Exp, accum_out=small[:, t:t + 1])
            ins.then_inc(s["act_step"], 1)
            act.wait_ge(s["act_step"], 1)
            act.activation(small[:], small[:], ACT.Ln).then_inc(s["lse_ready"], 1)
            sqrt_of(rstd[:], 5)
            for g, (t0, k) in enumerate(NODE_GROUPS):
                act.wait_ge(s["turn3_mm"], g + 1)
                act.copy(x3T[:, t0 * P:(t0 + k) * P], ps[g % 2][:, 0:k * P]).then_inc(s["xT3_evac"], 1)

            with act.Fori(0, GROUPS // 2) as it:
                for half in range(2):
                    for u in range(U):
                        act.wait_ge(s["pre_done"], it * (2 * U) + (half * U + u + 1))
                        row = hidden[0:CHUNK, half, u, :]
                        act.activation(row, row, ACT.Relu).then_inc(s["relu_done"], 1)
            for t in range(TILES):
                act.wait_ge(s["hst_mm"], t + 1)
                if t >= 2:
                    act.wait_ge(s["s_mm"], t - 1)
                act.copy(hsT[:, t % 2, :], ps[t % 2][:, :]).then_inc(s["hst_evac"], 1)
            for g, (t0, k) in enumerate(NODE_GROUPS):
                act.wait_ge(s["turn3_mm"], NG + g + 1)
                act.copy(sT[:, t0 * P:(t0 + k) * P], ps[4 + g % 2][:, 0:k * P]).then_inc(s["xT3_evac"], 1)
            act.wait_ge(s["ub_ready"], 1)
            for g, (t0, k) in enumerate(NODE_GROUPS):
                for c in range(4):
                    act.wait_ge(s["u_mm"], 4 * g + c + 1)
                    if g >= 2:
                        act.wait_ge(s["o_mm"], g - 1)
                    act.activation(ubuf[:, g % 2, c, 0:k * P], ps[c][:, 0:k * P], ACT.Relu,
                                   bias=u_bias[:, c:c + 1]).then_inc(s["u_evac"], 1)
            sqrt_of(col_b, 6)
            sqrt_of(rstd[:], 7)

        @block.tensor
        def _(pe):
            mm = pe.matmul
            pe.wait_ge(s["loaded_w"], 32)
            for t in range(TILES):
                for h, evac in enumerate((s["rel_evac_a"], s["rel_evac_v"])):
                    if t >= 2:
                        pe.wait_ge(evac, t - 1)
                    ins = mm(ps[2 * (t % 2) + h][:, :], xT[:, t * P:(t + 1) * P], w_rel[:, h * 512:(h + 1) * 512],
                             start=True, stop=True)
                ins.then_inc(s["rel_mm"], 1)

            pe.wait_ge(s["consts"], 10)
            pe.wait_ge(s["reach_made"], 1)
            pe.transpose(ps[4][0:2 * SUBS, 0:GROUPS], reach[:, 0, :], ident[0:GROUPS, 0:GROUPS]).then_inc(s["reach_tr"], 1)
            pe.wait_ge(s["reach_max"], 1)
            pe.transpose(ps[5][0:1, 0:2 * SUBS], reach_col, ident[0:2 * SUBS, 0:2 * SUBS]).then_inc(s["reach_row"], 1)

            steps = pe.alloc_register("pe_steps")
            pe.reg_mov(steps, 1)
            pe.wait_ge(s["subs_made"], 1)
            pe.wait_ge(s["rel_evac_a"], TILES)
            pe.wait_ge(s["rel_evac_v"], TILES)
            with pe.Fori(0, TILES) as t:
                for par in range(2):
                    pe.wait_ge(block_taken[par], t + 1)
                    first, end = steps_of(pe, t * 2 + par)
                    for b in range(4):
                        n = min(BLOCKS_A_BANK, TILES - b * BLOCKS_A_BANK) * SUB
                        mm(ps[4 * par + b][:, 0:n], zero16[:], src_line[0:1, 0:n], start=True, stop=False,
                           skip_group_check=True)
                    with pe.Fori(first, end):
                        n = pe.snap(steps, min_val=1, max_val=SUBS * STEPS + 1)
                        for u in range(CP):
                            pe.wait_ge(oh_ready[u], n)
                            for j in range(TILES):
                                c0 = (j % BLOCKS_A_BANK) * SUB
                                ins = mm(ps[4 * par + j // BLOCKS_A_BANK][:, c0:c0 + SUB],
                                         oh_src[:, u, j * P:(j + 1) * P], oh_dst[:, u, :], start=False, stop=False,
                                         skip_group_check=True)
                            ins.then_inc(oh_used[u], 1)
                        pe.reg_add(steps, steps, 1)
                    mm(ps[4 * par + 3][:, 0:SUB], zero16[:], src_line[0:1, 0:SUB], start=False, stop=True,
                       skip_group_check=True).then_inc(s["block_done"], 1)

            more = pe.alloc_register("pe_more")
            pe.reg_mov(more, 1)

            def add_group(k, width, rhs_of, slot, banks):
                pe.wait_ge(s["oh_first_ready"], k + 1)
                pe.wait_ge(s["first_added"], k + 1)
                for u in range(U):
                    ins = mm(ps[banks[slot]][:, 0:width], onehot[:, slot, u, :], rhs_of(u), start=(u == 0), stop=(u == U - 1))
                ins.then_inc(s["seg_first"], 1)
                return None

            def add_more(group, width, rhs_of, bank):
                first, end = span_of(pe, group)
                with pe.If(end > first + 1):
                    with pe.Fori(first + 1, end):
                        n = pe.snap(more, min_val=1, max_val=2 * GROUPS * TILES + 1)
                        pe.wait_ge(s["more_ready"], n)
                        pe.wait_ge(s["more_added"], n)
                        for u in range(U):
                            ins = mm(ps[bank][:, 0:width], onehot[:, 2, u, :], rhs_of(u), start=(u == 0), stop=(u == U - 1))
                        ins.then_inc(s["seg_more"], 1)
                        pe.reg_add(more, more, 1)

            for par in range(2):
                pe.wait_ge(block_taken[par], TILES + 1)
            pe.wait_ge(s["spans_in"], 16)
            with pe.Fori(0, ROUNDS) as it:
                for q in range(Q):
                    pe.wait_ge(message_in[q], it * 16 + 16)
                    rhs_of = lambda u: rows_in[:, q * U + u, 0:D + 1]
                    add_group(it * Q + q, D + 1, rhs_of, q % 2, (0, 1))
                    add_more(it * Q + q, D + 1, rhs_of, 2)
            pe.wait_ge(s["loaded_e"], 16 * EARLY_LOADS)
            for g, (t0, k) in enumerate(NODE_GROUPS):
                pe.wait_ge(x_loaded[g % 2], 32 * (g // 2 + 1))
                if g >= 2:
                    pe.wait_ge(s["x_used"], g - 1)
                for i in range(k):
                    ins = mm(ps[3 + g % 2][:, i * P:(i + 1) * P], xT_grp[g % 2][:, i * P:(i + 1) * P], w_self[:],
                             start=True, stop=True)
                ins.then_inc(s["x_mm"], 1)
            pe.wait_ge(s["inv_tr"], 1)
            pe.transpose(ps[7][0:TILES, 0:P], inv_deg[:], ident[:]).then_inc(s["inv_tr"], 1)

            def dense_group(g, base):
                t0, k = NODE_GROUPS[g]
                if base + g >= 2:
                    pe.wait_ge(s["dense_taken"], base + g - 1)
                for j in range(TILES):
                    for part in range(2):
                        ins = mm(tiles_of(ps[g % 2], k), split[:, j, part, :], AT[:, t0:t0 + k, j, :],
                                 start=(j == 0 and part == 0), stop=(j == TILES - 1 and part == 1))
                ins.then_inc(s["dense_mm"], 1)

            def turn_group(g, base):
                t0, k = NODE_GROUPS[g]
                if base + g >= 1:
                    pe.wait_ge(s["turn_evac"], base + g)
                for i in range(k):
                    ins = pe.transpose(ps[2][:, i * P:(i + 1) * P], val[:, t0 + i, :], ident[:])
                ins.then_inc(s["turn_mm"], 1)

            def column_sums(src, bank, n):
                pe.wait_ge(s["col_ready"], n)
                for t in range(TILES):
                    k = P if t < TILES - 1 else TAIL
                    ins = mm(ps[bank][:, 0:D], ones[0:k, :], src[0:k, t, :], start=(t == 0), stop=(t == TILES - 1))
                ins.then_inc(s["col_mm"], 1)

            def lin_group(g):
                t0, k = NODE_GROUPS[g]
                pe.wait_ge(s["dense_taken"], g + 1)
                pe.wait_ge(s["turn_evac"], g + 1)
                if g >= 1:
                    pe.wait_ge(s["lin_taken"], g)
                for i in range(k):
                    cols = slice(i * P, (i + 1) * P)
                    mm(ps[3][:, cols], aggT_buf[:, cols], w_l[:], start=True, stop=False)
                    ins = mm(ps[3][:, cols], xT_buf[:, cols], w_r[:], start=False, stop=True)
                ins.then_inc(s["lin_mm"], 1)

            pe.wait_ge(s["split_ready"], 1)
            for g in range(NG):
                dense_group(g, 0)
                if g >= 1:
                    lin_group(g - 1)
                turn_group(g, 0)
            lin_group(NG - 1)
            column_sums(val, 4, 1)
            column_sums(square, 5, 2)

            def hid_group(g):
                t0, k = NODE_GROUPS[g]
                pe.wait_ge(s["dense_taken"], NG + g + 1)
                pe.wait_ge(s["turn_evac"], NG + g + 1)
                for h in range(2):
                    if g >= 1:
                        pe.wait_ge(s["hid_evac"], 2 * (g - 1) + h + 1)
                    mm(ps[3 + h][:, 0:k * P], w1[:, 0, h * D:(h + 1) * D], xT_buf[:, 0:k * P], start=True, stop=False)
                    mm(ps[3 + h][:, 0:k * P], w1[:, 1, h * D:(h + 1) * D], aggT_buf[:, 0:k * P], start=False,
                       stop=True).then_inc(s["hid_mm"], 1)

            def yz_group(g):
                t0, k = NODE_GROUPS[g]
                pe.wait_ge(s["hid_evac"], 2 * g + 2)
                if g >= 1:
                    pe.wait_ge(s["y_evac"], g)
                for i in range(k):
                    for h in range(2):
                        ins = mm(ps[5 + i // 2][:, (i % 2) * 256:(i % 2 + 1) * 256], hT_buf[:, h, i * P:(i + 1) * P],
                                 w2[:, h, :, :].rearrange("p s n -> p (s n)"), start=(h == 0), stop=(h == 1))
                ins.then_inc(s["yz_mm"], 1)

            pe.wait_ge(s["split_ready"], 2)
            for g in range(NG):
                dense_group(g, NG)
                if g >= 1:
                    hid_group(g - 1)
                turn_group(g, NG)
                if g >= 1:
                    yz_group(g - 1)
            hid_group(NG - 1)
            yz_group(NG - 1)
            pe.wait_ge(s["split3_ready"], NG)
            for t in range(TILES):
                if t >= 2:
                    pe.wait_ge(s["sum_taken"], t - 1)
                for j in range(TILES):
                    ins = mm(ps[t % 2][:, 0:3 * D], AT[:, t, j, :], split3[:, j, :, :].rearrange("p s d -> p (s d)"),
                             start=(j == 0), stop=(j == TILES - 1))
                ins.then_inc(s["sum_mm"], 1)

            pe.wait_ge(s["x3_ready"], 1)
            for g, (t0, k) in enumerate(NODE_GROUPS):
                if g >= 2:
                    pe.wait_ge(s["xT3_evac"], g - 1)
                for i in range(k):
                    ins = pe.transpose(ps[g % 2][:, i * P:(i + 1) * P], val[:, t0 + i, :], ident[:])
                ins.then_inc(s["turn3_mm"], 1)
            pe.wait_ge(s["loaded_late"], 16 * LATE_LOADS)
            for t in range(TILES):
                if t % BANK == 0:
                    pe.wait_ge(s["xT3_evac"], t // BANK + 1)
                if t >= 2:
                    pe.wait_ge(s["p_evac"], t - 1)
                mm(ps[2 + t % 2][:, :], x3T[:, t * P:(t + 1) * P], w1a[:, 0, :], start=True, stop=True).then_inc(s["p_mm"], 1)
            for c in range(4):
                ins = mm(ps[7][:, c:c + 1], w1u[:, 2, c * D:(c + 1) * D], u_col[:], start=True, stop=True)
            ins.then_inc(s["ub_mm"], 1)
            pe.wait_ge(s["p_evac"], TILES)

            def edge_products(it, q, first=False):
                pe.wait_ge(edge_loaded[q], it * 16 + 16)
                for u in range(U):
                    if not first:
                        pe.wait_ge(s["pre_done"], it * (Q * U) + (q * U + u + 1 - U))
                    mm(ps[u][0:CHUNK, :], edge_in[:, q, u * CHUNK:(u + 1) * CHUNK], w1a[:, 1, :],
                       start=True, stop=True).then_inc(s["edge_ready"], 1)

            def hidden_rows(it, q, last=False):
                pe.wait_ge(s["relu_done"], it * (Q * U) + (q + 1) * U)
                k = it * Q + q
                pe.wait_ge(s["oh_first_ready"], k + (GROUPS + 1) + 1)
                pe.wait_ge(s["first_added"], k + (GROUPS + 1))
                for u in range(U):
                    ins = mm(ps[4 + q % 2][:, :], onehot[:, q % 2, u, :], hidden[0:CHUNK, q % 2, u, :],
                             start=(u == 0), stop=(u == U - 1))
                ins.then_inc(s["seg_first"], 1)
                add_more(k, HID, lambda u: hidden[0:CHUNK, q % 2, u, :], 6)

            edge_products(0, 0, first=True)
            edge_products(0, 1)
            with pe.Fori(0, ROUNDS - 1) as it:
                for q in range(Q):
                    hidden_rows(it, q)
                    edge_products(it + (q + 2) // Q, (q + 2) % Q)
            for q in range(Q):
                hidden_rows(ROUNDS - 1, q)
                if q + 2 < Q:
                    edge_products(ROUNDS - 1, q + 2)

            pe.wait_ge(s["scaled"], 1)
            for t in range(TILES + 1):
                if t < TILES:
                    if t >= 2:
                        pe.wait_ge(s["hst_evac"], t - 1)
                    for c in range(4):
                        ins = pe.transpose(ps[t % 2][:, c * P:(c + 1) * P], hsum[:, t, c * P:(c + 1) * P], ident[:])
                    ins.then_inc(s["hst_mm"], 1)
                if t >= 1:
                    q = t - 1
                    pe.wait_ge(s["hst_evac"], q + 1)
                    if q >= 2:
                        pe.wait_ge(s["s_evac"], q - 1)
                    for c in range(4):
                        ins = mm(ps[2 + q % 2][:, 0:D], hsT[:, q % 2, c * P:(c + 1) * P], w2a[:, c, :],
                                 start=(c == 0), stop=(c == 3))
                    ins.then_inc(s["s_mm"], 1)
            for g, (t0, k) in enumerate(NODE_GROUPS):
                pe.wait_ge(s["s_evac"], t0 + k)
                if g >= 2:
                    pe.wait_ge(s["xT3_evac"], NG + g - 1)
                for i in range(k):
                    ins = pe.transpose(ps[4 + g % 2][:, i * P:(i + 1) * P], s_nodes[:, t0 + i, :], ident[:])
                ins.then_inc(s["turn3_mm"], 1)
            for g, (t0, k) in enumerate(NODE_GROUPS):
                pe.wait_ge(s["xT3_evac"], NG + g + 1)
                cols = slice(t0 * P, (t0 + k) * P)
                for c in range(4):
                    if g >= 1:
                        pe.wait_ge(s["u_evac"], 4 * (g - 1) + c + 1)
                    mm(ps[c][:, 0:k * P], w1u[:, 0, c * D:(c + 1) * D], x3T[:, cols], start=True, stop=False)
                    mm(ps[c][:, 0:k * P], w1u[:, 1, c * D:(c + 1) * D], sT[:, cols], start=False,
                       stop=True).then_inc(s["u_mm"], 1)
                pe.wait_ge(s["u_evac"], 4 * g + 4)
                if g >= 2:
                    pe.wait_ge(s["o_taken"], g - 1)
                for i in range(k):
                    for c in range(4):
                        ins = mm(ps[6 + g % 2][:, i * P:(i + 1) * P], ubuf[:, g % 2, c, i * P:(i + 1) * P],
                                 w2u[:, c, :], start=(c == 0), stop=(c == 3))
                ins.then_inc(s["o_mm"], 1)
            column_sums(val3, 4, 3)
            column_sums(square, 5, 4)

        @block.vector
        def _(dve):
            chain = [0]

            def link(ins):
                chain[0] += 1
                ins.then_inc(s["dve_step"], 1)
                dve.wait_ge(s["dve_step"], chain[0])

            tt, ts, stt = dve.tensor_tensor, dve.tensor_scalar, dve.scalar_tensor_tensor

            def over_tiles(v, n=TILES):
                return v.rearrange("p (a d) -> p a d", a=1).broadcast_to([P, n, D])

            dve.sem_inc(s["first_added"], 2)
            dve.sem_inc(s["more_added"], 1)
            for x in (*rows_used, *oh_used, *block_taken):
                dve.sem_inc(x, 1)

            dve.wait_ge(s["loaded_dst"], 16)
            link(dve.tensor_copy(dst_gf, dst_g))
            halves = dst_gf.rearrange("g (q e) -> g q e", q=2)
            dve.tensor_reduce(lows[:, 0:2], halves, AX_X, ALU.min)
            link(dve.tensor_reduce(lows[:, 2:4], halves, AX_X, ALU.max))
            tt(spans_f[:, 0:1], lows[:, 0:1], lows[:, 1:2], ALU.min)
            link(tt(spans_f[:, 1:2], lows[:, 2:3], lows[:, 3:4], ALU.max))
            link(dve.tensor_copy(spans_i, spans_f))
            link(ts(spans_i, spans_i, P.bit_length() - 1, None, ALU.arith_shift_right))
            ts(spans_i[:, 1:2], spans_i[:, 1:2], 1, None, ALU.add).then_inc(s["spans_made"], 1)
            dve.wait_ge(s["consts"], 10)
            for q in range(2):
                ts(reach[:, q, 0:SUBS], tile_off[0:GROUPS, :], lows[:, 2 + q:3 + q], weight_c[:, q:q + 1], ALU.is_le, ALU.mult)
                link(ts(reach[:, q, SUBS:], tile_off[0:GROUPS, :], float(SUB), lows[:, q:q + 1], ALU.add, ALU.is_gt))
                link(ts(reach[:, q, SUBS:], reach[:, q, SUBS:], weight_c[:, 2 + q:3 + q], None, ALU.mult))
            tt(reach[:, 0, :], reach[:, 0, :], reach[:, 1, :], ALU.max).then_inc(s["reach_made"], 1)
            dve.wait_ge(s["loaded_idx"], 48)
            stt(rel_c, src_c, float(R), typ_c, ALU.mult, ALU.add).then_inc(s["tables_made"], 1)
            ts(src_f, src_c, float(MID), None, ALU.subtract).then_inc(s["tables_made"], 1)
            dve.tensor_copy(dst_f[:, 0:CHUNKS], dst_c).then_inc(s["tables_made"], 1)

            for t in range(TILES):
                dve.wait_ge(s["rel_mm"], t + 1)
                if t >= 2:
                    dve.wait_ge(rel_stored[t % 2], 16 * (t // 2))
                dve.tensor_copy(wide[:, t % 2, 512:1024], ps[2 * (t % 2) + 1][:, :]).then_inc(s["rel_evac_v"], 1)

            dve.wait_ge(s["reach_tr"], 1)
            dve.tensor_reduce(reach_col, ps[4][0:2 * SUBS, 0:GROUPS], AX_X, ALU.max).then_inc(s["reach_max"], 1)
            dve.wait_ge(s["reach_row"], 1)
            row = reach_line
            link(ts(row[:, 0:SUBS], ps[5][0:1, 0:SUBS], -1.0, float(STEPS), ALU.mult, ALU.add))
            link(ts(row[:, 0:SUBS], row[:, 0:SUBS], float(STEPS - 1), None, ALU.min))
            link(stt(row[:, SUBS:], row[:, 0:SUBS], 1.0, ps[5][0:1, SUBS:2 * SUBS], ALU.add, ALU.max))
            dve.tensor_copy(sub_span[:], row).then_inc(s["subs_made"], 1)
            dve.wait_ge(s["subs_made"], 1)
            dve.wait_ge(s["tables_made"], 3)

            dve.wait_ge(s["spans_out"], 16)
            steps = dve.alloc_register("dve_steps")
            dve.reg_mov(steps, 1)
            with dve.Fori(0, SUBS) as blk:
                first, end = steps_of(dve, blk)
                with dve.Fori(first, end) as step:
                    n = dve.snap(steps, min_val=1, max_val=SUBS * STEPS + 1)
                    for u in range(CP):
                        dve.wait_ge(oh_used[u], n)
                        chunk = bass.ds(step * CP + u, 1)
                        ts(oh_src[:, u, :], src_line, src_f[:, chunk], None, ALU.is_equal)
                        ts(oh_dst[:, u, :], lane[0:CHUNK, 0:SUB], tile_off[0:CHUNK, bass.ds(blk, 1)], dst_f[:, chunk],
                           ALU.add, ALU.is_equal).then_inc(oh_ready[u], 1)
                    dve.reg_add(steps, steps, 1)
            total = dve.snap(steps, min_val=1, max_val=SUBS * STEPS + 1)
            for u in range(CP):
                dve.wait_ge(oh_used[u], total)
            for q in range(Q):
                dve.wait_ge(message_out[q], 16 * ROUNDS)
            link(dve.memset(rows_in[:, :, D:D + 1], 1.0))
            link(dve.memset(agg, 0.0))
            dve.sem_inc(s["agg_clear"], 1)

            more = dve.alloc_register("dve_more")
            dve.reg_mov(more, 1)
            dve.wait_ge(s["spans_in"], 16)

            def one_hots(tile, group, slot, ready):
                for u in range(U):
                    ins = ts(onehot[:, slot, u, :], lane[0:CHUNK, :], tile_off[0:CHUNK, bass.ds(tile * (P // SUB), 1)],
                             dst_f[:, bass.ds(group * U + u, 1)], ALU.add, ALU.is_equal)
                ins.then_inc(ready, 1)

            def add_part(total, tile, bank, width, done):
                part = total[:, bass.ds(tile, 1), 0:width].rearrange("p a d -> p (a d)")
                tt(part, ps[bank][:, 0:width], part, ALU.add).then_inc(done, 1)

            def take_group(group, slot, total, width, banks, more_bank, before, ahead=None):
                nxt, _ = span_of(dve, group + 1)
                one_hots(nxt, group + 1, 1 - slot, s["oh_first_ready"])
                if ahead:
                    ahead()
                first, end = span_of(dve, group)
                dve.wait_ge(s["seg_first"], group + (before + 1))
                dve.wait_ge(s["first_added"], group + (before + 2))
                add_part(total, first, banks[slot], width, s["first_added"])
                with dve.If(end > first + 1):
                    with dve.Fori(first + 1, end) as t:
                        n = dve.snap(more, min_val=1, max_val=2 * GROUPS * TILES + 1)
                        one_hots(t, group, 2, s["more_ready"])
                        dve.wait_ge(s["seg_more"], n)
                        dve.wait_ge(s["more_added"], n)
                        dve.wait_ge(s["first_added"], group + (before + 3))
                        add_part(total, t, more_bank, width, s["more_added"])
                        dve.reg_add(more, more, 1)
                    dve.wait_ge(s["more_added"], dve.snap(more, min_val=1, max_val=2 * GROUPS * TILES + 1))
                    dve.sem_inc(s["wait_carried"], 1)

            first, _ = span_of(dve, 0)
            one_hots(first, 0, 0, s["oh_first_ready"])
            with dve.Fori(0, ROUNDS) as it:
                for q in range(Q):
                    take_group(it * Q + q, q % 2, agg, D + 1, (0, 1), 2, 0)
                    dve.sem_inc(rows_used[q], 1)
            dve.wait_ge(s["first_added"], GROUPS + 2)

            def layer_norm(n_sqrt, v):
                for t in range(TILES):
                    ins = dve.bn_stats(stats[:, t, :], v[:, t, :])
                link(ins)
                for t in range(TILES):
                    ins = dve.bn_aggr(mv[:, t, :], stats[:, t, :])
                link(ins)
                ts(rstd[:], mv[:, :, 1], LN_EPS, None, ALU.add).then_inc(s["var_ready"], 1)
                dve.wait_ge(s["std_ready"], n_sqrt)
                link(dve.reciprocal(rstd[:], rstd[:]))

            def normalise(v):
                for t in range(TILES):
                    ins = ts(v[:, t, :], v[:, t, :], mv[:, t, 0:1], rstd[:, t:t + 1], ALU.subtract, ALU.mult)
                return ins

            def split_rows():
                link(ts(split[:, :, 0, :], val, ROW_SCALE, None, ALU.mult))
                stt(split[:, :, 1, :], val, ROW_SCALE, split[:, :, 0, :], ALU.mult, ALU.subtract).then_inc(s["split_ready"], 1)

            ts(has_edge[:], agg[:, :, D], 0.0, None, ALU.is_gt)
            link(ts(inv_deg[:], agg[:, :, D], 1.0, None, ALU.max))
            dve.reciprocal(inv_deg[:], inv_deg[:]).then_inc(s["inv_tr"], 1)
            for g, (t0, k) in enumerate(NODE_GROUPS):
                dve.wait_ge(s["x_mm"], g + 1)
                part = val[:, t0:t0 + k, :]
                link(tt(part, tiles_of(ps[3 + g % 2], k), part, ALU.add))
                link(tt(part, part, over_tiles(b0_b[:], k), ALU.add))
                link(stt(part, part, 0.0, x_grp[g % 2][:, 0:k * D].rearrange("p (t d) -> p t d", d=D), ALU.max, ALU.add))
                dve.sem_inc(s["x_used"], 1)
            dve.wait_ge(s["inv_tr"], 2)
            dve.tensor_copy(aggT_buf[0:TILES, 256:256 + P], ps[7][0:TILES, 0:P]).then_inc(s["inv_row"], 1)
            layer_norm(1, val)
            normalise(val).then_inc(s["x1_ready"], 1)
            dve.wait_ge(s["x1_ready"], 1)
            split_rows()

            def dense_taken(g, base):
                t0, k = NODE_GROUPS[g]
                dve.wait_ge(s["dense_mm"], base + g + 1)
                dve.wait_ge(inv_loaded, 16 * (base + g + 1))
                stt(aggT_buf[:, 0:k * P], ps[g % 2][:, 0:k * P], 1.0 / ROW_SCALE, inv_b[:, 0:k * P],
                    ALU.mult, ALU.mult).then_inc(s["dense_taken"], 1)

            def lin_taken(g):
                t0, k = NODE_GROUPS[g]
                dve.wait_ge(s["lin_mm"], g + 1)
                tt(val[:, t0:t0 + k, :], tiles_of(ps[3], k), over_tiles(bl_b[:], k), ALU.add).then_inc(s["lin_taken"], 1)

            dve.wait_ge(s["inv_stored"], 16)
            dve.wait_ge(x1_stored, 16)
            for g in range(NG):
                if g >= 1:
                    dve.wait_ge(s["lin_mm"], g)
                dense_taken(g, 0)
                if g >= 1:
                    lin_taken(g - 1)
            lin_taken(NG - 1)
            dve.wait_ge(s["lin_taken"], NG)
            for t in range(TILES):
                ins = dve.tensor_tensor_reduce(square[:, t, :], val[:, t, :], val[:, t, :], 1.0, 0.0,
                                               ALU.mult, ALU.add, small[:, t:t + 1])
            link(ins)
            ts(small[:], small[:], 1e-24, None, ALU.max).then_inc(s["var_ready"], 1)
            dve.wait_ge(s["std_ready"], 2)
            link(dve.reciprocal(small[:], small[:]))
            for t in range(TILES):
                ins = ts(val[:, t, :], val[:, t, :], small[:, t:t + 1], None, ALU.mult)
            ins.then_inc(s["col_ready"], 1)
            dve.wait_ge(s["col_mm"], 1)
            dve.wait_ge(s["col_ready"], 1)
            link(ts(col_a, ps[4][:, 0:D], 1.0 / N, None, ALU.mult))
            link(tt(val, val, over_tiles(col_a), ALU.subtract))
            tt(square, val, val, ALU.mult).then_inc(s["col_ready"], 1)
            dve.wait_ge(s["col_mm"], 2)
            dve.sem_inc(s["square_done"], 1)
            ts(col_b, ps[5][:, 0:D], 1.0 / N, LN_EPS, ALU.mult, ALU.add).then_inc(s["var_ready"], 1)
            dve.wait_ge(s["std_ready"], 3)
            link(dve.reciprocal(col_b, col_b))
            link(tt(col_b, col_b, gamma_b[:], ALU.mult))
            link(tt(val, val, over_tiles(col_b), ALU.mult))
            link(tt(val, val, over_tiles(beta_b[:]), ALU.add))
            dve.wait_ge(s["x1_back"], 16)
            link(stt(val, val, 0.0, square, ALU.max, ALU.add))
            layer_norm(4, val)
            normalise(val).then_inc(s["x2_ready"], 1)
            dve.wait_ge(s["x2_ready"], 1)
            split_rows()

            def y_taken(g):
                t0, k = NODE_GROUPS[g]
                dve.wait_ge(s["z_evac"], g + 1)
                for b in range((k + 1) // 2):
                    n = min(2, k - 2 * b)
                    ins = dve.tensor_copy(val[:, t0 + 2 * b:t0 + 2 * b + n, :],
                                          ps[5 + b][:, 0:n * 256].rearrange("p (t s d) -> p t s d", s=2, d=D)[:, :, 0, :])
                ins.then_inc(s["y_evac"], 1)

            dve.wait_ge(x2_stored, 16)
            for g in range(NG):
                if g >= 1:
                    dve.wait_ge(s["hid_mm"], 2 * g)
                dense_taken(g, NG)
                if g >= 1:
                    y_taken(g - 1)
            y_taken(NG - 1)
            dve.wait_ge(z_stored, 16 * NG)
            for g, (t0, k) in enumerate(NODE_GROUPS):
                dve.wait_ge(z_loaded[g % 2], 16 * (g // 2 + 1))
                zv = z_in[:, g % 2, 0:k * P].rearrange("p (t d) -> p t d", d=D)
                rest = z_mid[:, 0:k * P].rearrange("p (t d) -> p t d", d=D)
                link(dve.tensor_copy(split3[:, t0:t0 + k, 0, :], zv))
                link(tt(rest, zv, split3[:, t0:t0 + k, 0, :], ALU.subtract))
                link(dve.tensor_copy(split3[:, t0:t0 + k, 1, :], rest))
                link(tt(split3[:, t0:t0 + k, 2, :], rest, split3[:, t0:t0 + k, 1, :], ALU.subtract))
                dve.sem_inc(s["z_split"], 1)
                dve.sem_inc(s["split3_ready"], 1)
            for t in range(TILES):
                dve.wait_ge(s["sum_mm"], t + 1)
                tmp = aggT_buf[:, 0:D]
                link(dve.tensor_copy(tmp, ps[t % 2][:, 2 * D:3 * D]))
                link(tt(tmp, ps[t % 2][:, D:2 * D], tmp, ALU.add))
                tt(tmp, ps[t % 2][:, 0:D], tmp, ALU.add).then_inc(s["sum_taken"], 1)
                dve.wait_ge(s["sum_taken"], t + 1)
                link(stt(val[:, t, :], tmp, inv_deg[:, t:t + 1], val[:, t, :], ALU.mult, ALU.add))
            link(tt(val, val, over_tiles(b2_b[:]), ALU.add))
            link(dve.tensor_reduce(small[:], val, AX_X, ALU.max))
            for t in range(TILES):
                ins = ts(val[:, t, :], val[:, t, :], small[:, t:t + 1], None, ALU.subtract)
            ins.then_inc(s["max_ready"], 1)
            dve.wait_ge(s["lse_ready"], 1)
            dve.wait_ge(s["x2_loaded"], 16)
            for t in range(TILES):
                ins = stt(val[:, t, :], val[:, t, :], small[:, t:t + 1], x2_back[:, t, :], ALU.subtract, ALU.add)
            link(ins)
            layer_norm(5, val)
            normalise(val).then_inc(s["x3_ready"], 1)

            dve.wait_ge(s["loaded_late"], 16 * LATE_LOADS)
            for t in range(TILES):
                dve.wait_ge(s["p_mm"], t + 1)
                if t >= 2:
                    dve.wait_ge(p_stored[t % 2], 16 * (t // 2))
                tt(hidden[:, 0, t % 2, :], ps[2 + t % 2][:, :], b1a_b, ALU.add).then_inc(s["p_evac"], 1)
            dve.wait_ge(s["ub_mm"], 1)
            tt(u_bias[:], ps[7][:, 0:4], b1u_col[:], ALU.add).then_inc(s["ub_ready"], 1)
            link(dve.memset(hsum, 0.0))
            dve.wait_ge(p_stored[0], 16 * ((TILES + 1) // 2))
            dve.wait_ge(p_stored[1], 16 * (TILES // 2))

            def hidden_rows(it, q):
                dve.wait_ge(p_gathered[q], it * (16 * U) + 16 * U)
                for u in range(U):
                    dve.wait_ge(s["edge_ready"], it * (Q * U) + (q * U + u + 1))
                    tt(hidden[0:CHUNK, q % 2, u, :], ps[u][0:CHUNK, :], rows_p[0:CHUNK, q * U + u, :],
                       ALU.add).then_inc(s["pre_done"], 1)

            first, _ = span_of(dve, 0)
            one_hots(first, 0, 0, s["oh_first_ready"])
            hidden_rows(0, 0)
            with dve.Fori(0, ROUNDS - 1) as it:
                for q in range(Q):
                    take_group(it * Q + q, q % 2, hsum, HID, (4, 5), 6, GROUPS,
                               lambda: hidden_rows(it + (q + 1) // Q, (q + 1) % Q))
            for q in range(Q):
                take_group((ROUNDS - 1) * Q + q, q % 2, hsum, HID, (4, 5), 6, GROUPS,
                           (lambda: hidden_rows(ROUNDS - 1, q + 1)) if q + 1 < Q else None)
            dve.wait_ge(s["first_added"], 2 * GROUPS + 2)
            for t in range(TILES):
                ins = ts(hsum[:, t, :], hsum[:, t, :], inv_deg[:, t:t + 1], None, ALU.mult)
            ins.then_inc(s["scaled"], 1)
            for t in range(TILES):
                dve.wait_ge(s["s_mm"], t + 1)
                stt(s_nodes[:, t, :], b2a_b, has_edge[:, t:t + 1], ps[2 + t % 2][:, 0:D],
                    ALU.mult, ALU.add).then_inc(s["s_evac"], 1)
            for g, (t0, k) in enumerate(NODE_GROUPS):
                dve.wait_ge(s["o_mm"], g + 1)
                tt(val3[:, t0:t0 + k, :], tiles_of(ps[6 + g % 2], k), over_tiles(b2u_b, k), ALU.add).then_inc(s["o_taken"], 1)
            dve.wait_ge(s["o_taken"], NG)
            tt(val3, val3, val, ALU.add).then_inc(s["col_ready"], 1)
            dve.wait_ge(s["col_mm"], 3)
            dve.wait_ge(s["col_ready"], 3)
            link(stt(col_a, ps[4][:, 0:D], 1.0 / N, gna_b, ALU.mult, ALU.mult))
            link(tt(val3, val3, over_tiles(col_a), ALU.subtract))
            tt(square, val3, val3, ALU.mult).then_inc(s["col_ready"], 1)
            dve.wait_ge(s["col_mm"], 4)
            ts(col_b, ps[5][:, 0:D], 1.0 / N, LN_EPS, ALU.mult, ALU.add).then_inc(s["var_ready"], 1)
            dve.wait_ge(s["std_ready"], 6)
            link(dve.reciprocal(col_b, col_b))
            link(tt(col_b, col_b, gnw_b, ALU.mult))
            link(tt(val3, val3, over_tiles(col_b), ALU.mult))
            link(tt(val3, val3, over_tiles(gnb_b), ALU.add))
            link(tt(val3, val3, val, ALU.add))
            layer_norm(7, val3)
            normalise(val3).then_inc(s["out_ready"], 1)


EARLY_LOADS = 14
LATE_LOADS = 11


def kernel(**inputs):
    import numpy as np
    import concourse.bacc as bacc
    from concourse.bass_utils import run_bass_kernel_spmd

    g = {k: np.ascontiguousarray(v) for k, v in inputs.items()}
    c = np.ascontiguousarray
    chunks = lambda v: c(v.reshape(CHUNKS, CHUNK).T)
    columns = lambda v: c(v.reshape(-1, P).T)
    arrays = {
        "x": g["x"], "xT": c(g["x"].T), "dst": g["dst"],
        "src_c": chunks(g["src"]), "dst_c": chunks(g["dst"]), "typ_c": chunks(g["edge_type_8"]),
        "edgeT": c(g["edge_attr_128"].T),
        "w_rel": c(g["L0_gnn_weight"].transpose(1, 0, 2).reshape(D, R * D)),
        "w_self": g["L0_gnn_self_loop_weight"], "b0": g["L0_gnn_bias"],
        "w_lT": c(g["L1_gnn_W_l"].T), "bl": g["L1_gnn_b_l"], "w_rT": c(g["L1_gnn_W_r"].T),
        "gamma": g["L1_gnn_gamma"], "beta": g["L1_gnn_beta"],
        "w1": g["L2_gnn_W1"], "b1_col": columns(g["L2_gnn_b1"]), "w2": g["L2_gnn_W2"], "b2": g["L2_gnn_b2"],
        "u_col": c(g["L3_gnn_u"][0:1].T), "w1a": g["L3_gnn_W1a"], "b1a": g["L3_gnn_b1a"],
        "w2a": g["L3_gnn_W2a"], "b2a": g["L3_gnn_b2a"], "w1u": g["L3_gnn_W1u"],
        "b1u_col": columns(g["L3_gnn_b1u"]), "w2u": g["L3_gnn_W2u"], "b2u": g["L3_gnn_b2u"],
        "gnw": g["L3_gnn_gn_weight"], "gnb": g["L3_gnn_gn_bias"], "gna": g["L3_gnn_gn_alpha"],
    }
    nc = bacc.Bacc("TRN2", target_bir_lowering=False, num_devices=1)
    aps = {k: nc.dram_tensor("in_" + k, v.shape, mybir.dt.from_np(v.dtype), kind="ExternalInput").ap()
           for k, v in arrays.items()}
    out = nc.dram_tensor("out", (N, D), F32, kind="ExternalOutput").ap()
    build(nc, aps, out)
    r = run_bass_kernel_spmd(nc, [{"in_" + k: v for k, v in arrays.items()}], core_ids=[0])
    return r.results[0]["out"]
```

```python
from contextlib import ExitStack

import concourse.bass as bass
from concourse import mybir

ALU = mybir.AluOpType
ACT = mybir.ActivationFunctionType
F32 = mybir.dt.float32
F16 = mybir.dt.float16
BF16 = mybir.dt.bfloat16
I32 = mybir.dt.int32
AX_X = mybir.AxisListType.X

P = 128
N = 3125
E = 50000
D = 128
R = 8
HID = 4 * D
TILES = (N + P - 1) // P
NP = TILES * P
TAIL = N - (TILES - 1) * P
BANK = 4
CHUNK = 125
U = 4
CHUNKS = E // CHUNK
GROUPS = CHUNKS // U
GE = CHUNK * U
Q = 4
ROUNDS = GROUPS // Q
STEPS = CHUNKS // 2
A_BANKS = (TILES + BANK - 1) // BANK
MID = NP // 2
LN_EPS = 1e-5
ROW_SCALE = 4096.0
assert CHUNK * CHUNKS == E and ROUNDS * Q * U == CHUNKS
assert TILES % BANK == 1 and U == 4
assert MID <= 2048 and (D - 1) ** 0.5 * ROW_SCALE < 65504

NODE_GROUPS = [(g * BANK, min(BANK, TILES - g * BANK)) for g in range((TILES + BANK - 1) // BANK)]
NG = len(NODE_GROUPS)


def build(nc, a, out):
    scratch = lambda name, shape, dt=F32: nc.dram_tensor(name, shape, dt, kind="Internal").ap()
    rel_table = scratch("rel_table", (N * R, 3 * D), BF16)
    x1_table = scratch("x1_table", (NP, D))
    x2_table = scratch("x2_table", (NP, D))
    z_table = scratch("z_table", (NP, D))
    p_table = scratch("p_table", (N, HID))
    inv_table = scratch("inv_table", (NP,))
    tile_table = scratch("tile_table", (GROUPS, 4), I32)

    by_tile = lambda table: table.rearrange("(t p) d -> p t d", p=P)

    with ExitStack() as ctx:
        def sb(name, shape, dt=F32):
            return ctx.enter_context(nc.sbuf_tensor(name, shape, dt))

        def sem(name):
            return ctx.enter_context(nc.semaphore(name))

        arena = sb("arena", [P, TILES * TILES * P], F16)
        AT = arena[:, :].rearrange("p (t j n) -> p t j n", t=TILES, j=TILES)

        def in_arena(start_f32, n_f32):
            return arena[:, 2 * start_f32:2 * (start_f32 + n_f32)].bitcast(F32)

        at = [(TILES - 9) * NP // 2]

        def early(n):
            at[0] += n
            assert at[0] <= TILES * NP // 2
            return in_arena(at[0] - n, n)

        xT = early(NP)
        w_rel = early(R * D)
        rel_parts = early(6 * R * D).bitcast(BF16).rearrange("p (b r s d) -> p b r s d", b=4, r=R, s=3)
        rel_rest = early(2 * R * D).rearrange("p (h r d) -> p h r d", h=4, d=D)
        src_c = early(CHUNKS)[0:CHUNK, :].bitcast(I32)
        typ_c = early(CHUNKS)[0:CHUNK, :].bitcast(I32)
        dst_c = early(CHUNKS)[0:CHUNK, :].bitcast(I32)

        at3 = [0]

        def late(n):
            at3[0] += n
            assert at3[0] <= TILES * NP // 2
            return in_arena(at3[0] - n, n)

        rows_p = late(Q * U * HID).rearrange("p (s h) -> p s h", h=HID)
        w1a = late(2 * HID).rearrange("p (k n) -> p k n", k=2)
        w2a = late(4 * D).rearrange("p (k n) -> p k n", k=4)
        w1u = late(3 * HID).rearrange("p (k n) -> p k n", k=3)
        w2u = late(4 * D).rearrange("p (k n) -> p k n", k=4)
        b1a_b = late(HID)
        b2a_b, b2u_b, gnw_b, gnb_b, gna_b = (late(D) for _ in range(5))
        src_late = late(CHUNKS)[0:CHUNK, :].bitcast(I32)
        weights_tiles = -(-at3[0] // (TILES * P // 2))
        x3T = late(NP)
        hsum = late(TILES * HID).rearrange("p (t h) -> p t h", h=HID)
        hidden = late(2 * U * HID).rearrange("p (b u h) -> p b u h", b=2, u=U)
        edge_in = late(Q * GE).rearrange("p (q e) -> p q e", q=Q)
        x2_back = rows_p.rearrange("p s h -> p (s h)")[:, 0:NP].rearrange("p (t d) -> p t d", d=D)
        ubuf = rows_p.rearrange("p s h -> p (s h)")[:, 0:2 * 4 * 512].rearrange("p (b c n) -> p b c n", b=2, c=4)
        sT = rows_p.rearrange("p s h -> p (s h)")[:, 4096:4096 + NP]
        s_nodes = hidden.rearrange("p b u h -> p (b u h)")[:, 0:NP].rearrange("p (t d) -> p t d", d=D)
        hsT = edge_in.rearrange("p q e -> p (q e)")[:, 0:2 * HID].rearrange("p (b h) -> p b h", b=2)
        val3 = hsum.rearrange("p t h -> p (t h)")[:, 0:NP].rearrange("p (t d) -> p t d", d=D)

        share = sb("share", [P, TILES * 3 * D], F16)
        oh_src = share[0:CHUNK, 0:2 * NP].bitcast(BF16).rearrange("p (u n) -> p u n", u=2)
        src_line = share[0:CHUNK, 2 * NP:3 * NP]
        share_f = share[:, :].bitcast(F32)
        onehot = share_f[0:CHUNK, 2112:2112 + 3 * U * P].rearrange("p (b u n) -> p b u n", b=3, u=U)
        split = share[:, 0:TILES * 2 * D].rearrange("p (t s d) -> p t s d", t=TILES, s=2)
        square = share_f[:, 0:NP].rearrange("p (t d) -> p t d", d=D)
        xT_buf = share_f[:, 3200:3712]
        inv_b = share_f[:, 3712:4224]
        z_out = share_f[:, 4224:4736]
        split3 = share[:, :].bitcast(BF16).rearrange("p (t s d) -> p t s d", t=TILES, s=3)

        nodes = sb("nodes", [P, TILES * (D + 4)])
        agg = nodes[:, :].rearrange("p (t d) -> p t d", d=D + 4)
        deg = agg[:, :, 3]
        val = agg[:, :, 4:D + 4]

        hT_buf = sb("hT_buf", [P, 2, 512])
        x_grp = [share_f[:, 3648:4160], hT_buf[:, 0, :]]
        xT_grp = [share_f[:, 4160:4672], hT_buf[:, 1, :]]
        aggT_buf = sb("aggT_buf", [P, 512])
        dst_g = hT_buf[0:GROUPS, 0, 0:GE].bitcast(I32)
        dst_gf = hT_buf[0:GROUPS, 1, 0:GE]
        rows_g = hT_buf[0:CHUNK, :, :].rearrange("p a n -> p (a n)").bitcast(BF16)[:, 0:U * (3 * D + 2)] \
            .rearrange("p (u d) -> p u d", u=U)
        col_a = hT_buf[:, 0, 0:D]
        col_b = hT_buf[:, 1, 0:D]
        z_in = [hT_buf[:, 0, :], hT_buf[:, 1, :], aggT_buf[:, :]]
        stats = aggT_buf[:, 0:TILES * 6].rearrange("p (t s) -> p t s", s=6)
        rel_c = aggT_buf[0:CHUNK, 0:CHUNKS + 2].bitcast(I32)

        dst_f = sb("dst_f", [CHUNK, CHUNKS + U])
        oh_dst_f = sb("oh_dst", [P, 2 * P])
        oh_dst = oh_dst_f[0:CHUNK, :].bitcast(BF16).rearrange("p (u n) -> p u n", u=U)
        ones = oh_dst_f[:, 0:P]
        zero16 = sb("zero16", [1, P], BF16)
        idx = sb("idx", [CHUNK, Q, U], I32)
        tile_span = sb("tile_span", [1, 2 * TILES], I32)
        lane = sb("lane", [P, P])
        tile_off = sb("tile_off", [P, TILES])
        ident = sb("ident", [P, P])
        w_self = sb("w_self", [P, D])
        w_l = sb("w_l", [P, D])
        w_r = sb("w_r", [P, D])
        w1 = sb("w1", [P, 2, 2 * D])
        src_f = w1[0:CHUNK, :, :].rearrange("p k n -> p (k n)")[:, 0:CHUNKS + 2]
        w2 = sb("w2", [P, 2, 2, D])
        span = w1[0:1, :, :].rearrange("p k n -> p (k n)")[:, 0:4 * (GROUPS + 1)].bitcast(I32)
        b1_col = sb("b1_col", [P, 2])
        b1u_col = sb("b1u_col", [P, 4])
        u_col = sb("u_col", [P, 1])
        b0_b, bl_b, gamma_b, beta_b, b2_b = (sb(n, [P, D]) for n in ("b0_b", "bl_b", "gamma_b", "beta_b", "b2_b"))
        mv = sb("mv", [P, TILES, 2])
        rstd = sb("rstd", [P, TILES])
        inv_deg = sb("inv_deg", [P, TILES])
        has_edge = sb("has_edge", [P, TILES])
        small = sb("small", [P, TILES])
        u_bias = sb("u_bias", [P, 4])
        lows = share_f[0:GROUPS, 1024:1028]
        spans_f = share_f[0:GROUPS, 1032:1036]
        spans_i = share_f[0:GROUPS, 1036:1040].bitcast(I32)
        weight_c = share_f[0:GROUPS, 1040:1044]
        reach = share_f[0:GROUPS, 0:4 * TILES].rearrange("p (q n) -> p q n", q=2)
        reach_col = share_f[0:2 * TILES, 4 * TILES:4 * TILES + 1]
        reach_line = share_f[0:1, 4 * TILES + 4:6 * TILES + 4]

        ps = [ctx.enter_context(nc.psum_tensor(f"ps{i}", [P, 512], F32)) for i in range(8)]

        names = """zeroed loaded_w loaded_dst loaded_idx loaded_late loaded_e loaded_first ones_made consts
            const_step spans_made spans_out spans_in tables_made reach_made reach_tr reach_max reach_row
            tiles_made rel_mm hi_ready rest_ready mid_ready lo_pool lo_dve idx_copied idx3_copied wait_carried
            tile_done bank_taken seg_first oh_first_ready first_added more_ready seg_more more_added a_done
            dve_step act_step x_mm b0_added x_used var_ready std_ready x1_ready x2_ready inv_tr inv_row
            inv_stored split_ready dense_mm dense_taken turn_mm turn_evac lin_mm lin_taken norm_ready split_hi
            col_mm hid_mm hid_evac yz_mm z_evac y_evac sum_mm sum_taken x2_loaded max_ready lse_ready x3_ready
            pre_done relu_done edge_ready p_mm p_evac ub_mm ub_ready edges_done bn_centred bn_squared
            pool_step hsum_zero z_hi z_mid z_lo centred squared scaled_cols res_ready cols_ready hst_mm
            hst_evac s_mm s_evac u_mm u_evac o_mm o_taken out_ready out_stored xT3_evac turn3_mm z_split""".split()
        s = {n: sem(n) for n in names}
        rel_stored = [sem(f"rel_stored{i}") for i in range(4)]
        gathered = [sem(f"gathered{i}") for i in range(U)]
        oh_ready = [sem(f"oh_ready{i}") for i in range(2)]
        oh_used = [sem(f"oh_used{i}") for i in range(2)]
        x_loaded = [sem(f"x_loaded{i}") for i in range(2)]
        x1_stored, x2_stored, z_stored, inv_loaded = sem("x1_stored"), sem("x2_stored"), sem("z_stored"), sem("inv_loaded")
        x1_back = [sem(f"x1_back{i}") for i in range(NG)]
        z_loaded = [sem(f"z_loaded{i}") for i in range(3)]
        p_stored = [sem(f"p_stored{i}") for i in range(8)]
        edge_loaded = [sem(f"edge_loaded{i}") for i in range(Q)]
        p_gathered = [sem(f"p_gathered{i}") for i in range(Q)]

        block = ctx.enter_context(nc.Block())

        def first_tile(eng, group):
            return eng.value_load(span[0:1, bass.ds(group * 4, 1)], min_val=0, max_val=TILES - 1)

        def span_of(eng, group):
            first = first_tile(eng, group)
            end = eng.value_load(span[0:1, bass.ds(group * 4 + 1, 1)], min_val=0, max_val=TILES)
            return first, end

        def steps_of(eng, tile):
            first = eng.value_load(tile_span[0:1, bass.ds(tile, 1)], min_val=0, max_val=STEPS - 1)
            end = eng.value_load(tile_span[0:1, bass.ds(tile + TILES, 1)], min_val=1, max_val=STEPS)
            return first, end

        def count_of(eng, reg):
            return eng.snap(reg, min_val=1, max_val=STEPS * TILES + 2)

        def tiles_of(bank, k):
            return bank[:, 0:k * P].rearrange("p (t d) -> p t d", d=D)

        def over_tiles(v, n=TILES):
            return v.rearrange("p (a d) -> p a d", a=1).broadcast_to([P, n, D])

        @block.sync
        def _(sp):
            def load(dst, src, done):
                sp.dma_start(dst, src).then_inc(done, 16)

            row = lambda name, n: a[name].rearrange("(a n) -> a n", a=1).broadcast_to([P, n])

            load(dst_g, a["dst"].rearrange("(g e) -> g e", e=GE), s["loaded_dst"])
            sp.wait_ge(s["zeroed"], 1)
            load(xT[:, 0:N], a["xT"], s["loaded_w"])
            load(w_rel, a["w_rel"], s["loaded_w"])
            load(src_c, a["src_c"], s["loaded_idx"])
            load(typ_c, a["typ_c"], s["loaded_idx"])
            load(dst_c, a["dst_c"], s["loaded_idx"])
            sp.wait_ge(s["spans_made"], 1)
            load(tile_table, spans_i, s["spans_out"])

            for t in range(TILES):
                n = P if t < TILES - 1 else TAIL
                sp.wait_ge(s["lo_dve"], t + 1)
                sp.wait_ge(s["lo_pool"], t + 1)
                load(rel_table.rearrange("(n r) d -> n (r d)", r=R)[t * P:t * P + n, :],
                     rel_parts[0:n, t % 4, :, :, :].rearrange("p r s d -> p (r s d)"), rel_stored[t % 4])

            sp.wait_ge(s["a_done"], 1)
            early_loads = [(w_self[:], a["w_self"]), (b0_b[:], row("b0", D)), (w_l[:], a["w_lT"]), (w_r[:], a["w_rT"]),
                           (w1[:], a["w1"].rearrange("(k p) n -> p k n", p=P)),
                           (w2[:, :, 0, :], a["w2"][0:2 * D, :].rearrange("(h p) n -> p h n", p=P)),
                           (w2[:, :, 1, :], a["w2"][2 * D:4 * D, :].rearrange("(h p) n -> p h n", p=P)),
                           (b1_col[:], a["b1_col"]), (b1u_col[:], a["b1u_col"]), (u_col[:], a["u_col"]),
                           (bl_b[:], row("bl", D)), (gamma_b[:], row("gamma", D)),
                           (beta_b[:], row("beta", D)), (b2_b[:], row("b2", D))]
            assert len(early_loads) == EARLY_LOADS
            for dst, src in early_loads[:2]:
                load(dst, src, s["loaded_first"])
            for g, (t0, k) in enumerate(NODE_GROUPS):
                if g >= 2:
                    sp.wait_ge(s["x_used"], g - 1)
                full = k if t0 + k < TILES else k - 1
                if full:
                    load(x_grp[g % 2][:, 0:full * D].rearrange("p (t d) -> p t d", d=D),
                         by_tile(a["x"][t0 * P:(t0 + full) * P, :]), x_loaded[g % 2])
                else:
                    load(x_grp[g % 2][0:TAIL, 0:D], a["x"][t0 * P:N, :], x_loaded[g % 2])
                cols = min(N, (t0 + k) * P) - t0 * P
                load(xT_grp[g % 2][:, 0:cols], a["xT"][:, t0 * P:t0 * P + cols], x_loaded[g % 2])
                if g == 1:
                    for dst, src in early_loads[2:]:
                        load(dst, src, s["loaded_e"])

            sp.wait_ge(s["inv_row"], 1)
            load(inv_table.rearrange("(t p) -> t p", p=P), aggT_buf[0:TILES, 256:256 + P], s["inv_stored"])

            def inv_group(g):
                t0, k = NODE_GROUPS[g]
                load(inv_b[:, 0:k * P], inv_table[t0 * P:(t0 + k) * P].rearrange("(a n) -> a n", a=1)
                     .broadcast_to([P, k * P]), inv_loaded)

            sp.wait_ge(s["inv_stored"], 16)
            sp.wait_ge(s["x_used"], NG)
            inv_group(0)
            sp.wait_ge(s["x1_ready"], NG)
            load(by_tile(x1_table), val, x1_stored)
            for g in range(1, NG):
                sp.wait_ge(s["dense_taken"], g)
                inv_group(g)
            sp.wait_ge(s["col_mm"], 2)
            sp.wait_ge(x1_stored, 16)
            for g, (t0, k) in enumerate(NODE_GROUPS):
                load(square[:, t0:t0 + k, :], by_tile(x1_table[t0 * P:(t0 + k) * P, :]), x1_back[g])
            sp.wait_ge(s["x2_ready"], NG)
            load(by_tile(x2_table), val, x2_stored)
            for g, (t0, k) in enumerate(NODE_GROUPS):
                sp.wait_ge(s["dense_taken"], NG + g)
                inv_group(g)
                if g >= 2:
                    gz, (tz, kz) = g - 2, NODE_GROUPS[g - 2]
                    sp.wait_ge(s["z_evac"], gz + 1)
                    load(by_tile(z_table[tz * P:(tz + kz) * P, :]), z_out[:, 0:kz * P].rearrange("p (t d) -> p t d", d=D), z_stored)
            for gz in (NG - 2, NG - 1):
                tz, kz = NODE_GROUPS[gz]
                sp.wait_ge(s["z_evac"], gz + 1)
                load(by_tile(z_table[tz * P:(tz + kz) * P, :]), z_out[:, 0:kz * P].rearrange("p (t d) -> p t d", d=D), z_stored)
            sp.wait_ge(z_stored, 16 * NG)
            for g, (t0, k) in enumerate(NODE_GROUPS):
                if g >= 3:
                    sp.wait_ge(s["z_lo"], g - 2)
                else:
                    sp.wait_ge(s["y_evac"], NG)
                load(tiles_of(z_in[g % 3], k), by_tile(z_table[t0 * P:(t0 + k) * P, :]), z_loaded[g % 3])

            sp.wait_ge(s["spans_out"], 16)
            load(span[:, 0:4 * GROUPS], tile_table.rearrange("(a g) s -> a (g s)", a=1), s["spans_in"])
            load(span[:, 4 * GROUPS:], tile_table[0:1, :], s["spans_in"])
            sp.wait_ge(s["sum_mm"], 2)
            load(x2_back, by_tile(x2_table), s["x2_loaded"])
            late_loads = [(w1a, a["w1a"].rearrange("(k p) n -> p k n", p=P)), (w2a, a["w2a"].rearrange("(k p) n -> p k n", p=P)),
                          (w1u, a["w1u"].rearrange("(k p) n -> p k n", p=P)), (w2u, a["w2u"].rearrange("(k p) n -> p k n", p=P)),
                          (b1a_b, row("b1a", HID)), (b2a_b, row("b2a", D)), (b2u_b, row("b2u", D)),
                          (gnw_b, row("gnw", D)), (gnb_b, row("gnb", D)), (gna_b, row("gna", D)), (src_late, a["src_c"])]
            assert len(late_loads) == LATE_LOADS
            sp.wait_ge(s["sum_mm"], weights_tiles)
            for dst, src in late_loads:
                load(dst, src, s["loaded_late"])

            def load_edges(it, q):
                load(edge_in[:, q, :], a["edgeT"][:, bass.ds((it * Q + q) * GE, GE)], edge_loaded[q])

            sp.wait_ge(s["sum_mm"], TILES)
            for q in range(Q):
                load_edges(0, q)
            for t in range(TILES):
                n = P if t < TILES - 1 else TAIL
                sp.wait_ge(s["p_evac"], t + 1)
                load(p_table[t * P:t * P + n, :], hidden[0:n, t // 4 % 2, t % 4, :], p_stored[t % 8])
            with sp.Fori(1, ROUNDS) as it:
                for q in range(Q):
                    sp.wait_ge(s["edge_ready"], it * (Q * U) + ((q + 1) * U - Q * U))
                    load_edges(it, q)

            for g, (t0, k) in enumerate(NODE_GROUPS):
                sp.wait_ge(s["out_ready"], g + 1)
                if t0 + k < TILES:
                    load(by_tile(out[t0 * P:(t0 + k) * P, :]), val3[:, t0:t0 + k, :], s["out_stored"])
                else:
                    assert k == 1
                    load(out[N - TAIL:N, :], val3[0:TAIL, TILES - 1, :], s["out_stored"])
            sp.wait_ge(s["out_stored"], 16 * NG)
            sp.wait_ge(x2_stored, 16)
            sp.wait_ge(x1_stored, 16)

        @block.gpsimd
        def _(pool):
            pool.memset(xT[:, N:NP], 0.0).then_inc(s["zeroed"], 1)
            pool.memset(ident[:], 0.0).then_inc(s["const_step"], 1)
            pool.iota(tile_off[:], pattern=[[P, TILES]], base=0, channel_multiplier=0,
                      allow_small_or_imprecise_dtypes=True).then_inc(s["consts"], 1)
            pool.iota(weight_c[:, 0:2], pattern=[[-1, 2]], base=STEPS, channel_multiplier=-2,
                      allow_small_or_imprecise_dtypes=True).then_inc(s["consts"], 1)
            pool.iota(weight_c[:, 2:4], pattern=[[1, 2]], base=1, channel_multiplier=2,
                      allow_small_or_imprecise_dtypes=True).then_inc(s["consts"], 1)
            pool.iota(lane[:], pattern=[[1, P]], base=0, channel_multiplier=0,
                      allow_small_or_imprecise_dtypes=True).then_inc(s["consts"], 1)
            pool.iota(src_line, pattern=[[1, NP]], base=-MID, channel_multiplier=0,
                      allow_small_or_imprecise_dtypes=True).then_inc(s["consts"], 1)
            pool.memset(zero16[:], 0.0).then_inc(s["consts"], 1)
            pool.memset(dst_f[:, CHUNKS:], -1.0).then_inc(s["consts"], 1)
            pool.wait_ge(s["const_step"], 1)
            pool.affine_select(out=ident[:], in_=ident[:], compare_op=ALU.not_equal, fill=1.0,
                               base=0, pattern=[[-1, P]], channel_multiplier=1).then_inc(s["consts"], 1)

            def gather_group(q, table, buf, index, it, done):
                pool.tensor_copy(idx[:, q, :], index[:, bass.ds((it * Q + q) * U, U)]).then_inc(s["idx3_copied"], 1)
                pool.wait_ge(s["idx3_copied"], (q + 1) + it * Q)
                pool.sem_inc(s["wait_carried"], 1)
                for u in range(U):
                    pool.indirect_dma_start(buf[0:CHUNK, q * U + u, :], None, table,
                                            bass.IndirectOffsetOnAxis(ap=idx[:, q, u:u + 1], axis=0)).then_inc(done[q], 16)

            for n in range(1, 2 * TILES, 2):
                pool.wait_ge(s["mid_ready"], n + 1)
                part = rel_parts[:, (n // 2) % 4, (n % 2) * 4:(n % 2) * 4 + 4, :, :]
                pool.tensor_tensor(part[:, :, 2, :], rel_rest[:, n % 4], part[:, :, 1, :], ALU.subtract).then_inc(s["lo_pool"], 1)

            step_no = pool.alloc_register("pool_step_no")
            last_use = [pool.alloc_register(f"pool_last_use{i}") for i in range(2)]
            for reg in (step_no, *last_use):
                pool.reg_mov(reg, 1)

            def gather_step(step, half):
                pool.wait_ge(oh_used[1], count_of(pool, last_use[half]))
                cols = slice(2 * half, 2 * half + 2)
                pool.tensor_copy(idx[:, 0, cols], rel_c[:, bass.ds(step * 2, 2)]).then_inc(s["idx_copied"], 1)
                pool.wait_ge(s["idx_copied"], count_of(pool, step_no))
                pool.sem_inc(s["wait_carried"], 1)
                for u in (2 * half, 2 * half + 1):
                    pool.indirect_dma_start(rows_g[:, u, 2:2 + 3 * D], None, rel_table,
                                            bass.IndirectOffsetOnAxis(ap=idx[:, 0, u:u + 1], axis=0)).then_inc(gathered[u], 16)
                pool.reg_add(last_use[half], step_no, 1)
                pool.reg_add(step_no, step_no, 1)

            pool.wait_ge(s["tables_made"], 3)
            pool.wait_ge(s["tiles_made"], 1)
            pool.memset(rows_g[:, :, 1:2], 1.0).then_inc(s["const_step"], 1)
            for b in range(4):
                pool.wait_ge(rel_stored[b], 16 * ((TILES + 3 - b) // 4))
            pool.sem_inc(s["wait_carried"], 1)
            with pool.Fori(0, TILES) as t:
                first, end = steps_of(pool, t)
                with pool.Fori(first, end, 2) as step:
                    gather_step(step, 0)
                    with pool.If(end > step + 1):
                        gather_step(step + 1, 1)

            pool.wait_ge(s["a_done"], 1)
            pool.memset(ones, 1.0).then_inc(s["ones_made"], 1)
            def scale_columns(v, shift, norm):
                pool.wait_ge(s["cols_ready"], norm + 1)
                for g, (t0, k) in enumerate(NODE_GROUPS):
                    part = v[:, t0:t0 + k, :]
                    pool.tensor_tensor(part, part, over_tiles(col_b, k), ALU.mult).then_inc(s["pool_step"], 1)
                    pool.wait_ge(s["pool_step"], norm * NG + g + 1)
                    pool.tensor_tensor(part, part, over_tiles(shift, k), ALU.add).then_inc(s["scaled_cols"], 1)

            pool.wait_ge(s["bank_taken"], A_BANKS * (TILES + 1))
            pool.wait_ge(s["loaded_first"], 32)
            for t0, k in NODE_GROUPS:
                part = val[:, t0:t0 + k, :]
                pool.tensor_tensor(part, part, over_tiles(b0_b[:], k), ALU.add).then_inc(s["b0_added"], 1)

            scale_columns(val, beta_b[:], 0)
            for g, (t0, k) in enumerate(NODE_GROUPS):
                pool.wait_ge(s["z_mid"], g + 1)
                pool.tensor_tensor(split3[:, t0:t0 + k, 2, :], tiles_of(z_in[g % 3], k), split3[:, t0:t0 + k, 1, :],
                                   ALU.subtract).then_inc(s["z_lo"], 1)

            pool.wait_ge(s["sum_mm"], TILES)
            pool.memset(hsum, 0.0).then_inc(s["hsum_zero"], 1)
            pool.wait_ge(s["loaded_late"], 16 * LATE_LOADS)
            for b in range(8):
                pool.wait_ge(p_stored[b], 16 * ((TILES + 7 - b) // 8))
            for q in range(Q):
                gather_group(q, p_table, rows_p, src_late, 0, p_gathered)
            with pool.Fori(1, ROUNDS) as it:
                for q in range(Q):
                    pool.wait_ge(s["pre_done"], it * (Q * U) + ((q + 1) * U - Q * U))
                    gather_group(q, p_table, rows_p, src_late, it, p_gathered)

            scale_columns(val3, gnb_b, 1)

        @block.scalar
        def _(act):
            def mid(n):
                act.wait_ge(s["rest_ready"], n + 1)
                part = rel_parts[:, (n // 2) % 4, (n % 2) * 4:(n % 2) * 4 + 4, :, :]
                act.copy(part[:, :, 1, :], rel_rest[:, n % 4]).then_inc(s["mid_ready"], 1)

            for n in range(2 * TILES):
                t = n // 2
                act.wait_ge(s["rel_mm"], n + 1)
                if t >= 4:
                    act.wait_ge(rel_stored[t % 4], 16 * (t // 4))
                part = rel_parts[:, t % 4, (n % 2) * 4:(n % 2) * 4 + 4, :, :]
                act.copy(part[:, :, 0, :], ps[n % 4][:, :].rearrange("p (r d) -> p r d", d=D)).then_inc(s["hi_ready"], 1)
                if n >= 1:
                    mid(n - 1)
            mid(2 * TILES - 1)

            for b in range(4):
                act.wait_ge(rel_stored[b], 16 * ((TILES + 3 - b) // 4))
            act.wait_ge(s["tables_made"], 3)
            with act.Fori(0, TILES) as t:
                act.wait_ge(s["tile_done"], t + 1)
                for b in range(A_BANKS):
                    j0, j1 = b * BANK, min(TILES, (b + 1) * BANK)
                    ins = act.copy(AT[:, bass.ds(t, 1), j0:j1, :].rearrange("p a j n -> p (a j) n"),
                                   tiles_of(ps[b], j1 - j0))
                    if b == A_BANKS - 1:
                        ins = act.copy(agg[:, bass.ds(t, 1), 3:D + 4].rearrange("p a d -> p (a d)"), ps[b][:, P:P + D + 1])
                    ins.then_inc(s["bank_taken"], 1)

            roots = [0]

            def sqrt_of(arr):
                roots[0] += 1
                act.wait_ge(s["var_ready"], roots[0])
                act.activation(arr, arr, ACT.Sqrt).then_inc(s["std_ready"], 1)

            def roots_and_split(base):
                for g in range(NG + 1):
                    if g < NG:
                        t0, k = NODE_GROUPS[g]
                        sqrt_of(rstd[:, t0:t0 + k])
                    if g >= 1:
                        t0, k = NODE_GROUPS[g - 1]
                        act.wait_ge(s["x1_ready"] if base == 0 else s["x2_ready"], g)
                        act.activation(split[:, t0:t0 + k, 0, :], val[:, t0:t0 + k, :], ACT.Copy,
                                       scale=ROW_SCALE).then_inc(s["split_hi"], 1)

            roots_and_split(0)
            for g, (t0, k) in enumerate(NODE_GROUPS):
                act.wait_ge(s["turn_mm"], g + 1)
                if g >= 1:
                    act.wait_ge(s["lin_mm"], g)
                act.copy(xT_buf[:, 0:k * P], ps[2][:, 0:k * P]).then_inc(s["turn_evac"], 1)
                if g >= 1:
                    t1, k1 = NODE_GROUPS[g - 1]
                    sqrt_of(small[:, t1:t1 + k1])
            t1, k1 = NODE_GROUPS[NG - 1]
            sqrt_of(small[:, t1:t1 + k1])
            for g, (t0, k) in enumerate(NODE_GROUPS):
                act.wait_ge(s["bn_centred"], g + 1)
                act.activation(square[:, t0:t0 + k, :], val[:, t0:t0 + k, :], ACT.Square).then_inc(s["bn_squared"], 1)
            sqrt_of(col_b)
            roots_and_split(NG)

            act.wait_ge(s["loaded_e"], 16 * (EARLY_LOADS - 2))

            def hidden_group(g):
                t0, k = NODE_GROUPS[g]
                for h in range(2):
                    act.wait_ge(s["hid_mm"], 2 * g + h + 1)
                    if g >= 1:
                        act.wait_ge(s["yz_mm"], g)
                    act.activation(hT_buf[:, h, 0:k * P], ps[3 + h][:, 0:k * P], ACT.Relu,
                                   bias=b1_col[:, h:h + 1]).then_inc(s["hid_evac"], 1)

            def z_group(g):
                t0, k = NODE_GROUPS[g]
                act.wait_ge(s["yz_mm"], g + 1)
                if g >= 1:
                    act.wait_ge(z_stored, 16 * g)
                for b in range((k + 1) // 2):
                    n = min(2, k - 2 * b)
                    ins = act.copy(z_out[:, 2 * b * P:(2 * b + n) * P].rearrange("p (t d) -> p t d", d=D),
                                   ps[5 + b][:, 0:n * 256].rearrange("p (t s d) -> p t s d", s=2, d=D)[:, :, 1, :])
                ins.then_inc(s["z_evac"], 1)

            for g, (t0, k) in enumerate(NODE_GROUPS):
                if g >= 1:
                    hidden_group(g - 1)
                act.wait_ge(s["turn_mm"], NG + g + 1)
                act.copy(xT_buf[:, 0:k * P], ps[2][:, 0:k * P]).then_inc(s["turn_evac"], 1)
                if g >= 1:
                    z_group(g - 1)
            hidden_group(NG - 1)
            z_group(NG - 1)

            for g in range(NG + 1):
                if g < NG:
                    t0, k = NODE_GROUPS[g]
                    act.wait_ge(z_loaded[g % 3], 16 * (g // 3 + 1))
                    act.copy(split3[:, t0:t0 + k, 0, :], tiles_of(z_in[g % 3], k)).then_inc(s["z_hi"], 1)
                if g >= 1:
                    t0, k = NODE_GROUPS[g - 1]
                    act.wait_ge(s["z_split"], g)
                    act.copy(split3[:, t0:t0 + k, 1, :], tiles_of(z_in[(g - 1) % 3], k)).then_inc(s["z_mid"], 1)

            for g in range(NG + 2):
                if g < NG:
                    t0, k = NODE_GROUPS[g]
                    act.wait_ge(s["max_ready"], g + 1)
                    for t in range(t0, t0 + k):
                        ins = act.activation(hT_buf[:, t % 8 // 4, (t % 4) * D:(t % 4 + 1) * D], val[:, t, :], ACT.Exp, accum_out=small[:, t:t + 1])
                    ins.then_inc(s["act_step"], 1)
                    act.wait_ge(s["act_step"], g + 1)
                    act.activation(small[:, t0:t0 + k], small[:, t0:t0 + k], ACT.Ln).then_inc(s["lse_ready"], 1)
                if 1 <= g <= NG:
                    t0, k = NODE_GROUPS[g - 1]
                    sqrt_of(rstd[:, t0:t0 + k])
                if g >= 2:
                    t0, k = NODE_GROUPS[g - 2]
                    act.wait_ge(s["turn3_mm"], g - 1)
                    act.copy(x3T[:, t0 * P:(t0 + k) * P], ps[4 + g % 2][:, 0:k * P]).then_inc(s["xT3_evac"], 1)

            with act.Fori(0, GROUPS // 2) as it:
                for half in range(2):
                    for u in range(U):
                        act.wait_ge(s["pre_done"], it * (2 * U) + (half * U + u + 1))
                        row = hidden[0:CHUNK, half, u, :]
                        act.activation(row, row, ACT.Relu).then_inc(s["relu_done"], 1)
            for t in range(TILES):
                act.wait_ge(s["hst_mm"], t + 1)
                if t >= 2:
                    act.wait_ge(s["s_mm"], t - 1)
                act.copy(hsT[:, t % 2, :], ps[t % 2][:, :]).then_inc(s["hst_evac"], 1)
            for g, (t0, k) in enumerate(NODE_GROUPS):
                act.wait_ge(s["turn3_mm"], NG + g + 1)
                act.copy(sT[:, t0 * P:(t0 + k) * P], ps[4 + g % 2][:, 0:k * P]).then_inc(s["xT3_evac"], 1)
            act.wait_ge(s["ub_ready"], 1)
            for g, (t0, k) in enumerate(NODE_GROUPS):
                for c in range(4):
                    act.wait_ge(s["u_mm"], 4 * g + c + 1)
                    if g >= 2:
                        act.wait_ge(s["o_mm"], g - 1)
                    act.activation(ubuf[:, g % 2, c, 0:k * P], ps[c][:, 0:k * P], ACT.Relu,
                                   bias=u_bias[:, c:c + 1]).then_inc(s["u_evac"], 1)
            for g, (t0, k) in enumerate(NODE_GROUPS):
                act.wait_ge(s["centred"], g + 1)
                act.activation(square[:, t0:t0 + k, :], val3[:, t0:t0 + k, :], ACT.Square).then_inc(s["squared"], 1)
            sqrt_of(col_b)
            for t0, k in NODE_GROUPS:
                sqrt_of(rstd[:, t0:t0 + k])

        @block.tensor
        def _(pe):
            mm = pe.matmul
            pe.wait_ge(s["loaded_w"], 32)
            for n in range(2 * TILES):
                if n >= 4:
                    pe.wait_ge(s["rest_ready"], n - 3)
                t, h = n // 2, n % 2
                mm(ps[n % 4][:, :], xT[:, t * P:(t + 1) * P], w_rel[:, h * 512:(h + 1) * 512],
                   start=True, stop=True).then_inc(s["rel_mm"], 1)

            pe.wait_ge(s["consts"], 8)
            pe.wait_ge(s["reach_made"], 1)
            pe.transpose(ps[4][0:2 * TILES, 0:GROUPS], reach[:, 0, :], ident[0:GROUPS, 0:GROUPS]).then_inc(s["reach_tr"], 1)
            pe.wait_ge(s["reach_max"], 1)
            pe.transpose(ps[5][0:1, 0:2 * TILES], reach_col, ident[0:2 * TILES, 0:2 * TILES]).then_inc(s["reach_row"], 1)

            step_no = pe.alloc_register("pe_step_no")
            half_no = [pe.alloc_register(f"pe_half_no{i}") for i in range(2)]
            for reg in (step_no, *half_no):
                pe.reg_mov(reg, 1)

            def sum_step(t, half, opening=False):
                n = count_of(pe, step_no)
                n_half = count_of(pe, half_no[half])
                for slot in range(2):
                    u = 2 * half + slot
                    opens = opening and slot == 0
                    pe.wait_ge(oh_ready[slot], n)
                    for j in range(TILES):
                        if opens and j % BANK == 0:
                            pe.wait_ge(s["bank_taken"], t * A_BANKS + (j // BANK + 1))
                        c0 = (j % BANK) * P
                        mm(ps[j // BANK][:, c0:c0 + P], oh_src[:, slot, j * P:(j + 1) * P], oh_dst[:, u, :],
                           start=opens and j % BANK == 0, stop=False, skip_group_check=True)
                    pe.wait_ge(gathered[u], n_half * 16)
                    bank = ps[A_BANKS - 1]
                    mm(bank[:, P:P + D + 1], oh_dst[:, u, :], rows_g[:, u, 1:D + 2], start=False, stop=False,
                       skip_group_check=True)
                    for part in (1, 2):
                        ins = mm(bank[:, P + 1:P + D + 1], oh_dst[:, u, :], rows_g[:, u, 2 + part * D:2 + (part + 1) * D],
                                 start=False, stop=False, skip_group_check=True)
                    ins.then_inc(oh_used[slot], 1)
                pe.reg_add(step_no, step_no, 1)
                pe.reg_add(half_no[half], half_no[half], 1)

            pe.wait_ge(s["tiles_made"], 1)
            pe.wait_ge(s["rest_ready"], 2 * TILES)
            pe.wait_ge(s["const_step"], 2)
            with pe.Fori(0, TILES) as t:
                first, end = steps_of(pe, t)
                sum_step(t, 0, opening=True)
                with pe.If(end > first + 1):
                    sum_step(t, 1)
                with pe.If(end > first + 2):
                    with pe.Fori(first + 2, end, 2) as step:
                        sum_step(t, 0)
                        with pe.If(end > step + 1):
                            sum_step(t, 1)
                mm(ps[A_BANKS - 1][:, 0:P], zero16[:], zero16[:], start=False, stop=True,
                   skip_group_check=True).then_inc(s["tile_done"], 1)

            more = pe.alloc_register("pe_more")
            pe.reg_mov(more, 1)

            pe.wait_ge(s["bank_taken"], A_BANKS * (TILES + 1))
            pe.wait_ge(s["inv_tr"], 1)
            pe.transpose(ps[7][0:TILES, 0:P], inv_deg[:], ident[:]).then_inc(s["inv_tr"], 1)
            pe.wait_ge(s["loaded_first"], 32)
            for g, (t0, k) in enumerate(NODE_GROUPS):
                pe.wait_ge(x_loaded[g % 2], 32 * (g // 2 + 1))
                if g >= 2:
                    pe.wait_ge(s["x_used"], g - 1)
                for i in range(k):
                    ins = mm(ps[3 + g % 2][:, i * P:(i + 1) * P], xT_grp[g % 2][:, i * P:(i + 1) * P], w_self[:],
                             start=True, stop=True)
                ins.then_inc(s["x_mm"], 1)

            def dense_group(g, base):
                t0, k = NODE_GROUPS[g]
                if base + g >= 2:
                    pe.wait_ge(s["dense_taken"], base + g - 1)
                for j in range(TILES):
                    if g == 0 and j % BANK == 0:
                        pe.wait_ge(s["split_ready"], base + j // BANK + 1)
                    for part in range(2):
                        ins = mm(tiles_of(ps[g % 2], k), split[:, j, part, :], AT[:, t0:t0 + k, j, :],
                                 start=(j == 0 and part == 0), stop=(j == TILES - 1 and part == 1))
                ins.then_inc(s["dense_mm"], 1)

            def turn_group(g, base):
                t0, k = NODE_GROUPS[g]
                if base + g >= 1:
                    pe.wait_ge(s["turn_evac"], base + g)
                for i in range(k):
                    ins = pe.transpose(ps[2][:, i * P:(i + 1) * P], val[:, t0 + i, :], ident[:])
                ins.then_inc(s["turn_mm"], 1)

            def column_sum(src, bank, g, ready):
                pe.wait_ge(ready, g + 1)
                t0, k = NODE_GROUPS[g]
                for t in range(t0, t0 + k):
                    n = P if t < TILES - 1 else TAIL
                    ins = mm(ps[bank][:, 0:D], ones[0:n, :], src[0:n, t, :], start=(t == 0), stop=(t == TILES - 1))
                if g == NG - 1:
                    ins.then_inc(s["col_mm"], 1)

            pe.wait_ge(s["loaded_e"], 16 * (EARLY_LOADS - 2))
            pe.wait_ge(s["ones_made"], 1)

            def lin_group(g):
                t0, k = NODE_GROUPS[g]
                pe.wait_ge(s["dense_taken"], g + 1)
                pe.wait_ge(s["turn_evac"], g + 1)
                if g >= 1:
                    pe.wait_ge(s["lin_taken"], g)
                for i in range(k):
                    cols = slice(i * P, (i + 1) * P)
                    mm(ps[3][:, cols], aggT_buf[:, cols], w_l[:], start=True, stop=False)
                    ins = mm(ps[3][:, cols], xT_buf[:, cols], w_r[:], start=False, stop=True)
                ins.then_inc(s["lin_mm"], 1)

            for g in range(NG):
                dense_group(g, 0)
                if g >= 1:
                    lin_group(g - 1)
                turn_group(g, 0)
                if g >= 2:
                    column_sum(val, 4, g - 2, s["norm_ready"])
            lin_group(NG - 1)
            column_sum(val, 4, NG - 2, s["norm_ready"])
            column_sum(val, 4, NG - 1, s["norm_ready"])
            for g in range(NG):
                column_sum(square, 5, g, s["bn_squared"])

            def hid_group(g):
                t0, k = NODE_GROUPS[g]
                pe.wait_ge(s["dense_taken"], NG + g + 1)
                pe.wait_ge(s["turn_evac"], NG + g + 1)
                for h in range(2):
                    if g >= 1:
                        pe.wait_ge(s["hid_evac"], 2 * (g - 1) + h + 1)
                    mm(ps[3 + h][:, 0:k * P], w1[:, 0, h * D:(h + 1) * D], xT_buf[:, 0:k * P], start=True, stop=False)
                    mm(ps[3 + h][:, 0:k * P], w1[:, 1, h * D:(h + 1) * D], aggT_buf[:, 0:k * P], start=False,
                       stop=True).then_inc(s["hid_mm"], 1)

            def yz_group(g):
                t0, k = NODE_GROUPS[g]
                pe.wait_ge(s["hid_evac"], 2 * g + 2)
                if g >= 1:
                    pe.wait_ge(s["y_evac"], g)
                for i in range(k):
                    for h in range(2):
                        ins = mm(ps[5 + i // 2][:, (i % 2) * 256:(i % 2 + 1) * 256], hT_buf[:, h, i * P:(i + 1) * P],
                                 w2[:, h, :, :].rearrange("p s n -> p (s n)"), start=(h == 0), stop=(h == 1))
                ins.then_inc(s["yz_mm"], 1)

            for g in range(NG):
                dense_group(g, NG)
                if g >= 1:
                    hid_group(g - 1)
                turn_group(g, NG)
                if g >= 1:
                    yz_group(g - 1)
            hid_group(NG - 1)
            yz_group(NG - 1)
            def turn3_group(g):
                t0, k = NODE_GROUPS[g]
                pe.wait_ge(s["x3_ready"], g + 1)
                if g >= 2:
                    pe.wait_ge(s["xT3_evac"], g - 1)
                for i in range(k):
                    ins = pe.transpose(ps[4 + g % 2][:, i * P:(i + 1) * P], val[:, t0 + i, :], ident[:])
                ins.then_inc(s["turn3_mm"], 1)

            for g, (t0, k) in enumerate(NODE_GROUPS):
                for t in range(t0, t0 + k):
                    if t >= 4:
                        pe.wait_ge(s["sum_taken"], t - 3)
                    for j in range(TILES):
                        if t == 0 and j % BANK == 0:
                            pe.wait_ge(s["z_lo"], j // BANK + 1)
                        ins = mm(ps[t % 4][:, 0:3 * D], AT[:, t, j, :], split3[:, j, :, :].rearrange("p s d -> p (s d)"),
                                 start=(j == 0), stop=(j == TILES - 1))
                    ins.then_inc(s["sum_mm"], 1)
                if g >= 2:
                    turn3_group(g - 2)
            turn3_group(NG - 2)
            turn3_group(NG - 1)

            pe.wait_ge(s["sum_taken"], TILES)
            pe.wait_ge(s["loaded_late"], 16 * LATE_LOADS)
            for t in range(TILES):
                if t % BANK == 0:
                    pe.wait_ge(s["xT3_evac"], t // BANK + 1)
                if t >= 4:
                    pe.wait_ge(s["p_evac"], t - 3)
                mm(ps[t % 4][:, :], x3T[:, t * P:(t + 1) * P], w1a[:, 0, :], start=True, stop=True).then_inc(s["p_mm"], 1)
            for c in range(4):
                ins = mm(ps[7][:, c:c + 1], w1u[:, 2, c * D:(c + 1) * D], u_col[:], start=True, stop=True)
            ins.then_inc(s["ub_mm"], 1)
            pe.wait_ge(s["p_evac"], TILES)

            pe.wait_ge(s["spans_in"], 32)
            def edge_products(it, q, first=False):
                pe.wait_ge(edge_loaded[q], it * 16 + 16)
                for u in range(U):
                    if not first:
                        pe.wait_ge(s["pre_done"], it * (Q * U) + (q * U + u + 1 - U))
                    mm(ps[u][0:CHUNK, :], edge_in[:, q, u * CHUNK:(u + 1) * CHUNK], w1a[:, 1, :],
                       start=True, stop=True).then_inc(s["edge_ready"], 1)

            def add_chunks(bank, slot, q, chunks, done):
                for u in chunks:
                    ins = mm(ps[bank][:, :], onehot[:, slot, u, :], hidden[0:CHUNK, q % 2, u, :],
                             start=(u == chunks[0]), stop=(u == chunks[-1]))
                ins.then_inc(done, 1)

            def hidden_rows(it, q):
                pe.wait_ge(s["relu_done"], it * (Q * U) + (q + 1) * U)
                k = it * Q + q
                pe.wait_ge(s["oh_first_ready"], k + 1)
                pe.wait_ge(s["first_added"], k + 1)
                first = first_tile(pe, k)
                later = pe.value_load(span[0:1, bass.ds(k * 4 + 3, 1)], min_val=0, max_val=TILES - 1)
                with pe.If(later > first):
                    add_chunks(4 + q % 2, q % 2, q, (0, 1), s["seg_first"])
                with pe.If(later < first + 1):
                    add_chunks(4 + q % 2, q % 2, q, range(U), s["seg_first"])

            def more_spans(it, q):
                k = it * Q + q
                first, end = span_of(pe, k)
                return first, end, pe.value_load(span[0:1, bass.ds(k * 4 + 2, 1)], min_val=1, max_val=TILES)

            def more_rows(first, end, early_end, q):
                with pe.If(end > first + 1):
                    with pe.Fori(first + 1, end) as t:
                        n = pe.snap(more, min_val=1, max_val=2 * GROUPS * TILES + 1)
                        pe.wait_ge(s["more_ready"], n)
                        pe.wait_ge(s["more_added"], n)
                        with pe.If(early_end > t):
                            add_chunks(6, 2, q, range(U), s["seg_more"])
                        with pe.If(early_end < t + 1):
                            add_chunks(6, 2, q, range(2, U), s["seg_more"])
                        pe.reg_add(more, more, 1)

            edge_products(0, 0, first=True)
            edge_products(0, 1)
            with pe.Fori(0, ROUNDS - 1) as it:
                for q in range(Q):
                    hidden_rows(it, q)
                    spans = more_spans(it, q)
                    edge_products(it + (q + 2) // Q, (q + 2) % Q)
                    more_rows(*spans, q)
            for q in range(Q):
                hidden_rows(ROUNDS - 1, q)
                spans = more_spans(ROUNDS - 1, q)
                if q + 2 < Q:
                    edge_products(ROUNDS - 1, q + 2)
                more_rows(*spans, q)

            pe.wait_ge(s["edges_done"], 1)
            for t in range(TILES + 1):
                if t < TILES:
                    if t >= 2:
                        pe.wait_ge(s["hst_evac"], t - 1)
                    for c in range(4):
                        ins = pe.transpose(ps[t % 2][:, c * P:(c + 1) * P], hsum[:, t, c * P:(c + 1) * P], ident[:])
                    ins.then_inc(s["hst_mm"], 1)
                if t >= 1:
                    q = t - 1
                    pe.wait_ge(s["hst_evac"], q + 1)
                    if q >= 2:
                        pe.wait_ge(s["s_evac"], q - 1)
                    for c in range(4):
                        ins = mm(ps[2 + q % 2][:, 0:D], hsT[:, q % 2, c * P:(c + 1) * P], w2a[:, c, :],
                                 start=(c == 0), stop=(c == 3))
                    ins.then_inc(s["s_mm"], 1)
            for g, (t0, k) in enumerate(NODE_GROUPS):
                pe.wait_ge(s["s_evac"], t0 + k)
                if g >= 2:
                    pe.wait_ge(s["xT3_evac"], NG + g - 1)
                for i in range(k):
                    ins = pe.transpose(ps[4 + g % 2][:, i * P:(i + 1) * P], s_nodes[:, t0 + i, :], ident[:])
                ins.then_inc(s["turn3_mm"], 1)
            def node_hidden(g):
                t0, k = NODE_GROUPS[g]
                pe.wait_ge(s["xT3_evac"], NG + g + 1)
                cols = slice(t0 * P, (t0 + k) * P)
                for c in range(4):
                    if g >= 1:
                        pe.wait_ge(s["u_evac"], 4 * (g - 1) + c + 1)
                    mm(ps[c][:, 0:k * P], w1u[:, 0, c * D:(c + 1) * D], x3T[:, cols], start=True, stop=False)
                    mm(ps[c][:, 0:k * P], w1u[:, 1, c * D:(c + 1) * D], sT[:, cols], start=False,
                       stop=True).then_inc(s["u_mm"], 1)

            def node_out(g):
                t0, k = NODE_GROUPS[g]
                pe.wait_ge(s["u_evac"], 4 * g + 4)
                if g >= 2:
                    pe.wait_ge(s["o_taken"], g - 1)
                for i in range(k):
                    for c in range(4):
                        ins = mm(ps[6 + g % 2][:, i * P:(i + 1) * P], ubuf[:, g % 2, c, i * P:(i + 1) * P],
                                 w2u[:, c, :], start=(c == 0), stop=(c == 3))
                ins.then_inc(s["o_mm"], 1)

            for g in range(NG):
                node_hidden(g)
                if g >= 1:
                    node_out(g - 1)
                if g >= 2:
                    column_sum(val3, 4, g - 2, s["res_ready"])
            node_out(NG - 1)
            column_sum(val3, 4, NG - 2, s["res_ready"])
            column_sum(val3, 4, NG - 1, s["res_ready"])
            for g in range(NG):
                column_sum(square, 5, g, s["squared"])

        @block.vector
        def _(dve):
            chain = [0]

            def link(ins):
                chain[0] += 1
                ins.then_inc(s["dve_step"], 1)
                dve.wait_ge(s["dve_step"], chain[0])

            tt, ts, stt = dve.tensor_tensor, dve.tensor_scalar, dve.scalar_tensor_tensor

            dve.sem_inc(s["first_added"], 2)
            dve.sem_inc(s["more_added"], 1)
            for x in oh_used:
                dve.sem_inc(x, 1)
            dve.sem_inc(s["bank_taken"], A_BANKS)

            dve.wait_ge(s["loaded_dst"], 16)
            link(dve.tensor_copy(dst_gf, dst_g))
            halves = dst_gf.rearrange("g (q e) -> g q e", q=2)
            dve.tensor_reduce(lows[:, 0:2], halves, AX_X, ALU.min)
            link(dve.tensor_reduce(lows[:, 2:4], halves, AX_X, ALU.max))
            tt(spans_f[:, 0:1], lows[:, 0:1], lows[:, 1:2], ALU.min)
            link(tt(spans_f[:, 1:2], lows[:, 2:3], lows[:, 3:4], ALU.max))
            dve.tensor_copy(spans_f[:, 2:3], lows[:, 2:3])
            link(dve.tensor_copy(spans_f[:, 3:4], lows[:, 1:2]))
            link(dve.tensor_copy(spans_i, spans_f))
            link(ts(spans_i, spans_i, P.bit_length() - 1, None, ALU.arith_shift_right))
            ts(spans_i[:, 1:3], spans_i[:, 1:3], 1, None, ALU.add).then_inc(s["spans_made"], 1)
            dve.wait_ge(s["consts"], 8)
            for q in range(2):
                ts(reach[:, q, 0:TILES], tile_off[0:GROUPS, :], lows[:, 2 + q:3 + q], weight_c[:, q:q + 1], ALU.is_le, ALU.mult)
                link(ts(reach[:, q, TILES:], tile_off[0:GROUPS, :], float(P), lows[:, q:q + 1], ALU.add, ALU.is_gt))
                link(ts(reach[:, q, TILES:], reach[:, q, TILES:], weight_c[:, 2 + q:3 + q], None, ALU.mult))
            tt(reach[:, 0, :], reach[:, 0, :], reach[:, 1, :], ALU.max).then_inc(s["reach_made"], 1)
            dve.wait_ge(s["loaded_idx"], 48)
            stt(rel_c[:, 0:CHUNKS], src_c, float(R), typ_c, ALU.mult, ALU.add).then_inc(s["tables_made"], 1)
            ts(src_f[:, 0:CHUNKS], src_c, float(MID), None, ALU.subtract).then_inc(s["tables_made"], 1)
            dve.tensor_copy(dst_f[:, 0:CHUNKS], dst_c).then_inc(s["tables_made"], 1)

            def rel_low(n):
                dve.wait_ge(s["mid_ready"], n + 1)
                part = rel_parts[:, (n // 2) % 4, 0:4, :, :]
                tt(part[:, :, 2, :], rel_rest[:, n % 4], part[:, :, 1, :], ALU.subtract).then_inc(s["lo_dve"], 1)

            for n in range(2 * TILES):
                if n % 2 == 0 and n >= 2:
                    rel_low(n - 2)
                if n % 2 == 0 and n >= 4:
                    dve.wait_ge(s["lo_dve"], n // 2 - 1)
                if n % 2 == 1 and n >= 5:
                    dve.wait_ge(s["lo_pool"], (n - 3) // 2)
                dve.wait_ge(s["hi_ready"], n + 1)
                part = rel_parts[:, (n // 2) % 4, (n % 2) * 4:(n % 2) * 4 + 4, :, :]
                tt(rel_rest[:, n % 4], ps[n % 4][:, :].rearrange("p (r d) -> p r d", d=D), part[:, :, 0, :],
                   ALU.subtract).then_inc(s["rest_ready"], 1)
            rel_low(2 * TILES - 2)

            dve.wait_ge(s["reach_tr"], 1)
            dve.tensor_reduce(reach_col, ps[4][0:2 * TILES, 0:GROUPS], AX_X, ALU.max).then_inc(s["reach_max"], 1)
            dve.wait_ge(s["reach_row"], 1)
            row = reach_line
            link(ts(row[:, 0:TILES], ps[5][0:1, 0:TILES], -1.0, float(STEPS), ALU.mult, ALU.add))
            link(ts(row[:, 0:TILES], row[:, 0:TILES], float(STEPS - 1), None, ALU.min))
            link(stt(row[:, TILES:], row[:, 0:TILES], 1.0, ps[5][0:1, TILES:2 * TILES], ALU.add, ALU.max))
            dve.tensor_copy(tile_span[:], row).then_inc(s["tiles_made"], 1)
            dve.wait_ge(s["tiles_made"], 1)
            dve.wait_ge(s["tables_made"], 3)
            dve.wait_ge(s["spans_out"], 16)

            def chunk_one_hots(to, tile, chunk, n):
                lanes = lane[0:CHUNK, :].rearrange("p (a n) -> p a n", a=1).broadcast_to([CHUNK, n, P])
                dsts = dst_f[:, bass.ds(chunk, n)].rearrange("p (u a) -> p u a", a=1).broadcast_to([CHUNK, n, P])
                return stt(to, lanes, tile_off[0:CHUNK, bass.ds(tile, 1)], dsts, ALU.add, ALU.is_equal)

            step_no = dve.alloc_register("dve_step_no")
            last_use = [dve.alloc_register(f"dve_last_use{i}") for i in range(2)]
            for reg in (step_no, *last_use):
                dve.reg_mov(reg, 1)

            def step_one_hots(t, step, half):
                n = count_of(dve, step_no)
                dve.wait_ge(oh_used[1], count_of(dve, last_use[half]))
                chunk_one_hots(oh_dst[:, 2 * half:2 * half + 2, :], t, step * 2, 2)
                for slot in range(2):
                    dve.wait_ge(oh_used[slot], n)
                    ts(oh_src[:, slot, :], src_line, src_f[:, bass.ds(step * 2 + slot, 1)], None,
                       ALU.is_equal).then_inc(oh_ready[slot], 1)
                dve.reg_add(last_use[half], step_no, 1)
                dve.reg_add(step_no, step_no, 1)

            with dve.Fori(0, TILES) as t:
                first, end = steps_of(dve, t)
                with dve.Fori(first, end, 2) as step:
                    step_one_hots(t, step, 0)
                    with dve.If(end > step + 1):
                        step_one_hots(t, step + 1, 1)
            total = count_of(dve, step_no)
            for slot in range(2):
                dve.wait_ge(oh_used[slot], total)
            dve.sem_inc(s["a_done"], 1)
            dve.wait_ge(s["bank_taken"], A_BANKS * (TILES + 1))

            more = dve.alloc_register("dve_more")
            dve.reg_mov(more, 1)
            def one_hots(tile, group, slot, ready):
                chunk_one_hots(onehot[:, slot], tile, group * U, U).then_inc(ready, 1)

            def add_part(total, tile, bank, width, done):
                part = total[:, bass.ds(tile, 1), 0:width].rearrange("p a d -> p (a d)")
                tt(part, ps[bank][:, 0:width], part, ALU.add).then_inc(done, 1)

            def take_group(group, slot, total, width, banks, more_bank, ahead=None):
                if ahead:
                    ahead()
                one_hots(first_tile(dve, group + 1), group + 1, 1 - slot, s["oh_first_ready"])
                first, end = span_of(dve, group)
                dve.wait_ge(s["seg_first"], group + 1)
                dve.wait_ge(s["first_added"], group + 2)
                add_part(total, first, banks[slot], width, s["first_added"])
                with dve.If(end > first + 1):
                    with dve.Fori(first + 1, end) as t:
                        n = dve.snap(more, min_val=1, max_val=2 * GROUPS * TILES + 1)
                        one_hots(t, group, 2, s["more_ready"])
                        dve.wait_ge(s["seg_more"], n)
                        dve.wait_ge(s["more_added"], n)
                        dve.wait_ge(s["first_added"], group + 3)
                        add_part(total, t, more_bank, width, s["more_added"])
                        dve.reg_add(more, more, 1)
                    dve.wait_ge(s["more_added"], dve.snap(more, min_val=1, max_val=2 * GROUPS * TILES + 1))
                    dve.sem_inc(s["wait_carried"], 1)

            roots = [0]

            def root_of(ins):
                ins.then_inc(s["var_ready"], 1)
                roots[0] += 1
                return roots[0]

            def row_stats(v, g):
                t0, k = NODE_GROUPS[g]
                for t in range(t0, t0 + k):
                    ins = dve.bn_stats(stats[:, t, :], v[:, t, :])
                link(ins)
                for t in range(t0, t0 + k):
                    ins = dve.bn_aggr(mv[:, t, :], stats[:, t, :])
                link(ins)
                return root_of(ts(rstd[:, t0:t0 + k], mv[:, t0:t0 + k, 1], LN_EPS, None, ALU.add))

            def normalise_group(v, g, root):
                t0, k = NODE_GROUPS[g]
                dve.wait_ge(s["std_ready"], root)
                link(dve.reciprocal(rstd[:, t0:t0 + k], rstd[:, t0:t0 + k]))
                for t in range(t0, t0 + k):
                    ins = ts(v[:, t, :], v[:, t, :], mv[:, t, 0:1], rstd[:, t:t + 1], ALU.subtract, ALU.mult)
                return ins

            def split_low(g):
                t0, k = NODE_GROUPS[g]
                splits[0] += 1
                dve.wait_ge(s["split_hi"], splits[0])
                stt(split[:, t0:t0 + k, 1, :], val[:, t0:t0 + k, :], ROW_SCALE, split[:, t0:t0 + k, 0, :],
                    ALU.mult, ALU.subtract).then_inc(s["split_ready"], 1)

            splits = [0]

            def norm_groups(v, before, ready, split_too=False):
                root = None
                for g in range(NG + 2):
                    if g < NG:
                        before(g)
                        next_root = row_stats(v, g)
                    if 1 <= g <= NG:
                        normalise_group(v, g - 1, root).then_inc(ready, 1)
                    if g >= 2 and split_too:
                        split_low(g - 2)
                    root = next_root

            ts(has_edge[:], deg, 0.0, None, ALU.is_gt)
            link(ts(inv_deg[:], deg, 1.0, None, ALU.max))
            dve.reciprocal(inv_deg[:], inv_deg[:]).then_inc(s["inv_tr"], 1)
            dve.wait_ge(s["inv_tr"], 2)
            dve.tensor_copy(aggT_buf[0:TILES, 256:256 + P], ps[7][0:TILES, 0:P]).then_inc(s["inv_row"], 1)

            def layer0_rows(g):
                t0, k = NODE_GROUPS[g]
                dve.wait_ge(s["x_mm"], g + 1)
                part = val[:, t0:t0 + k, :]
                dve.wait_ge(s["b0_added"], g + 1)
                link(tt(part, tiles_of(ps[3 + g % 2], k), part, ALU.add))
                link(stt(part, part, 0.0, x_grp[g % 2][:, 0:k * D].rearrange("p (t d) -> p t d", d=D), ALU.max, ALU.add))
                dve.sem_inc(s["x_used"], 1)
            norm_groups(val, layer0_rows, s["x1_ready"], split_too=True)

            def dense_taken(g, base):
                t0, k = NODE_GROUPS[g]
                dve.wait_ge(s["dense_mm"], base + g + 1)
                dve.wait_ge(inv_loaded, 16 * (base + g + 1))
                stt(aggT_buf[:, 0:k * P], ps[g % 2][:, 0:k * P], 1.0 / ROW_SCALE, inv_b[:, 0:k * P],
                    ALU.mult, ALU.mult).then_inc(s["dense_taken"], 1)

            dve.wait_ge(s["loaded_e"], 16 * (EARLY_LOADS - 2))

            def lin_taken(g):
                t0, k = NODE_GROUPS[g]
                dve.wait_ge(s["lin_mm"], g + 1)
                tt(val[:, t0:t0 + k, :], tiles_of(ps[3], k), over_tiles(bl_b[:], k), ALU.add).then_inc(s["lin_taken"], 1)

            def row_norms(g):
                t0, k = NODE_GROUPS[g]
                dve.wait_ge(s["lin_taken"], g + 1)
                for t in range(t0, t0 + k):
                    ins = dve.tensor_tensor_reduce(hT_buf[:, g % 2, (t - t0) * D:(t - t0 + 1) * D], val[:, t, :], val[:, t, :],
                                                   1.0, 0.0, ALU.mult, ALU.add, small[:, t:t + 1])
                link(ins)
                norms = small[:, t0:t0 + k]
                dve.wait_ge(s["std_ready"], root_of(ts(norms, norms, 1e-24, None, ALU.max)))
                link(dve.reciprocal(norms, norms))
                for t in range(t0, t0 + k):
                    ins = ts(val[:, t, :], val[:, t, :], small[:, t:t + 1], None, ALU.mult)
                ins.then_inc(s["norm_ready"], 1)

            dve.wait_ge(s["inv_stored"], 16)
            dve.wait_ge(x1_stored, 16)
            for g in range(NG):
                if g >= 1:
                    dve.wait_ge(s["lin_mm"], g)
                dense_taken(g, 0)
                if g >= 1:
                    lin_taken(g - 1)
                    row_norms(g - 1)
            lin_taken(NG - 1)
            row_norms(NG - 1)
            dve.wait_ge(s["col_mm"], 1)
            dve.wait_ge(s["norm_ready"], NG)
            link(ts(col_a, ps[4][:, 0:D], 1.0 / N, None, ALU.mult))
            for g, (t0, k) in enumerate(NODE_GROUPS):
                part = val[:, t0:t0 + k, :]
                tt(part, part, over_tiles(col_a, k), ALU.subtract).then_inc(s["bn_centred"], 1)
            dve.wait_ge(s["col_mm"], 2)
            dve.wait_ge(s["std_ready"], root_of(ts(col_b, ps[5][:, 0:D], 1.0 / N, LN_EPS, ALU.mult, ALU.add)))
            link(dve.reciprocal(col_b, col_b))
            tt(col_b, col_b, gamma_b[:], ALU.mult).then_inc(s["cols_ready"], 1)

            def layer1_rows(g):
                t0, k = NODE_GROUPS[g]
                part = val[:, t0:t0 + k, :]
                dve.wait_ge(s["scaled_cols"], g + 1)
                dve.wait_ge(x1_back[g], 16)
                link(stt(part, part, 0.0, square[:, t0:t0 + k, :], ALU.max, ALU.add))

            norm_groups(val, layer1_rows, s["x2_ready"], split_too=True)

            def y_taken(g):
                t0, k = NODE_GROUPS[g]
                dve.wait_ge(s["z_evac"], g + 1)
                for b in range((k + 1) // 2):
                    n = min(2, k - 2 * b)
                    ins = dve.tensor_copy(val[:, t0 + 2 * b:t0 + 2 * b + n, :],
                                          ps[5 + b][:, 0:n * 256].rearrange("p (t s d) -> p t s d", s=2, d=D)[:, :, 0, :])
                ins.then_inc(s["y_evac"], 1)

            dve.wait_ge(x2_stored, 16)
            for g in range(NG):
                if g >= 1:
                    dve.wait_ge(s["hid_mm"], 2 * g)
                dense_taken(g, NG)
                if g >= 1:
                    y_taken(g - 1)
            y_taken(NG - 1)
            for g, (t0, k) in enumerate(NODE_GROUPS):
                dve.wait_ge(s["z_hi"], g + 1)
                zv = tiles_of(z_in[g % 3], k)
                tt(zv, zv, split3[:, t0:t0 + k, 0, :], ALU.subtract).then_inc(s["z_split"], 1)

            def sums_taken(g):
                t0, k = NODE_GROUPS[g]
                for t in range(t0, t0 + k):
                    dve.wait_ge(s["sum_mm"], t + 1)
                    tmp, bank = aggT_buf[:, 384:384 + D], ps[t % 4]
                    link(dve.tensor_copy(tmp, bank[:, 2 * D:3 * D]))
                    link(tt(tmp, bank[:, D:2 * D], tmp, ALU.add))
                    tt(tmp, bank[:, 0:D], tmp, ALU.add).then_inc(s["sum_taken"], 1)
                    dve.wait_ge(s["sum_taken"], t + 1)
                    link(stt(val[:, t, :], tmp, inv_deg[:, t:t + 1], val[:, t, :], ALU.mult, ALU.add))
                part = val[:, t0:t0 + k, :]
                link(tt(part, part, over_tiles(b2_b[:], k), ALU.add))
                link(dve.tensor_reduce(small[:, t0:t0 + k], part, AX_X, ALU.max))
                for t in range(t0, t0 + k):
                    ins = ts(val[:, t, :], val[:, t, :], small[:, t:t + 1], None, ALU.subtract)
                ins.then_inc(s["max_ready"], 1)

            for g in range(NG + 1):
                if g < NG:
                    sums_taken(g)
                if g >= 1:
                    t0, k = NODE_GROUPS[g - 1]
                    dve.wait_ge(s["lse_ready"], g)
                    dve.wait_ge(s["x2_loaded"], 16)
                    for t in range(t0, t0 + k):
                        ins = stt(val[:, t, :], val[:, t, :], small[:, t:t + 1], x2_back[:, t, :], ALU.subtract, ALU.add)
                    link(ins)
                    root = row_stats(val, g - 1)
                    normalise_group(val, g - 1, root).then_inc(s["x3_ready"], 1)

            dve.wait_ge(s["loaded_late"], 16 * LATE_LOADS)
            for t in range(TILES):
                dve.wait_ge(s["p_mm"], t + 1)
                if t >= 8:
                    dve.wait_ge(p_stored[t % 8], 16 * (t // 8))
                tt(hidden[:, t // 4 % 2, t % 4, :], ps[t % 4][:, :], b1a_b, ALU.add).then_inc(s["p_evac"], 1)
            dve.wait_ge(s["ub_mm"], 1)
            tt(u_bias[:], ps[7][:, 0:4], b1u_col[:], ALU.add).then_inc(s["ub_ready"], 1)
            dve.wait_ge(s["hsum_zero"], 1)
            for b in range(8):
                dve.wait_ge(p_stored[b], 16 * ((TILES + 7 - b) // 8))

            def hidden_rows(it, q):
                dve.wait_ge(p_gathered[q], it * (16 * U) + 16 * U)
                for u in range(U):
                    dve.wait_ge(s["edge_ready"], it * (Q * U) + (q * U + u + 1))
                    tt(hidden[0:CHUNK, q % 2, u, :], ps[u][0:CHUNK, :], rows_p[0:CHUNK, q * U + u, :],
                       ALU.add).then_inc(s["pre_done"], 1)

            dve.wait_ge(s["spans_in"], 32)
            one_hots(first_tile(dve, 0), 0, 0, s["oh_first_ready"])
            hidden_rows(0, 0)
            with dve.Fori(0, ROUNDS - 1) as it:
                for q in range(Q):
                    take_group(it * Q + q, q % 2, hsum, HID, (4, 5), 6,
                               lambda: hidden_rows(it + (q + 1) // Q, (q + 1) % Q))
            for q in range(Q):
                take_group((ROUNDS - 1) * Q + q, q % 2, hsum, HID, (4, 5), 6,
                           (lambda: hidden_rows(ROUNDS - 1, q + 1)) if q + 1 < Q else None)
            dve.wait_ge(s["first_added"], GROUPS + 2)
            dve.sem_inc(s["edges_done"], 1)
            for t in range(TILES):
                dve.wait_ge(s["s_mm"], t + 1)
                link(ts(s_nodes[:, t, :], ps[2 + t % 2][:, 0:D], inv_deg[:, t:t + 1], None, ALU.mult))
                stt(s_nodes[:, t, :], b2a_b, has_edge[:, t:t + 1], s_nodes[:, t, :],
                    ALU.mult, ALU.add).then_inc(s["s_evac"], 1)
            for g, (t0, k) in enumerate(NODE_GROUPS):
                part = val3[:, t0:t0 + k, :]
                dve.wait_ge(s["o_mm"], g + 1)
                tt(part, tiles_of(ps[6 + g % 2], k), over_tiles(b2u_b, k), ALU.add).then_inc(s["o_taken"], 1)
                dve.wait_ge(s["o_taken"], g + 1)
                tt(part, part, val[:, t0:t0 + k, :], ALU.add).then_inc(s["res_ready"], 1)
            dve.wait_ge(s["col_mm"], 3)
            dve.wait_ge(s["res_ready"], NG)
            link(stt(col_a, ps[4][:, 0:D], 1.0 / N, gna_b, ALU.mult, ALU.mult))
            for g, (t0, k) in enumerate(NODE_GROUPS):
                part = val3[:, t0:t0 + k, :]
                tt(part, part, over_tiles(col_a, k), ALU.subtract).then_inc(s["centred"], 1)
            dve.wait_ge(s["col_mm"], 4)
            dve.wait_ge(s["std_ready"], root_of(ts(col_b, ps[5][:, 0:D], 1.0 / N, LN_EPS, ALU.mult, ALU.add)))
            link(dve.reciprocal(col_b, col_b))
            tt(col_b, col_b, gnw_b, ALU.mult).then_inc(s["cols_ready"], 1)

            def layer3_rows(g):
                t0, k = NODE_GROUPS[g]
                part = val3[:, t0:t0 + k, :]
                dve.wait_ge(s["scaled_cols"], NG + g + 1)
                link(tt(part, part, val[:, t0:t0 + k, :], ALU.add))

            norm_groups(val3, layer3_rows, s["out_ready"])


EARLY_LOADS = 14
LATE_LOADS = 11


def kernel(**inputs):
    import numpy as np
    import concourse.bacc as bacc
    from concourse.bass_utils import run_bass_kernel_spmd

    g = {k: np.ascontiguousarray(v) for k, v in inputs.items()}
    c = np.ascontiguousarray
    chunks = lambda v: c(v.reshape(CHUNKS, CHUNK).T)
    columns = lambda v: c(v.reshape(-1, P).T)
    arrays = {
        "x": g["x"], "xT": c(g["x"].T), "dst": g["dst"],
        "src_c": chunks(g["src"]), "dst_c": chunks(g["dst"]), "typ_c": chunks(g["edge_type_8"]),
        "edgeT": c(g["edge_attr_128"].T),
        "w_rel": c(g["L0_gnn_weight"].transpose(1, 0, 2).reshape(D, R * D)),
        "w_self": g["L0_gnn_self_loop_weight"], "b0": g["L0_gnn_bias"],
        "w_lT": c(g["L1_gnn_W_l"].T), "bl": g["L1_gnn_b_l"], "w_rT": c(g["L1_gnn_W_r"].T),
        "gamma": g["L1_gnn_gamma"], "beta": g["L1_gnn_beta"],
        "w1": g["L2_gnn_W1"], "b1_col": columns(g["L2_gnn_b1"]), "w2": g["L2_gnn_W2"], "b2": g["L2_gnn_b2"],
        "u_col": c(g["L3_gnn_u"][0:1].T), "w1a": g["L3_gnn_W1a"], "b1a": g["L3_gnn_b1a"],
        "w2a": g["L3_gnn_W2a"], "b2a": g["L3_gnn_b2a"], "w1u": g["L3_gnn_W1u"],
        "b1u_col": columns(g["L3_gnn_b1u"]), "w2u": g["L3_gnn_W2u"], "b2u": g["L3_gnn_b2u"],
        "gnw": g["L3_gnn_gn_weight"], "gnb": g["L3_gnn_gn_bias"], "gna": g["L3_gnn_gn_alpha"],
    }
    nc = bacc.Bacc("TRN2", target_bir_lowering=False, num_devices=1)
    aps = {k: nc.dram_tensor("in_" + k, v.shape, mybir.dt.from_np(v.dtype), kind="ExternalInput").ap()
           for k, v in arrays.items()}
    out = nc.dram_tensor("out", (N, D), F32, kind="ExternalOutput").ap()
    build(nc, aps, out)
    r = run_bass_kernel_spmd(nc, [{"in_" + k: v for k, v in arrays.items()}], core_ids=[0])
    return r.results[0]["out"]
```
